# Optimizing a Trainium2 kernel written in Bass

```python
import numpy as np
import jax
import jax.numpy as jnp

def _softmax(x, axis=-1):
    return jax.nn.softmax(x, axis=axis)

def _gelu(x):
    return jax.nn.gelu(x, approximate=True)

def _silu(x):
    return jax.nn.silu(x)

def _sigmoid(x):
    return jax.nn.sigmoid(x)

def _layernorm(x, axis=-1, eps=1e-05):
    m = jnp.mean(x, axis=axis, keepdims=True)
    v = jnp.var(x, axis=axis, keepdims=True)
    return (x - m) / jnp.sqrt(v + eps)

def _scatter_add(tgt, idx, src, axis=0):
    return tgt.at[idx].add(src)

def _segment_sum(src, seg, n):
    return jax.ops.segment_sum(src, seg, n)
kernel_name = 'mk_seq_postln_d1_jaxref_r4_5ff5ba'

def setup_inputs(seed: int=0):
    np.random.seed(seed)
    _w = jnp.asarray

    def _L0_attn_setup():
        import jax, jax.numpy as jnp
        import numpy as np
        HIDDEN = 512
        HEADS = 16
        HEAD_DIM = HIDDEN // HEADS
        BATCH = 2
        SEQ = 512
        key = jax.random.key(seed)
        ks = jax.random.split(key, 9)
        s = 0.02
        return {'x': jax.random.normal(ks[0], (BATCH, SEQ, HIDDEN), dtype=jnp.float32), 'wq': jax.random.normal(ks[1], (HIDDEN, HIDDEN), dtype=jnp.float32) * s, 'bq': jax.random.normal(ks[2], (HIDDEN,), dtype=jnp.float32) * s, 'wk': jax.random.normal(ks[3], (HIDDEN, HIDDEN), dtype=jnp.float32) * s, 'bk': jax.random.normal(ks[4], (HIDDEN,), dtype=jnp.float32) * s, 'wv': jax.random.normal(ks[5], (HIDDEN, HIDDEN), dtype=jnp.float32) * s, 'bv': jax.random.normal(ks[6], (HIDDEN,), dtype=jnp.float32) * s, 'wo': jax.random.normal(ks[7], (HIDDEN, HIDDEN), dtype=jnp.float32) * s, 'bo': jax.random.normal(ks[8], (HIDDEN,), dtype=jnp.float32) * s}
    _L0_attn_in = _L0_attn_setup()

    def _L0_ffn_setup():
        import jax, jax.numpy as jnp
        import numpy as np
        N_EXPERTS = 8
        TOP_K = 2
        C = 512
        H = 256
        HS = 512
        B, T = (1, 128)
        SCALE = 0.02
        key = jax.random.key(seed)
        ks = jax.random.split(key, 10)
        x = jax.random.normal(ks[0], (B, T, C), dtype=jnp.float32)
        gate_w = jax.random.normal(ks[1], (N_EXPERTS, C), dtype=jnp.float32) * SCALE
        w_gate = jax.random.normal(ks[2], (N_EXPERTS, H, C), dtype=jnp.float32) * SCALE
        w_up = jax.random.normal(ks[3], (N_EXPERTS, H, C), dtype=jnp.float32) * SCALE
        w_down = jax.random.normal(ks[4], (N_EXPERTS, C, H), dtype=jnp.float32) * SCALE
        sh_gate = jax.random.normal(ks[5], (HS, C), dtype=jnp.float32) * SCALE
        sh_up = jax.random.normal(ks[6], (HS, C), dtype=jnp.float32) * SCALE
        sh_down = jax.random.normal(ks[7], (C, HS), dtype=jnp.float32) * SCALE
        se_gate_w = jax.random.normal(ks[8], (1, C), dtype=jnp.float32) * SCALE
        return {'x': x, 'gate_w': gate_w, 'w_gate': w_gate, 'w_up': w_up, 'w_down': w_down, 'sh_gate': sh_gate, 'sh_up': sh_up, 'sh_down': sh_down, 'se_gate_w': se_gate_w}
    _L0_ffn_in = _L0_ffn_setup()
    _d = {'L0_attn_x': _L0_attn_in['x'], 'L0_attn_wq': _L0_attn_in['wq'], 'L0_attn_bq': _L0_attn_in['bq'], 'L0_attn_wk': _L0_attn_in['wk'], 'L0_attn_bk': _L0_attn_in['bk'], 'L0_attn_wv': _L0_attn_in['wv'], 'L0_attn_bv': _L0_attn_in['bv'], 'L0_attn_wo': _L0_attn_in['wo'], 'L0_attn_bo': _L0_attn_in['bo'], 'L0_ffn_gate_w': _L0_ffn_in['gate_w'], 'L0_ffn_w_gate': _L0_ffn_in['w_gate'], 'L0_ffn_w_up': _L0_ffn_in['w_up'], 'L0_ffn_w_down': _L0_ffn_in['w_down'], 'L0_ffn_sh_gate': _L0_ffn_in['sh_gate'], 'L0_ffn_sh_up': _L0_ffn_in['sh_up'], 'L0_ffn_sh_down': _L0_ffn_in['sh_down'], 'L0_ffn_se_gate_w': _L0_ffn_in['se_gate_w']}
    _x0 = _d['L0_attn_x']
    _d['L0_attn_x'] = jax.random.normal(jax.random.fold_in(jax.random.key(seed), 1), (4, 1024, 512), dtype=_x0.dtype)
    del _x0
    return _d

def reference(L0_attn_x, L0_attn_wq, L0_attn_bq, L0_attn_wk, L0_attn_bk, L0_attn_wv, L0_attn_bv, L0_attn_wo, L0_attn_bo, L0_ffn_gate_w, L0_ffn_w_gate, L0_ffn_w_up, L0_ffn_w_down, L0_ffn_sh_gate, L0_ffn_sh_up, L0_ffn_sh_down, L0_ffn_se_gate_w):

    def _L0_attn_ref(x, wq, bq, wk, bk, wv, bv, wo, bo):
        import jax, jax.numpy as jnp
        import numpy as np
        HIDDEN = 512
        HEADS = 16
        HEAD_DIM = HIDDEN // HEADS
        BATCH = 2
        SEQ = 512
        B, S, _ = x.shape
        scale = jnp.sqrt(jnp.float32(HEAD_DIM))

        def proj(w, b):
            return (x @ w.T + b).reshape(B, S, HEADS, HEAD_DIM).transpose(0, 2, 1, 3)
        q = proj(wq, bq)
        k = proj(wk, bk)
        v = proj(wv, bv)
        scores = jnp.einsum('bhqd,bhkd->bhqk', q, k) / scale
        probs = jax.nn.softmax(scores, axis=-1)
        ctx = jnp.einsum('bhqk,bhkd->bhqd', probs, v)
        ctx = ctx.transpose(0, 2, 1, 3).reshape(B, S, HIDDEN)
        return ctx @ wo.T + bo

    def _L0_ffn_ref(x, gate_w, w_gate, w_up, w_down, sh_gate, sh_up, sh_down, se_gate_w):
        import jax, jax.numpy as jnp
        import numpy as np
        N_EXPERTS = 8
        TOP_K = 2
        C = 512
        H = 256
        HS = 512
        B, T = (1, 128)
        SCALE = 0.02
        Bb, Tt, Cc = x.shape
        xf = x.reshape(-1, Cc)
        scores = xf @ gate_w.T
        ew, ei = jax.lax.top_k(scores, TOP_K)
        ew = jax.nn.softmax(ew, axis=-1)
        x1 = jax.nn.silu(jnp.einsum('td,ehd->teh', xf, w_gate))
        x3 = jnp.einsum('td,ehd->teh', xf, w_up)
        expert_out = jnp.einsum('teh,edh->ted', x1 * x3, w_down)
        onehot = jax.nn.one_hot(ei, N_EXPERTS, dtype=ew.dtype)
        comb = jnp.einsum('ta,tae->te', ew, onehot)
        routed = jnp.einsum('te,ted->td', comb, expert_out)
        shared = jax.nn.silu(xf @ sh_gate.T) * (xf @ sh_up.T) @ sh_down.T
        sgate = jax.nn.sigmoid(xf @ se_gate_w.T)
        return (routed + sgate * shared).reshape(Bb, Tt, Cc)
    x = L0_attn_x
    x = _layernorm(x + _L0_attn_ref(x, L0_attn_wq, L0_attn_bq, L0_attn_wk, L0_attn_bk, L0_attn_wv, L0_attn_bv, L0_attn_wo, L0_attn_bo), axis=-1)
    x = _layernorm(x + _L0_ffn_ref(x, L0_ffn_gate_w, L0_ffn_w_gate, L0_ffn_w_up, L0_ffn_w_down, L0_ffn_sh_gate, L0_ffn_sh_up, L0_ffn_sh_down, L0_ffn_se_gate_w), axis=-1)
    return x

_drawn_inputs = setup_inputs


def setup_inputs(seed=0):
    import zlib

    import numpy as np

    out = dict(_drawn_inputs(seed))
    spreads = {}
    factors = {'L0_attn_wq': 8.0,
     'L0_attn_bq': 8.0,
     'L0_attn_wk': 8.0,
     'L0_attn_bk': 64.0,
     'L0_attn_wv': 7.723,
     'L0_attn_bv': 5.93,
     'L0_attn_wo': 4.822,
     'L0_attn_bo': 18.389,
     'L0_ffn_se_gate_w': 23.785}
    for name, (base, spread) in spreads.items():
        noise = np.random.default_rng([zlib.crc32(name.encode()), seed]).standard_normal(out[name].shape)
        drawn = base * np.exp(spread * noise) if base else spread * noise
        out[name] = jnp.asarray(drawn.astype(out[name].dtype))
    for name, factor in factors.items():
        out[name] = (out[name] * factor).astype(out[name].dtype)
    return out
```

```python
from contextlib import ExitStack

import concourse.bass as bass
from concourse import mybir

ALU = mybir.AluOpType
ACT = mybir.ActivationFunctionType
AX = mybir.AxisListType
F32 = mybir.dt.float32
F32R = mybir.dt.float32r
BF16 = mybir.dt.bfloat16
I32 = mybir.dt.int32
U32 = mybir.dt.uint32

P = 128
B, S, D = 4, 1024, 512
HEADS = 16
HD = D // HEADS
C = D // P
HG = P // HD
G = HEADS // HG
HALF = 512
NHALF = S // HALF
KT = S // P
EPS = 1e-5

STEPS = NHALF * KT
PROJ = 4
PRE = HG * KT * NHALF
SIDE = PROJ + PRE + 1

SIDE_AT = [[] for _ in range(STEPS)]
SIDE_AT[0] = [0, 1]
SIDE_AT[1] = [2, 3]
_first, _last = 3, 14
for _u in range(PRE):
    SIDE_AT[_first + _u // 2 * (_last - _first) // (PRE // 2)].append(PROJ + _u)
SIDE_AT[_last].append(SIDE - 1)
SLOTS = 4


def side_in(step, slot):
    units = SIDE_AT[step]
    return units[slot * len(units) // SLOTS:(slot + 1) * len(units) // SLOTS]


def attention(nc, x, xT, wkqT, wvT, woT, bq, bk, bv, bo, x2):
    with ExitStack() as ctx:
        def sb(name, shape, dt=F32):
            return ctx.enter_context(nc.sbuf_tensor(name, shape, dt))

        def sem(name):
            return ctx.enter_context(nc.semaphore(name))

        ident = sb("ident", [P, P])
        ones = sb("ones", [P, HD])
        bkq = sb("bkq", [P, 2, G])
        bv_bc = sb("bv_bc", [P, D])
        bo_bc = sb("bo_bc", [P, D])
        wstage = sb("wstage", [P, C, P])
        wkq_hi = sb("wkq_hi", [P, 2, C, P], F32R)
        wkq_lo = sb("wkq_lo", [P, 2, C, P], F32R)
        wv_hi = sb("wv_hi", [P, C, D], F32R)
        wv_lo = sb("wv_lo", [P, C, D], F32R)
        wo = sb("wo", [P, C, D])
        xstage = sb("xstage", [P, 2, HALF])
        x_hi = sb("x_hi", [P, C, S], F32R)
        x_lo = sb("x_lo", [P, C, S], F32R)
        kq_hi = sb("kq_hi", [P, 2, S], F32R)
        kq_lo = sb("kq_lo", [P, 2, S], F32R)
        k_stack = [sb(f"k_stack{i}", [P, HG, S], F32R) for i in range(2)]
        q_stack = [sb(f"q_stack{i}", [P, HG, S], F32R) for i in range(2)]
        v_sb = sb("v_sb", [P, KT, D])
        probs = sb("probs", [P, 4, 2, HALF])
        ctx_sb = sb("ctx_sb", [P, G, S])
        max_half = sb("max_half", [P, HG * KT, NHALF])
        max_q = sb("max_q", [P, HG * KT])
        max_row = sb("max_row", [HG * KT, P], F32R)
        x_nat = xstage
        res = sb("res", [P, 2, D])
        rsum = res[:, 0, :]
        stats = sb("stats", [P, 2, 6])
        mv = sb("mv", [P, 2, 2])
        var_eps = sb("var_eps", [P, 2, 1])
        minus_half = sb("minus_half", [P, 1])
        rstd = sb("rstd", [P, 2, 1])

        ps_s = ctx.enter_context(nc.psum_tensor("ps_s", [P, 4, HALF], F32))
        ps_ctx = ctx.enter_context(nc.psum_tensor("ps_ctx", [P, HALF], F32))
        ps_sum = ctx.enter_context(nc.psum_tensor("ps_sum", [P, HALF], F32))
        ps_side = ctx.enter_context(nc.psum_tensor("ps_side", [P, 2, HALF], F32))

        const_in = sem("const_in")
        passed = sem("passed")
        const_set = sem("const_set")
        wv_split = sem("wv_split")
        w_in = sem("w_in")
        w_split = sem("w_split")
        x_in = [sem("x_in0"), sem("x_in1")]
        x_split = sem("x_split")
        wv_in = [sem("wv_in0"), sem("wv_in1")]
        w_high, x_high, wv_high = sem("w_high"), sem("x_high"), sem("wv_high")
        side_ready = sem("side_ready")
        side_hi = sem("side_hi")
        side_free = sem("side_free")
        stacked = [sem("stacked0"), sem("stacked1")]
        max_made = sem("max_made")
        row_in = sem("row_in")
        scores_ready = sem("scores_ready")
        probs_ready = sem("probs_ready")
        pv_done = sem("pv_done")
        ctx_taken = sem("ctx_taken")
        sum_taken = sem("sum_taken")
        recip_done = sem("recip_done")
        ctx_done = sem("ctx_done")
        tail_ready = sem("tail_ready")
        tail_free = sem("tail_free")
        xnat_in = [sem("xnat_in0"), sem("xnat_in1")]
        xbias = sem("xbias")
        ln_chain = sem("ln_chain")
        aggr_made = sem("aggr_made")
        var_made = sem("var_made")
        rstd_made = sem("rstd_made")
        x2_ready = sem("x2_ready")
        x2_out = [sem("x2_out0"), sem("x2_out1")]

        block = ctx.enter_context(nc.Block())

        BSTEPS = G * STEPS
        SPREAD = 16 * 3 * HG
        CONSTS = 16 * 5
        TAIL = 2 * KT
        CHUNKS = C * NHALF

        @block.sync
        def _(sp):
            for t, src in ((bkq[:, 0, :], bk), (bkq[:, 1, :], bq), (bv_bc[:], bv.partition_broadcast(P)),
                           (bo_bc[:], bo.partition_broadcast(P)), (wo[:], woT)):
                sp.dma_start(t, src).then_inc(const_in, 16)
            def load_w(n, g):
                for sel in range(2):
                    if not (isinstance(n, int) and n + sel == 0):
                        sp.wait_ge(w_split, 2 * n + sel)
                    sp.dma_start(wstage[:], wkqT[g, :, sel]).then_inc(w_in, 16)

            def load_x(b):
                for i in range(CHUNKS):
                    c, half = i % C, i // C
                    if i >= 2:
                        sp.wait_ge(x_split, b * CHUNKS + i - 1)
                    sp.dma_start(xstage[:, i % 2, :],
                                 xT[bass.ds(b, 1), :, c, half * HALF:(half + 1) * HALF].rearrange(
                                     "a p t -> (a p) t")).then_inc(x_in[i % 2], 16)

            def spread(n, par):
                for sel, dst, parts in ((0, k_stack[par], (kq_hi, kq_lo, kq_hi)),
                                        (1, q_stack[par], (kq_hi, kq_hi, kq_lo))):
                    sp.wait_ge(side_free, n * SIDE + 2 * sel + 2)
                    for h in range(HG):
                        for r, part in enumerate(parts):
                            sp.dma_start(dst[r * HD:(r + 1) * HD, h, :].bitcast(F32),
                                         part[h * HD:(h + 1) * HD, sel, :].bitcast(F32)).then_inc(stacked[sel], 16)

            def rows(n, par):
                sp.wait_ge(side_free, (n + 1) * SIDE)
                sp.dma_start(q_stack[par][3 * HD:3 * HD + 1, :, :].rearrange("a h (j q) -> a (h j) q", q=P).bitcast(F32),
                             max_row[:].bitcast(F32)).then_inc(row_in, 16)

            def side(n, par, b_next, g_next):
                spread(n, par)
                if g_next is not None:
                    load_w(n + 1, g_next)
                if b_next is not None:
                    load_x(b_next)
                rows(n, par)

            def tail(b):
                sp.wait_ge(x_split, CHUNKS * (b + 2 if not isinstance(b, int) else b + 1))
                for t in range(KT):
                    if t >= 2:
                        sp.wait_ge(x2_ready, b * KT + t - 1)
                    sp.dma_start(x_nat[:, t % 2, :], x[bass.ds(b, 1), t * P:(t + 1) * P, :].rearrange(
                        "a p d -> (a p) d")).then_inc(xnat_in[t % 2], 16)
                    if t >= 1:
                        store(b, t - 1)
                store(b, KT - 1)

            def store(b, t):
                sp.wait_ge(x2_ready, b * KT + t + 1)
                sp.dma_start(x2[bass.ds(b, 1), t * P:(t + 1) * P, :].rearrange("a p d -> (a p) d"),
                             res[:, t % 2, :]).then_inc(x2_out[t % 2], 16)

            for i in range(2):
                sp.sem_inc(x2_out[i], 16)
            load_w(0, 0)
            load_x(0)
            for c in range(C):
                if c >= 2:
                    sp.wait_ge(wv_split, c - 1)
                else:
                    sp.wait_ge(x_split, CHUNKS - 1 + c)
                sp.dma_start(x_nat[:, c % 2, :], wvT[:, c, :]).then_inc(wv_in[c % 2], 16)
            side(0, 0, None, 1)
            with sp.Fori(0, B - 1) as b:
                for g in range(G):
                    side(b * G + g + 1, (g + 1) % 2, b + 1 if g == 2 else None, (g + 2) % G)
                tail(b)
            b = B - 1
            for g in range(G - 1):
                side(b * G + g + 1, (g + 1) % 2, None, (g + 2) % G if g < G - 2 else None)
            tail(b)
            for i in range(2):
                sp.wait_ge(x2_out[i], 16 * (B * KT // 2 + 1))

        @block.gpsimd
        def _(pool):
            nc.gpsimd.memset(ident[:], 0.0).then_inc(const_set, 1)
            pool.wait_ge(const_set, 1)
            nc.gpsimd.affine_select(out=ident[:], in_=ident[:], compare_op=ALU.not_equal, fill=1.0, base=0,
                                    pattern=[[-1, P]], channel_multiplier=1).then_inc(const_set, 1)
            pool.wait_ge(const_set, 2)
            nc.gpsimd.memset(ones[:], 1.0).then_inc(const_set, 1)
            for i in range(2):
                pool.wait_ge(const_set, 3 + i)
                nc.gpsimd.memset(k_stack[i][3 * HD:3 * HD + 1, :, :].bitcast(F32), 1.0).then_inc(const_set, 1)
            pool.wait_ge(const_set, 5)
            nc.gpsimd.memset(minus_half[:], -0.5).then_inc(const_set, 1)
            pool.wait_ge(const_set, 6)

            def split(hi, lo, raw, high_made, count, done):
                nc.gpsimd.tensor_copy(hi, raw).then_inc(high_made, 1)
                pool.wait_ge(high_made, count)
                nc.gpsimd.tensor_tensor(lo, raw, hi.bitcast(F32), ALU.subtract).then_inc(done, 1)

            def split_w(n):
                for sel in range(2):
                    pool.wait_ge(w_in, 16 * (2 * n + sel + 1))
                    pool.sem_inc(passed, 1)
                    split(wkq_hi[:, sel], wkq_lo[:, sel], wstage[:], w_high, 2 * n + sel + 1, w_split)

            def split_x(b):
                for i in range(CHUNKS):
                    c, half = i % C, i // C
                    pool.wait_ge(x_in[i % 2], 16 * (b * (CHUNKS // 2) + i // 2 + 1))
                    pool.sem_inc(passed, 1)
                    at = (slice(None), c, slice(half * HALF, (half + 1) * HALF))
                    split(x_hi[at], x_lo[at], xstage[:, i % 2, :], x_high, b * CHUNKS + i + 1, x_split)

            def projected(n):
                pool.wait_ge(side_ready, n * SIDE + PROJ)

            def add_bo(b):
                for t in range(KT + 1):
                    if t < KT:
                        pool.wait_ge(xnat_in[t % 2], 16 * (b * (KT // 2) + t // 2 + 1))
                        nc.gpsimd.tensor_tensor(x_nat[:, t % 2, :], x_nat[:, t % 2, :], bo_bc[:],
                                                ALU.add).then_inc(xbias, 1)
                    if t >= 1:
                        s = (t - 1) % 2
                        pool.wait_ge(var_made, b * KT + t)
                        nc.gpsimd.tensor_tensor(rstd[:, s, :], var_eps[:, s, :], minus_half[:],
                                                ALU.pow).then_inc(rstd_made, 1)

            split_w(0)
            split_x(0)
            for c in range(C):
                pool.wait_ge(wv_in[c % 2], 16 * (c // 2 + 1))
                split(wv_hi[:, c, :], wv_lo[:, c, :], x_nat[:, c % 2, :], wv_high, c + 1, wv_split)
            projected(0)
            split_w(1)
            pool.wait_ge(const_in, CONSTS)
            with pool.Fori(0, B - 1) as b:
                for g in range(G):
                    n = b * G + g + 1
                    projected(n)
                    split_w(n + 1)
                    if g == G - 2:
                        split_x(b + 1)
                add_bo(b)
            b = B - 1
            for g in range(G - 2):
                projected(b * G + g + 1)
                split_w(b * G + g + 2)
            add_bo(b)

        @block.tensor
        def _(pe):
            def three(out, terms, first, last):
                for i, (w, m) in enumerate(terms):
                    done = nc.tensor.matmul(out, w, m, start=first and i == 0, stop=last and i == 2)
                return done

            def side_unit(n, u, par):
                if u == 0:
                    pe.wait_ge(w_split, 2 * n + 2)
                pe.wait_ge(side_free, n * SIDE + max(u - 1, 0))
                bank = ps_side[:, u % 2, :]
                if u < PROJ:
                    sel, half = u // 2, u % 2
                    for c in range(C):
                        wh, wl = wkq_hi[:, sel, c, :], wkq_lo[:, sel, c, :]
                        xh = x_hi[:, c, half * HALF:(half + 1) * HALF]
                        xl = x_lo[:, c, half * HALF:(half + 1) * HALF]
                        done = three(bank, ((wh, xh), (wl, xh), (wh, xl)), c == 0, c == C - 1)
                elif u < PROJ + PRE:
                    i = u - PROJ
                    h, j, half = i // (KT * NHALF), i // NHALF % KT, i % NHALF
                    if i == 0:
                        for s in stacked:
                            pe.wait_ge(s, SPREAD * (n + 1))
                    done = nc.tensor.matmul(bank, q_stack[par][0:3 * HD, h, j * P:(j + 1) * P],
                                            k_stack[par][0:3 * HD, h, half * HALF:(half + 1) * HALF],
                                            start=True, stop=True)
                else:
                    pe.wait_ge(max_made, n + 1)
                    done = nc.tensor.transpose(ps_side[0:HG * KT, 0, 0:P], max_q[:], ident[:])
                done.then_inc(side_ready, 1)

            def scores(b, loc, pair):
                g, half, kt = loc // STEPS, loc // KT % NHALF, loc % KT
                par = g % 2
                if loc % STEPS == 0 and pair == 0:
                    pe.wait_ge(row_in, 16 * (b * G + g + 1))
                if loc:
                    pe.wait_ge(probs_ready, b * 2 * BSTEPS + 2 * loc + pair - 1)
                for h in (2 * pair, 2 * pair + 1):
                    done = nc.tensor.matmul(ps_s[:, h, :], k_stack[par][0:3 * HD + 1, h, kt * P:(kt + 1) * P],
                                            q_stack[par][0:3 * HD + 1, h, half * HALF:(half + 1) * HALF],
                                            start=True, stop=True)
                done.then_inc(scores_ready, 1)

            def weighted(b, loc, is_sum):
                g, half, kt = loc // STEPS, loc // KT % NHALF, loc % KT
                out = ps_sum if is_sum else ps_ctx
                pe.wait_ge(probs_ready, b * 2 * BSTEPS + 2 * loc + 2)
                if kt == 0 and loc:
                    pe.wait_ge(sum_taken if is_sum else ctx_taken, b * G * NHALF + loc // KT)
                for h in range(HG):
                    lhsT = ones[:] if is_sum else v_sb[:, kt, (g * HG + h) * HD:(g * HG + h + 1) * HD]
                    done = nc.tensor.matmul(out[h * HD:(h + 1) * HD, :], lhsT,
                                            probs[:, (2 * loc + h // 2) % 4, h % 2, :],
                                            start=kt == 0, stop=kt == KT - 1)
                if is_sum:
                    done.then_inc(pv_done, 1)

            def v_tile(u, t):
                if t >= 4 or not isinstance(u, int):
                    pe.wait_ge(tail_free, u - 3)
                for c in range(C):
                    xh, xl = x_hi[:, c, t * P:(t + 1) * P], x_lo[:, c, t * P:(t + 1) * P]
                    wh, wl = wv_hi[:, c, :], wv_lo[:, c, :]
                    done = three(ps_s[:, t % 4, :], ((xh, wh), (xl, wh), (xh, wl)), c == 0, c == C - 1)
                done.then_inc(tail_ready, 1)

            def o_tile(u, t):
                pe.wait_ge(tail_free, u - 3)
                for g in range(G):
                    done = nc.tensor.matmul(ps_s[:, t % 4, :], ctx_sb[:, g, t * P:(t + 1) * P], wo[:, g, :],
                                            start=g == 0, stop=g == G - 1)
                done.then_inc(tail_ready, 1)

            def batch(b, last):
                for pair in range(2):
                    scores(b, 0, pair)
                for loc in range(BSTEPS):
                    g = loc // STEPS
                    if loc % STEPS == 0 and g == G - 1 and not last:
                        pe.wait_ge(x_split, (b + 2) * CHUNKS)
                    for slot in range(SLOTS):
                        if slot >= 2:
                            weighted(b, loc, slot == 3)
                        elif loc + 1 < BSTEPS:
                            scores(b, loc + 1, slot)
                        if not (last and g == G - 1):
                            for u in side_in(loc % STEPS, slot):
                                side_unit(b * G + g + 1, u, (g + 1) % 2)

            pe.wait_ge(x_split, CHUNKS)
            for u in range(PROJ):
                side_unit(0, u, 0)
            pe.wait_ge(wv_split, C)
            for t in range(KT):
                v_tile(t, t)
            pe.wait_ge(const_set, 5)
            pe.wait_ge(const_in, CONSTS)
            for u in range(PROJ, SIDE):
                side_unit(0, u, 0)
            with pe.Fori(0, B - 1) as b:
                pe.wait_ge(tail_free, b * TAIL + KT)
                batch(b, False)
                for t in range(KT):
                    v_tile(b * TAIL + KT + t, t)
                pe.wait_ge(ctx_done, (b + 1) * G * NHALF)
                for t in range(KT):
                    o_tile(b * TAIL + 2 * KT + t, t)
            b = B - 1
            pe.wait_ge(tail_free, b * TAIL + KT)
            batch(b, True)
            pe.wait_ge(ctx_done, (b + 1) * G * NHALF)
            for t in range(KT):
                o_tile(b * TAIL + KT + t, t)

        @block.scalar
        def _(act):
            def side_unit(n, u, g):
                if u >= PROJ:
                    return
                sel, half = u // 2, u % 2
                act.wait_ge(side_ready, n * SIDE + u + 1)
                act.wait_ge(stacked[sel], SPREAD * n)
                nc.scalar.activation(kq_hi[:, sel, half * HALF:(half + 1) * HALF], ps_side[:, u % 2, :], ACT.Identity,
                                     bias=bkq[:, sel, g:g + 1]).then_inc(side_hi, 1)

            def exps(b, loc, pair):
                act.wait_ge(scores_ready, b * 2 * BSTEPS + 2 * loc + pair + 1)
                if loc >= 2:
                    act.wait_ge(pv_done, b * BSTEPS + loc - 1)
                nc.scalar.activation(probs[:, (2 * loc + pair) % 4, :, :], ps_s[:, 2 * pair:2 * pair + 2, :],
                                     ACT.Exp, scale=HD ** -0.5).then_inc(probs_ready, 1)

            def batch(b, last):
                for pair in range(2):
                    exps(b, 0, pair)
                for loc in range(BSTEPS):
                    g = loc // STEPS
                    for slot in range(SLOTS):
                        if slot < 2 and loc + 1 < BSTEPS:
                            exps(b, loc + 1, slot)
                        if not (last and g == G - 1):
                            for u in side_in(loc % STEPS, slot):
                                side_unit(b * G + g + 1, u, (g + 1) % G)
                    if loc % KT == KT - 1:
                        k = b * G * NHALF + loc // KT
                        act.wait_ge(pv_done, b * BSTEPS + loc + 1)
                        if loc >= KT:
                            act.wait_ge(ctx_done, k)
                        else:
                            act.wait_ge(x2_out[0], 16 * (b * (KT // 2) + 1))
                        nc.scalar.activation(rsum, ps_sum[:], ACT.Identity).then_inc(sum_taken, 1)

            act.wait_ge(const_in, CONSTS)
            for u in range(PROJ):
                side_unit(0, u, 0)
            with act.Fori(0, B - 1) as b:
                batch(b, False)
            batch(B - 1, True)

        @block.vector
        def _(dve):
            def side_unit(n, u, g):
                sel, half = u // 2, slice(u % 2 * HALF, (u % 2 + 1) * HALF)
                if u < PROJ:
                    dve.wait_ge(side_hi, n * PROJ + u + 1)
                    dve.wait_ge(stacked[sel], SPREAD * n)
                    nc.vector.scalar_tensor_tensor(out=kq_lo[:, sel, half], in0=ps_side[:, u % 2, :],
                                                   scalar=bkq[:, sel, g:g + 1],
                                                   in1=kq_hi[:, sel, half].bitcast(F32), op0=ALU.add,
                                                   op1=ALU.subtract).then_inc(side_free, 1)
                elif u < PROJ + PRE:
                    i = u - PROJ
                    dve.wait_ge(side_ready, n * SIDE + u + 1)
                    nc.vector.reduce_max(max_half[:, i // 2, i % 2:i % 2 + 1], ps_side[:, u % 2, :],
                                         AX.X).then_inc(side_free, 1)
                    if i == PRE - 1:
                        dve.wait_ge(side_free, n * SIDE + u + 1)
                        nc.vector.tensor_reduce(out=max_q[:], in_=max_half[:], axis=AX.X, op=ALU.max,
                                                negate=True).then_inc(max_made, 1)
                else:
                    dve.wait_ge(side_ready, n * SIDE + u + 1)
                    dve.wait_ge(row_in, 16 * n)
                    nc.vector.tensor_copy(max_row[:], ps_side[0:HG * KT, 0, 0:P]).then_inc(side_free, 1)

            def normalise(b, loc):
                k = b * G * NHALF + loc // KT
                g, half = loc // STEPS, loc // KT % NHALF
                out = ctx_sb[:, g, half * HALF:(half + 1) * HALF]
                dve.wait_ge(pv_done, b * BSTEPS + loc + 1)
                nc.vector.tensor_copy(out, ps_ctx[:]).then_inc(ctx_taken, 1)
                dve.wait_ge(sum_taken, k + 1)
                nc.vector.reciprocal(rsum, rsum).then_inc(recip_done, 1)
                dve.wait_ge(recip_done, k + 1)
                nc.vector.tensor_tensor(out, out, rsum, ALU.mult).then_inc(ctx_done, 1)

            def batch(b, last):
                for loc in range(BSTEPS):
                    g = loc // STEPS
                    if not (last and g == G - 1):
                        for u in SIDE_AT[loc % STEPS]:
                            side_unit(b * G + g + 1, u, (g + 1) % G)
                    if loc % KT == KT - 1:
                        normalise(b, loc)

            def v_tile(u, t):
                dve.wait_ge(tail_ready, u + 1)
                nc.vector.tensor_tensor(v_sb[:, t, :], ps_s[:, t % 4, :], bv_bc[:], ALU.add).then_inc(tail_free, 1)

            def o_tile(u, b, t):
                s = t % 2
                k = b * KT + t
                dve.wait_ge(tail_ready, u + 1)
                dve.wait_ge(xbias, k + 1)
                dve.wait_ge(x2_out[s], 16 * (b * (KT // 2) + t // 2 + 1))
                nc.vector.tensor_tensor(res[:, s, :], ps_s[:, t % 4, :], x_nat[:, s, :], ALU.add).then_inc(tail_free, 1)
                dve.wait_ge(tail_free, u + 1)
                nc.vector.bn_stats(stats[:, s, :], res[:, s, :]).then_inc(ln_chain, 1)
                dve.wait_ge(const_in, CONSTS)
                dve.wait_ge(ln_chain, k + 1)
                nc.vector.bn_aggr(mv[:, s, :], stats[:, s, :]).then_inc(aggr_made, 1)
                dve.wait_ge(aggr_made, k + 1)
                nc.vector.tensor_scalar(var_eps[:, s, :], mv[:, s, 1:2], EPS, None, ALU.add).then_inc(var_made, 1)
                dve.wait_ge(rstd_made, k + 1)
                nc.vector.tensor_scalar(res[:, s, :], res[:, s, :], mv[:, s, 0:1], rstd[:, s, :],
                                        ALU.subtract, ALU.mult).then_inc(x2_ready, 1)

            dve.wait_ge(const_in, CONSTS)
            for u in range(PROJ):
                side_unit(0, u, 0)
            for t in range(KT):
                v_tile(t, t)
            for u in range(PROJ, SIDE):
                side_unit(0, u, 0)
            with dve.Fori(0, B - 1) as b:
                batch(b, False)
                for t in range(KT):
                    v_tile(b * TAIL + KT + t, t)
                for t in range(KT):
                    o_tile(b * TAIL + 2 * KT + t, b, t)
            b = B - 1
            batch(b, True)
            for t in range(KT):
                o_tile(b * TAIL + KT + t, b, t)


TOKENS = B * S
TT = TOKENS // P
E = 8
H = 256
CH = H // P
NT = 2 * TT + E
SLOTS_ALL = NT * P
RW = 16


def shared_and_scores(nc, x2, shg, shu, shd, rw, wgu, wd, base, gu_sb, wd_sb, gu_in, route, ident):
    with ExitStack() as ctx:
        def sb(name, shape, dt=F32):
            return ctx.enter_context(nc.sbuf_tensor(name, shape, dt))

        def sem(name):
            return ctx.enter_context(nc.semaphore(name))

        def psum(name, shape):
            return ctx.enter_context(nc.psum_tensor(name, shape, F32))

        wstage = sb("sh_stage", [P, 2, D])
        sgu_hi = sb("sgu_hi", [P, C, 2, D], F32R)
        sgu_lo = sb("sgu_lo", [P, C, 2, D], F32R)
        sd_hi = sb("sd_hi", [P, C, D], F32R)
        sd_lo = sb("sd_lo", [P, C, D], F32R)
        rw_raw = sb("rw_raw", [P, C, RW])
        rw_hi = sb("rw_hi", [P, C, RW], F32R)
        rw_lo = sb("rw_lo", [P, C, RW], F32R)
        x_t = sb("x_t", [P, 4, D])
        xT_hi = sb("xT_hi", [P, 2, C, P], F32R)
        xT_lo = sb("xT_lo", [P, 2, C, P], F32R)
        act_g = sb("act_g", [P, 2, D])
        hid = sb("hid", [P, 2, D])
        hT_hi = sb("hT_hi", [P, 2, C, P], F32R)
        hT_lo = sb("hT_lo", [P, 2, C, P], F32R)
        th = sb("th", [P, 2, 1])
        sgate = sb("sgate", [P, 2, 1])
        out_t = sb("out_t", [P, 2, D])

        ps_t = psum("ps_t", [P, 2, D])
        ps_gu = psum("ps_gu", [P, 2, D])
        ps_r = psum("ps_r", [P, D])
        ps_ht = psum("ps_ht", [P, D])
        ps_d = psum("ps_d", [P, 2, D])

        st_in = [sem("st_in0"), sem("st_in1")]
        st_high = sem("st_high")
        st_split = sem("st_split")
        rw_zero = sem("rw_zero")
        rw_in = sem("rw_in")
        x_in = [sem(f"xt_in{i}") for i in range(4)]
        t_ready = sem("t_ready")
        t_hi = sem("t_hi")
        t_lo = sem("t_lo")
        gu_ready = sem("gu_ready")
        silu_done = sem("silu_done")
        hid_done = sem("hid_done")
        sc_done = sem("sc_done")
        th_done = sem("th_done")
        gate_done = sem("gate_done")
        ht_ready = sem("ht_ready")
        ht_hi = sem("ht_hi")
        ht_lo = sem("ht_lo")
        d_ready = sem("d_ready")
        base_done = sem("base_done")
        base_out = [sem("base_out0"), sem("base_out1")]

        PIECES = 3 * C

        block = ctx.enter_context(nc.Block())

        @block.sync
        def _(sp):
            sp.wait_ge(rw_zero, 1)
            sp.dma_start(rw_raw[:, :, 0:E + 1], rw).then_inc(rw_in, 16)

            def load_tile(t, s):
                sp.dma_start(x_t[:, s, :], x2[bass.ds(t * P, P), :]).then_inc(x_in[s], 16)

            for i in range(PIECES):
                c = i % C
                src = (shg, shu, shd)[i // C]
                if i >= 2:
                    sp.wait_ge(st_split, i - 1)
                sp.dma_start(wstage[:, i % 2, :], src[:, c, :]).then_inc(st_in[i % 2], 16)
                if i < 4:
                    load_tile(i, i)
            for e in range(E):
                sp.dma_start(gu_sb[:, e], wgu[e]).then_inc(gu_in, 16)
                sp.dma_start(wd_sb[:, e], wd[e]).then_inc(gu_in, 16)

            def store(t, s):
                sp.wait_ge(base_done, t + 1)
                sp.dma_start(base[bass.ds(t * P, P), :], out_t[:, s % 2, :]).then_inc(base_out[s % 2], 16)

            with sp.Fori(0, TT // 4 - 1) as j:
                for s in range(4):
                    store(4 * j + s, s)
                    load_tile(4 * j + s + 4, s)
            for s in range(4):
                store(TT - 4 + s, s)
            for i in range(2):
                sp.wait_ge(base_out[i], 16 * TT // 2)

        @block.gpsimd
        def _(pool):
            def split(hi, lo, raw, k):
                nc.gpsimd.tensor_copy(hi, raw).then_inc(st_high, 1)
                pool.wait_ge(st_high, k + 1)
                nc.gpsimd.tensor_tensor(lo, raw, hi.bitcast(F32), ALU.subtract).then_inc(st_split, 1)

            nc.gpsimd.memset(rw_raw[:], 0.0).then_inc(rw_zero, 1)
            pool.wait_ge(rw_zero, 1)
            for i in range(PIECES):
                c = i % C
                pool.wait_ge(st_in[i % 2], 16 * (i // 2 + 1))
                if i < 2 * C:
                    split(sgu_hi[:, c, i // C, :], sgu_lo[:, c, i // C, :], wstage[:, i % 2, :], i)
                else:
                    split(sd_hi[:, c, :], sd_lo[:, c, :], wstage[:, i % 2, :], i)
            pool.wait_ge(rw_in, 16)
            split(rw_hi[:], rw_lo[:], rw_raw[:], PIECES)

        def pipeline(eng, step):
            step(0, 0, True, False)
            for s in range(1, 4):
                step(s, s, False, False)
            with eng.Fori(1, TT // 4 - 1) as j:
                for s in range(4):
                    step(4 * j + s, s, False, False)
            for s in range(4):
                step(TT - 4 + s, s, False, s == 3)

        @block.tensor
        def _(pe):
            def turn(t, s):
                pe.wait_ge(x_in[s], 16 * (t // 4 + 1) if isinstance(t, int) else x_count(t, s))
                if not (isinstance(t, int) and t < 2):
                    pe.wait_ge(t_hi, t - 1)
                    pe.wait_ge(t_lo, t - 1)
                for c in range(C):
                    done = nc.tensor.transpose(ps_t[:, s % 2, c * P:(c + 1) * P],
                                               x_t[:, s, c * P:(c + 1) * P], ident[:])
                done.then_inc(t_ready, 1)

            def x_count(t, s):
                return (t - s) * 4 + 16

            def three(out, a, b, c, last_c):
                for i, (w, m) in enumerate(((a[0], b[0]), (a[1], b[0]), (a[0], b[1]))):
                    done = nc.tensor.matmul(out, w, m, start=c == 0 and i == 0, stop=c == last_c and i == 2)
                return done

            def up(t, s):
                pe.wait_ge(t_hi, t + 1)
                pe.wait_ge(t_lo, t + 1)
                if not (isinstance(t, int) and t < 1):
                    pe.wait_ge(hid_done, t)
                    pe.wait_ge(sc_done, t)
                    pe.wait_ge(th_done, t)
                for out, m_of in ((ps_r[:, 0:RW], lambda c: (rw_hi[:, c, :], rw_lo[:, c, :])),
                                  (ps_gu[:, 0, :], lambda c: (sgu_hi[:, c, 0, :], sgu_lo[:, c, 0, :])),
                                  (ps_gu[:, 1, :], lambda c: (sgu_hi[:, c, 1, :], sgu_lo[:, c, 1, :]))):
                    for c in range(C):
                        done = three(out, (xT_hi[:, s % 2, c, :], xT_lo[:, s % 2, c, :]), m_of(c), c, C - 1)
                done.then_inc(gu_ready, 1)

            def turn_hidden(t, s):
                pe.wait_ge(hid_done, t + 1)
                if not (isinstance(t, int) and t < 1):
                    pe.wait_ge(ht_hi, t)
                    pe.wait_ge(ht_lo, t)
                for c in range(C):
                    done = nc.tensor.transpose(ps_ht[:, c * P:(c + 1) * P], hid[:, s % 2, c * P:(c + 1) * P], ident[:])
                done.then_inc(ht_ready, 1)

            def down(t, s):
                pe.wait_ge(ht_hi, t + 1)
                pe.wait_ge(ht_lo, t + 1)
                if not (isinstance(t, int) and t < 2):
                    pe.wait_ge(base_done, t - 1)
                for c in range(C):
                    done = three(ps_d[:, s % 2, :], (hT_hi[:, s % 2, c, :], hT_lo[:, s % 2, c, :]),
                                 (sd_hi[:, c, :], sd_lo[:, c, :]), c, C - 1)
                done.then_inc(d_ready, 1)

            def step(t, s, first, last):
                if first:
                    turn(t, s)
                up(t, s)
                if not first:
                    down(t - 1, s - 1 if s else 3)
                if not last:
                    turn(t + 1, (s + 1) % 4)
                turn_hidden(t, s)
                if last:
                    down(t, s)

            pe.wait_ge(st_split, PIECES + 1)
            pipeline(pe, step)

        @block.scalar
        def _(act):
            def x_high(t, s):
                act.wait_ge(t_ready, t + 1)
                if not (isinstance(t, int) and t < 2):
                    act.wait_ge(gu_ready, t - 1)
                nc.scalar.activation(xT_hi[:, s % 2], ps_t[:, s % 2, :].rearrange("p (c t) -> p c t", c=C),
                                     ACT.Copy).then_inc(t_hi, 1)

            def gate(t, s):
                act.wait_ge(gu_ready, t + 1)
                if not (isinstance(t, int) and t < 2):
                    act.wait_ge(hid_done, t - 1)
                    act.wait_ge(gate_done, t - 1)
                nc.scalar.activation(act_g[:, s % 2, :], ps_gu[:, 0, :], ACT.Silu).then_inc(silu_done, 1)
                nc.scalar.activation(th[:, s % 2, :], ps_r[:, E:E + 1], ACT.Tanh, scale=0.5).then_inc(th_done, 1)

            def h_high(t, s):
                act.wait_ge(ht_ready, t + 1)
                if not (isinstance(t, int) and t < 2):
                    act.wait_ge(d_ready, t - 1)
                nc.scalar.activation(hT_hi[:, s % 2], ps_ht[:].rearrange("p (c t) -> p c t", c=C),
                                     ACT.Copy).then_inc(ht_hi, 1)

            def step(t, s, first, last):
                if first:
                    x_high(t, s)
                if not last:
                    x_high(t + 1, s + 1)
                gate(t, s)
                h_high(t, s)

            pipeline(act, step)

        @block.vector
        def _(dve):
            def x_low(t, s):
                dve.wait_ge(t_hi, t + 1)
                if not (isinstance(t, int) and t < 2):
                    dve.wait_ge(gu_ready, t - 1)
                nc.vector.tensor_tensor(xT_lo[:, s % 2], ps_t[:, s % 2, :].rearrange("p (c t) -> p c t", c=C),
                                        xT_hi[:, s % 2].bitcast(F32), ALU.subtract).then_inc(t_lo, 1)

            def hidden(t, s):
                dve.wait_ge(silu_done, t + 1)
                if not (isinstance(t, int) and t < 2):
                    dve.wait_ge(ht_ready, t - 1)
                nc.vector.tensor_tensor(hid[:, s % 2, :], act_g[:, s % 2, :], ps_gu[:, 1, :],
                                        ALU.mult).then_inc(hid_done, 1)
                dve.wait_ge(th_done, t + 1)
                nc.vector.tensor_copy(route[:, bass.ds(t, 1), :].rearrange("p a e -> p (a e)"),
                                      ps_r[:, 0:E]).then_inc(sc_done, 1)
                nc.vector.tensor_scalar(sgate[:, s % 2, :], th[:, s % 2, :], 0.5, 0.5, ALU.mult,
                                        ALU.add).then_inc(gate_done, 1)

            def h_low(t, s):
                dve.wait_ge(ht_hi, t + 1)
                if not (isinstance(t, int) and t < 2):
                    dve.wait_ge(d_ready, t - 1)
                nc.vector.tensor_tensor(hT_lo[:, s % 2], ps_ht[:].rearrange("p (c t) -> p c t", c=C),
                                        hT_hi[:, s % 2].bitcast(F32), ALU.subtract).then_inc(ht_lo, 1)

            def finish(t, s):
                dve.wait_ge(d_ready, t + 1)
                dve.wait_ge(gate_done, t + 1)
                if not (isinstance(t, int) and t < 2):
                    dve.wait_ge(base_out[s % 2], 16 * (t // 2) if isinstance(t, int) else 8 * (t - s % 2))
                nc.vector.scalar_tensor_tensor(out=out_t[:, s % 2, :], in0=ps_d[:, s % 2, :], scalar=sgate[:, s % 2, :],
                                               in1=x_t[:, s, :], op0=ALU.mult, op1=ALU.add).then_inc(base_done, 1)

            def step(t, s, first, last):
                if first:
                    x_low(t, s)
                if not first:
                    finish(t - 1, s - 1 if s else 3)
                if not last:
                    x_low(t + 1, s + 1)
                hidden(t, s)
                h_low(t, s)
                if last:
                    finish(t, s)

            pipeline(dve, step)


def place(nc, route, weights, pos, tile_expert, table, ident):
    with ExitStack() as ctx:
        def sb(name, shape, dt=F32):
            return ctx.enter_context(nc.sbuf_tensor(name, shape, dt))

        def sem(name):
            return ctx.enter_context(nc.semaphore(name))

        expert = sb("expert", [P, TT, E])
        expert_i = sb("expert_i", [P, TT, E], I32)
        tri = sb("tri", [P, P])
        all_ones = sb("all_ones", [P, P])
        token = sb("token", [P, TT], I32)
        tile_start_i = sb("tile_start_i", [P, NT, E], I32)
        tile_start = sb("tile_start", [P, NT, E])
        zero_table = sb("zero_table", [P, NT], I32)
        big = [sb(f"big{i}", [P, TT, E]) for i in range(6)]
        one = [sb(f"one{i}", [P, 2, TT, E]) for i in range(1)][0]
        col = [sb(f"col{i}", [P, TT]) for i in range(8)]
        cnt = [sb(f"cnt{i}", [P, E]) for i in range(6)]
        cnt_i = [sb(f"cnt_i{i}", [P, E], I32) for i in range(3)]
        col_i = [sb(f"col_i{i}", [P, 2, TT], I32) for i in range(5)]
        ends = sb("ends", [P, NT, E])
        te = sb("te", [P, NT])
        index = sb("index", [P, 8], I32)
        who = sb("who", [P, 4], I32)
        ps_rank = ctx.enter_context(nc.psum_tensor("ps_rank", [P, TT * E], F32))
        ps_total = ctx.enter_context(nc.psum_tensor("ps_total", [P, TT * E], F32))

        passed = sem("passed_p")
        made = sem("made")
        zeroed = sem("zeroed")
        links = sem("links")
        visits = sem("visits")
        counted = sem("counted")
        gap_ready = sem("gap_ready")
        exp_done = sem("exp_done")
        placed = sem("placed")
        copied = sem("copied")
        scattered = [sem(f"scattered{i}") for i in range(8)]

        block = ctx.enter_context(nc.Block())

        @block.gpsimd
        def _(pool):
            n = [0]

            def after(ins):
                n[0] += 1
                ins.then_inc(made, 1)
                pool.wait_ge(made, n[0])

            after(nc.gpsimd.iota(expert_i[:], [[0, TT], [1, E]], base=0, channel_multiplier=0))
            after(nc.gpsimd.iota(token[:], [[P, TT]], base=0, channel_multiplier=1))
            after(nc.gpsimd.iota(tile_start_i[:], [[P, NT], [0, E]], base=0, channel_multiplier=0))
            after(nc.gpsimd.memset(all_ones[:], 1.0))
            after(nc.gpsimd.memset(zero_table[:], 0))
            after(nc.gpsimd.affine_select(out=tri[:], in_=all_ones[:], compare_op=ALU.is_gt, fill=0.0, base=0,
                                          pattern=[[1, P]], channel_multiplier=-1))
            pool.wait_ge(placed, 1)
            pool.wait_ge(zeroed, 16)
            def scatter(j, first):
                for s in range(4):
                    if not first:
                        for v in range(2):
                            pool.wait_ge(scattered[2 * s + v], 16 * j)
                        pool.sem_inc(passed, 1)
                    nc.gpsimd.tensor_copy(who[:, s:s + 1], token[:, bass.ds(4 * j + s, 1)]).then_inc(copied, 1)
                    for v in range(2):
                        nc.gpsimd.tensor_copy(index[:, 2 * s + v:2 * s + v + 1],
                                              col_i[4][:, v, bass.ds(4 * j + s, 1)]).then_inc(copied, 1)
                    pool.wait_ge(copied, 12 * j + 3 * s + 3)
                    pool.sem_inc(passed, 1)
                    for v in range(2):
                        nc.gpsimd.indirect_dma_start(
                            table, bass.IndirectOffsetOnAxis(ap=index[:, 2 * s + v:2 * s + v + 1].bitcast(U32), axis=0),
                            who[:, s:s + 1], None).then_inc(scattered[2 * s + v], 16)

            scatter(0, True)
            with pool.Fori(1, TT // 4) as j:
                scatter(j, False)
            for i in range(8):
                pool.wait_ge(scattered[i], 16 * (TT // 4))

        @block.sync
        def _(sp):
            sp.wait_ge(made, 5)
            sp.dma_start(table.rearrange("(p n) a -> p (n a)", p=P), zero_table[:]).then_inc(zeroed, 16)
            sp.wait_ge(zeroed, 16)

        @block.tensor
        def _(pe):
            pe.wait_ge(made, 6)
            pe.wait_ge(visits, 1)
            flat = big[4][:].rearrange("p t e -> p (t e)")
            nc.tensor.matmul(ps_rank[:], tri[:], flat, start=True, stop=True)
            nc.tensor.matmul(ps_total[:], all_ones[:], flat, start=True, stop=True).then_inc(counted, 1)

        @block.scalar
        def _(act):
            act.wait_ge(gap_ready, 1)
            nc.scalar.activation(col[4][:], col[3][:], ACT.Exp).then_inc(exp_done, 1)

        @block.vector
        def _(dve):
            n = [0]

            def link(ins):
                n[0] += 1
                ins.then_inc(links, 1)
                dve.wait_ge(links, n[0])

            def over_experts(x):
                return x.unsqueeze(2).broadcast_to((P, TT, E))

            v = nc.vector
            dve.wait_ge(made, 3)
            link(v.tensor_copy(expert[:], expert_i[:]))
            link(v.tensor_copy(tile_start[:], tile_start_i[:]))

            def pick(scores, largest, chosen):
                link(v.tensor_reduce(out=largest[:], in_=scores, axis=AX.X, op=ALU.max))
                link(v.tensor_tensor(big[0][:], scores, over_experts(largest[:]), ALU.is_equal))
                link(v.scalar_tensor_tensor(out=big[0][:], in0=big[0][:], scalar=-float(E), in1=expert[:],
                                            op0=ALU.mult, op1=ALU.add))
                link(v.tensor_reduce(out=col[2][:], in_=big[0][:], axis=AX.X, op=ALU.min))
                link(v.tensor_scalar(col[2][:], col[2][:], float(E), None, ALU.add))
                link(v.tensor_tensor(chosen, expert[:], over_experts(col[2][:]), ALU.is_equal))

            pick(route[:], col[0], one[:, 0])
            link(v.tensor_scalar(big[1][:], one[:, 0], -3.0e38, None, ALU.mult))
            link(v.tensor_scalar(big[2][:], one[:, 0], -3.0e38, 3.0e38, ALU.mult, ALU.add))
            link(v.tensor_tensor(big[1][:], big[1][:], big[2][:], ALU.add))
            link(v.tensor_tensor(big[1][:], route[:], big[1][:], ALU.min))
            pick(big[1][:], col[1], one[:, 1])
            link(v.tensor_tensor(big[4][:], one[:, 0], one[:, 1], ALU.add))
            v.tensor_tensor(col[3][:], col[1][:], col[0][:], ALU.subtract).then_inc(gap_ready, 1)
            dve.wait_ge(links, n[0])
            v.tensor_scalar(col[5][:], col[2][:], 0.0, None, ALU.mult).then_inc(visits, 1)
            dve.wait_ge(exp_done, 1)
            link(v.tensor_scalar(col[6][:], col[4][:], 1.0, None, ALU.add))
            link(v.reciprocal(weights[:, 0, :], col[6][:]))
            link(v.tensor_tensor(weights[:, 1, :], weights[:, 0, :], col[4][:], ALU.mult))
            dve.wait_ge(counted, 1)
            link(v.tensor_copy(big[0][:], ps_total[:].rearrange("p (t e) -> p t e", e=E)))
            src, dst = big[0], big[1]
            first = src
            step = 1
            bufs = [big[1], big[2]]
            while step < TT:
                dst = bufs[0]
                bufs.reverse()
                link(v.tensor_tensor(dst[:, step:, :], src[:, step:, :], src[:, :TT - step, :], ALU.add))
                link(v.tensor_copy(dst[:, :step, :], src[:, :step, :]))
                src = dst
                step *= 2
            link(v.tensor_tensor(big[3][:], src[:], first[:], ALU.subtract))
            link(v.tensor_tensor(big[3][:], big[3][:], ps_rank[:].rearrange("p (t e) -> p t e", e=E), ALU.add))
            link(v.tensor_scalar(cnt[0][:], src[:, TT - 1, :], float(P - 1), None, ALU.add))
            link(v.tensor_copy(cnt_i[0][:], cnt[0][:]))
            shift = P.bit_length() - 1
            link(v.tensor_scalar(cnt_i[1][:], cnt_i[0][:], shift, None, ALU.logical_shift_right))
            link(v.tensor_copy(cnt[1][:], cnt_i[1][:]))
            link(v.tensor_scalar(cnt[1][:], cnt[1][:], float(P), None, ALU.mult))
            a, others = cnt[1], [cnt[2], cnt[3]]
            step = 1
            while step < E:
                b = others[0]
                others.reverse()
                link(v.tensor_tensor(b[:, step:], a[:, step:], a[:, :E - step], ALU.add))
                link(v.tensor_copy(b[:, :step], a[:, :step]))
                a = b
                step *= 2
            end = a
            link(v.tensor_tensor(cnt[4][:], end[:], cnt[1][:], ALU.subtract))
            link(v.tensor_tensor(big[3][:], big[3][:], cnt[4][:].unsqueeze(1).broadcast_to((P, TT, E)), ALU.add))
            for k in range(2):
                link(v.tensor_tensor(big[5][:], big[3][:], one[:, k], ALU.mult))
                link(v.tensor_reduce(out=col[7][:], in_=big[5][:], axis=AX.X, op=ALU.add))
                link(v.tensor_copy(pos[:, k, :], col[7][:]))
            link(v.tensor_scalar(col_i[0][:], pos[:], P - 1, None, ALU.bitwise_and))
            link(v.tensor_scalar(col_i[1][:], pos[:], shift, None, ALU.logical_shift_right))
            rows = ends[:].rearrange("p n e -> p (n e)")[:, 0:4 * TT].rearrange("p (a k t) -> p a k t", a=2, k=2)
            link(v.tensor_copy(rows[:, 0], col_i[0][:]))
            link(v.tensor_copy(rows[:, 1], col_i[1][:]))
            link(v.scalar_tensor_tensor(out=rows[:, 0], in0=rows[:, 0], scalar=float(NT), in1=rows[:, 1],
                                        op0=ALU.mult, op1=ALU.add))
            v.tensor_copy(col_i[4][:], rows[:, 0]).then_inc(placed, 1)
            dve.wait_ge(placed, 1)
            link(v.tensor_tensor(ends[:], tile_start[:], end[:].unsqueeze(1).broadcast_to((P, NT, E)), ALU.is_ge))
            link(v.tensor_reduce(out=te[:], in_=ends[:], axis=AX.X, op=ALU.add))
            link(v.tensor_scalar(te[:], te[:], float(E - 1), None, ALU.min))
            link(v.tensor_copy(tile_expert[:], te[:]))


def experts(nc, x2, table, tile_expert, gu_sb, wd_sb, gu_in, y, ident):
    with ExitStack() as ctx:
        def sb(name, shape, dt=F32):
            return ctx.enter_context(nc.sbuf_tensor(name, shape, dt))

        def sem(name):
            return ctx.enter_context(nc.semaphore(name))

        def psum(name, shape):
            return ctx.enter_context(nc.psum_tensor(name, shape, F32))

        who_all = sb("who_all", [P, NT], I32)
        who = sb("who_e", [P, 4], I32)
        x_g = sb("x_g", [P, 4, D])
        xT = sb("xT_e", [P, 2, C, P])
        act_g = sb("act_e", [P, 2, H])
        hid = sb("hid_e", [P, 2, H])
        hT = sb("hT_e", [P, 2, CH, P])
        y_t = sb("y_t", [P, 4, D])
        ps_t = psum("pe_t", [P, 2, D])
        ps_h = psum("pe_h", [P, 2, D])
        ps_ht = psum("pe_ht", [P, 2, D])
        ps_y = psum("pe_y", [P, 2, D])

        passed = sem("passed_e")
        who_in = sem("who_in")
        who_copied = sem("who_copied")
        x_in = [sem(f"xg_in{i}") for i in range(4)]
        t_ready = sem("et_ready")
        t_done = sem("et_done")
        h_ready = sem("eh_ready")
        silu_done = sem("esilu_done")
        hid_done = sem("ehid_done")
        ht_ready = sem("eht_ready")
        ht_done = sem("eht_done")
        y_ready = sem("ey_ready")
        y_done = sem("ey_done")
        y_out = [sem(f"y_out{i}") for i in range(4)]

        block = ctx.enter_context(nc.Block())

        def static(t, n):
            return isinstance(t, int) and t < n

        def turns_of(t, s):
            return 4 * (t - s)

        @block.sync
        def _(sp):
            sp.dma_start(who_all[:], table.rearrange("(p n) a -> p (n a)", p=P)).then_inc(who_in, 16)
            with sp.Fori(0, NT // 4) as j:
                for s in range(4):
                    t = 4 * j + s
                    sp.wait_ge(y_done, t + 1)
                    sp.dma_start(y[bass.ds(t * P, P), :], y_t[:, s, :]).then_inc(y_out[s], 16)
            for s in range(4):
                sp.wait_ge(y_out[s], 16 * (NT // 4))

        @block.gpsimd
        def _(pool):
            pool.wait_ge(who_in, 16)

            def gather(t, s):
                if not static(t, 4):
                    pool.wait_ge(t_ready, t - 3)
                    pool.sem_inc(passed, 1)
                nc.gpsimd.tensor_copy(who[:, s:s + 1], who_all[:, bass.ds(t, 1)]).then_inc(who_copied, 1)
                pool.wait_ge(who_copied, t + 1)
                pool.sem_inc(passed, 1)
                nc.gpsimd.indirect_dma_start(
                    x_g[:, s, :], None, x2, bass.IndirectOffsetOnAxis(ap=who[:, s:s + 1].bitcast(U32), axis=0),
                ).then_inc(x_in[s], 16)

            for s in range(4):
                gather(s, s)
            with pool.Fori(1, NT // 4) as j:
                for s in range(4):
                    gather(4 * j + s, s)

        def pipeline(eng, step):
            step(0, 0, True, False)
            for s in range(1, 4):
                step(s, s, False, False)
            with eng.Fori(1, NT // 4 - 1) as j:
                for s in range(4):
                    step(4 * j + s, s, False, False)
            for s in range(4):
                step(NT - 4 + s, s, False, s == 3)

        @block.tensor
        def _(pe):
            def turn(t, s):
                pe.wait_ge(x_in[s], turns_of(t, s) + 16)
                if not static(t, 2):
                    pe.wait_ge(t_done, t - 1)
                for c in range(C):
                    done = nc.tensor.transpose(ps_t[:, s % 2, c * P:(c + 1) * P], x_g[:, s, c * P:(c + 1) * P], ident[:])
                done.then_inc(t_ready, 1)

            def up(t, s, e):
                pe.wait_ge(t_done, t + 1)
                if not static(t, 2):
                    pe.wait_ge(hid_done, t - 1)
                for c in range(C):
                    done = nc.tensor.matmul(ps_h[:, s % 2, :], xT[:, s % 2, c, :],
                                            gu_sb[:, bass.ds(e, 1), c, :].rearrange("p a n -> p (a n)"),
                                            start=c == 0, stop=c == C - 1)
                done.then_inc(h_ready, 1)

            def turn_hidden(t, s):
                pe.wait_ge(hid_done, t + 1)
                if not static(t, 2):
                    pe.wait_ge(ht_done, t - 1)
                for c in range(CH):
                    done = nc.tensor.transpose(ps_ht[:, s % 2, c * P:(c + 1) * P], hid[:, s % 2, c * P:(c + 1) * P], ident[:])
                done.then_inc(ht_ready, 1)

            def down(t, s, e):
                pe.wait_ge(ht_done, t + 1)
                if not static(t, 2):
                    pe.wait_ge(y_done, t - 1)
                for c in range(CH):
                    done = nc.tensor.matmul(ps_y[:, s % 2, :], hT[:, s % 2, c, :],
                                            wd_sb[:, bass.ds(e, 1), c, :].rearrange("p a n -> p (a n)"),
                                            start=c == 0, stop=c == CH - 1)
                done.then_inc(y_ready, 1)

            def expert_of(t):
                return pe.value_load(tile_expert[0:1, bass.ds(t, 1)], min_val=0, max_val=E - 1)

            def step(t, s, first, last):
                if first:
                    turn(t, s)
                up(t, s, expert_of(t))
                if not first:
                    down(t - 1, (s - 1) % 4, expert_of(t - 1))
                if not last:
                    turn(t + 1, (s + 1) % 4)
                turn_hidden(t, s)
                if last:
                    down(t, s, expert_of(t))

            pe.wait_ge(gu_in, 16 * 2 * E)
            pipeline(pe, step)

        @block.scalar
        def _(act):
            def x_copy(t, s):
                act.wait_ge(t_ready, t + 1)
                if not static(t, 2):
                    act.wait_ge(h_ready, t - 1)
                nc.scalar.activation(xT[:, s % 2], ps_t[:, s % 2, :].rearrange("p (c t) -> p c t", c=C),
                                     ACT.Copy).then_inc(t_done, 1)

            def gate(t, s):
                act.wait_ge(h_ready, t + 1)
                if not static(t, 2):
                    act.wait_ge(hid_done, t - 1)
                nc.scalar.activation(act_g[:, s % 2, :], ps_h[:, s % 2, 0:H], ACT.Silu).then_inc(silu_done, 1)

            def step(t, s, first, last):
                if first:
                    x_copy(t, s)
                if not last:
                    x_copy(t + 1, (s + 1) % 4)
                gate(t, s)

            pipeline(act, step)

        @block.vector
        def _(dve):
            def hidden(t, s):
                dve.wait_ge(silu_done, t + 1)
                if not static(t, 2):
                    dve.wait_ge(ht_ready, t - 1)
                nc.vector.tensor_tensor(hid[:, s % 2, :], act_g[:, s % 2, :], ps_h[:, s % 2, H:2 * H],
                                        ALU.mult).then_inc(hid_done, 1)

            def h_copy(t, s):
                dve.wait_ge(ht_ready, t + 1)
                if not static(t, 2):
                    dve.wait_ge(y_ready, t - 1)
                nc.vector.tensor_copy(hT[:, s % 2], ps_ht[:, s % 2, 0:H].rearrange("p (c t) -> p c t", c=CH)).then_inc(ht_done, 1)

            def y_copy(t, s):
                dve.wait_ge(y_ready, t + 1)
                if not static(t, 4):
                    dve.wait_ge(y_out[s], turns_of(t, s))
                nc.vector.tensor_copy(y_t[:, s, :], ps_y[:, s % 2, :]).then_inc(y_done, 1)

            def step(t, s, first, last):
                if not first:
                    y_copy(t - 1, (s - 1) % 4)
                hidden(t, s)
                h_copy(t, s)
                if last:
                    y_copy(t, s)

            pipeline(dve, step)


def combine(nc, base, y, pos, weights, out):
    with ExitStack() as ctx:
        def sb(name, shape, dt=F32):
            return ctx.enter_context(nc.sbuf_tensor(name, shape, dt))

        def sem(name):
            return ctx.enter_context(nc.semaphore(name))

        index = sb("c_index", [P, 8], I32)
        y_g = sb("y_g", [P, 4, 2, D])
        b_t = sb("b_t", [P, 4, D])
        w_t = sb("w_t", [P, 4, 2])
        acc = sb("acc", [P, 4, D])
        res = sb("res_c", [P, 4, D])
        stats = sb("stats_c", [P, 4, 6])
        mv = sb("mv_c", [P, 4, 2])
        var_eps = sb("var_eps_c", [P, 4, 1])
        minus_half = sb("minus_half_c", [P, 1])
        rstd = sb("rstd_c", [P, 4, 1])

        passed = sem("passed_c")
        copied = sem("c_copied")
        y_in = [sem(f"y_in{i}") for i in range(4)]
        b_in = [sem(f"b_in{i}") for i in range(4)]
        w_copied = sem("w_copied")
        first_added = sem("first_added")
        added = sem("added")
        stats_made = sem("stats_made")
        aggr_made = sem("c_aggr_made")
        var_made = sem("c_var_made")
        rstd_made = sem("c_rstd_made")
        normal = sem("normal")
        out_done = [sem(f"out_done{i}") for i in range(4)]
        half_set = sem("half_set")

        block = ctx.enter_context(nc.Block())
        GROUPS = TT // 4

        @block.sync
        def _(sp):
            def load(t, s):
                sp.dma_start(b_t[:, s, :], base[bass.ds(t * P, P), :]).then_inc(b_in[s], 16)

            def store(t, s):
                sp.wait_ge(normal, t + 1)
                sp.dma_start(out[bass.ds(t * P, P), :], res[:, s, :]).then_inc(out_done[s], 16)

            for s in range(4):
                load(s, s)
            with sp.Fori(0, GROUPS - 1) as j:
                for s in range(4):
                    store(4 * j + s, s)
                    load(4 * j + s + 4, s)
            for s in range(4):
                store(TT - 4 + s, s)
            for s in range(4):
                sp.wait_ge(out_done[s], 16 * GROUPS)

        @block.gpsimd
        def _(pool):
            nc.gpsimd.memset(minus_half[:], -0.5).then_inc(half_set, 1)
            pool.wait_ge(half_set, 1)

            def gather(t, s):
                for k in range(2):
                    nc.gpsimd.tensor_copy(index[:, 2 * s + k:2 * s + k + 1], pos[:, k, bass.ds(t, 1)]).then_inc(copied, 1)
                    pool.wait_ge(copied, 2 * t + k + 1)
                    pool.sem_inc(passed, 1)
                    nc.gpsimd.indirect_dma_start(
                        y_g[:, s, k, :], None, y,
                        bass.IndirectOffsetOnAxis(ap=index[:, 2 * s + k:2 * s + k + 1].bitcast(U32), axis=0),
                    ).then_inc(y_in[s], 16)

            def root(t, s):
                pool.wait_ge(var_made, t + 1)
                nc.gpsimd.tensor_tensor(rstd[:, s, :], var_eps[:, s, :], minus_half[:], ALU.pow).then_inc(rstd_made, 1)

            for s in range(4):
                gather(s, s)
            with pool.Fori(0, GROUPS - 1) as j:
                for s in range(4):
                    root(4 * j + s, s)
                    gather(4 * j + s + 4, s)
            for s in range(4):
                root(TT - 4 + s, s)

        @block.vector
        def _(dve):
            def one_tile(t, s, turn):
                dve.wait_ge(y_in[s], 32 * turn + 32)
                dve.wait_ge(b_in[s], 16 * turn + 16)
                nc.vector.tensor_copy(w_t[:, s, :], weights[:, :, bass.ds(t, 1)].rearrange("p k a -> p (k a)")).then_inc(w_copied, 1)
                dve.wait_ge(w_copied, t + 1)
                nc.vector.scalar_tensor_tensor(out=acc[:, s, :], in0=y_g[:, s, 0, :], scalar=w_t[:, s, 0:1],
                                               in1=b_t[:, s, :], op0=ALU.mult, op1=ALU.add).then_inc(first_added, 1)
                dve.wait_ge(first_added, t + 1)
                if not isinstance(turn, int):
                    dve.wait_ge(out_done[s], 16 * turn)
                nc.vector.scalar_tensor_tensor(out=res[:, s, :], in0=y_g[:, s, 1, :], scalar=w_t[:, s, 1:2],
                                               in1=acc[:, s, :], op0=ALU.mult, op1=ALU.add).then_inc(added, 1)
                dve.wait_ge(added, t + 1)
                nc.vector.bn_stats(stats[:, s, :], res[:, s, :]).then_inc(stats_made, 1)
                dve.wait_ge(y_in[s], 32)
                dve.wait_ge(stats_made, t + 1)
                nc.vector.bn_aggr(mv[:, s, :], stats[:, s, :]).then_inc(aggr_made, 1)
                dve.wait_ge(aggr_made, t + 1)
                nc.vector.tensor_scalar(var_eps[:, s, :], mv[:, s, 1:2], EPS, None, ALU.add).then_inc(var_made, 1)

            def norm(t, s):
                dve.wait_ge(rstd_made, t + 1)
                nc.vector.tensor_scalar(res[:, s, :], res[:, s, :], mv[:, s, 0:1], rstd[:, s, :],
                                        ALU.subtract, ALU.mult).then_inc(normal, 1)

            one_tile(0, 0, 0)
            for s in range(1, 4):
                one_tile(s, s, 0)
                norm(s - 1, s - 1)
            with dve.Fori(1, GROUPS) as j:
                for s in range(4):
                    one_tile(4 * j + s, s, j)
                    norm(4 * j + s - 1, (s - 1) % 4)
            norm(TT - 1, 3)


def moe(nc, x2, shg, shu, shd, rw, wgu, wd, out):
    base = nc.dram_tensor("base", (TOKENS, D), F32, kind="Internal").ap()
    y = nc.dram_tensor("y_slots", (SLOTS_ALL, D), F32, kind="Internal").ap()
    table = nc.dram_tensor("table", (SLOTS_ALL, 1), I32, kind="Internal").ap()
    with ExitStack() as ctx:
        ident = ctx.enter_context(nc.sbuf_tensor("ident_m", [P, P], F32))
        route = ctx.enter_context(nc.sbuf_tensor("route", [P, TT, E], F32))
        weights = ctx.enter_context(nc.sbuf_tensor("weights", [P, 2, TT], F32))
        pos = ctx.enter_context(nc.sbuf_tensor("pos", [P, 2, TT], I32))
        tile_expert = ctx.enter_context(nc.sbuf_tensor("tile_expert", [P, NT], I32))
        gu_in = ctx.enter_context(nc.semaphore("gu_in"))
        ident_set = ctx.enter_context(nc.semaphore("ident_set"))
        with nc.Block() as block:
            @block.gpsimd
            def _(pool):
                nc.gpsimd.memset(ident[:], 0.0).then_inc(ident_set, 1)
                pool.wait_ge(ident_set, 1)
                nc.gpsimd.affine_select(out=ident[:], in_=ident[:], compare_op=ALU.not_equal, fill=1.0, base=0,
                                        pattern=[[-1, P]], channel_multiplier=1).then_inc(ident_set, 1)
                pool.wait_ge(ident_set, 2)
        with ExitStack() as big:
            gu_sb = big.enter_context(nc.sbuf_tensor("gu_sb", [P, E, C, 2 * H], F32))
            wd_sb = big.enter_context(nc.sbuf_tensor("wd_sb", [P, E, CH, D], F32))
            shared_and_scores(nc, x2, shg, shu, shd, rw, wgu, wd, base, gu_sb, wd_sb, gu_in, route, ident)
            place(nc, route, weights, pos, tile_expert, table, ident)
            experts(nc, x2, table, tile_expert, gu_sb, wd_sb, gu_in, y, ident)
        combine(nc, base, y, pos, weights, out)


def build(nc, x, xT, wkqT, wvT, woT, bq, bk, bv, bo, shg, shu, shd, rw, wgu, wd, out):
    x2 = nc.dram_tensor("x2", (TOKENS, D), F32, kind="Internal").ap()
    attention(nc, x, xT, wkqT, wvT, woT, bq, bk, bv, bo, x2.rearrange("(b s) d -> b s d", b=B))
    moe(nc, x2, shg, shu, shd, rw, wgu, wd, out)


def kernel(L0_attn_x, L0_attn_wq, L0_attn_bq, L0_attn_wk, L0_attn_bk, L0_attn_wv, L0_attn_bv, L0_attn_wo,
           L0_attn_bo, L0_ffn_gate_w, L0_ffn_w_gate, L0_ffn_w_up, L0_ffn_w_down, L0_ffn_sh_gate, L0_ffn_sh_up,
           L0_ffn_sh_down, L0_ffn_se_gate_w):
    import numpy as np
    import concourse.bacc as bacc
    from concourse.bass_utils import run_bass_kernel_spmd

    def array(a):
        return np.ascontiguousarray(np.asarray(a))

    def turned(w):
        w = np.asarray(w)
        return array(w.T.reshape(-1, P, w.shape[0]).transpose(1, 0, 2))

    x = array(L0_attn_x)
    kq = np.stack([turned(L0_attn_wk), turned(L0_attn_wq)])
    arrays = {
        "x": x,
        "xT": array(x.transpose(0, 2, 1).reshape(B, C, P, S).transpose(0, 2, 1, 3)),
        "wkqT": array(kq.reshape(2, P, C, G, P).transpose(3, 1, 0, 2, 4)),
        "wvT": turned(L0_attn_wv),
        "woT": turned(L0_attn_wo),
        "bq": array(np.asarray(L0_attn_bq).reshape(G, P).T),
        "bk": array(np.asarray(L0_attn_bk).reshape(G, P).T),
        "bv": array(L0_attn_bv),
        "bo": array(L0_attn_bo),
        "shg": turned(L0_ffn_sh_gate),
        "shu": turned(L0_ffn_sh_up),
        "shd": turned(L0_ffn_sh_down),
        "rw": turned(np.concatenate([np.asarray(L0_ffn_gate_w), np.asarray(L0_ffn_se_gate_w)])),
        "wgu": array(np.stack([turned(np.concatenate([g, u])) for g, u in
                               zip(np.asarray(L0_ffn_w_gate), np.asarray(L0_ffn_w_up))])),
        "wd": array(np.stack([turned(w) for w in np.asarray(L0_ffn_w_down)])),
    }
    nc = bacc.Bacc("TRN2", target_bir_lowering=False, num_devices=1)
    drams = {n: nc.dram_tensor(n, a.shape, F32, kind="ExternalInput").ap() for n, a in arrays.items()}
    out = nc.dram_tensor("out", (TOKENS, D), F32, kind="ExternalOutput").ap()
    build(nc, **drams, out=out)
    r = run_bass_kernel_spmd(nc, [arrays], core_ids=[0])
    return r.results[0]["out"].reshape(B, S, D)
```

```python
from contextlib import ExitStack

import concourse.bass as bass
from concourse import mybir

ALU = mybir.AluOpType
ACT = mybir.ActivationFunctionType
AX = mybir.AxisListType
F32 = mybir.dt.float32
F32R = mybir.dt.float32r
BF16 = mybir.dt.bfloat16
I32 = mybir.dt.int32
U32 = mybir.dt.uint32

P = 128
B, S, D = 4, 1024, 512
HEADS = 16
HD = D // HEADS
C = D // P
HG = P // HD
G = HEADS // HG
HALF = 512
NHALF = S // HALF
KT = S // P
EPS = 1e-5

STEPS = NHALF * KT
PROJ = 4
PRE = HG * KT * NHALF

SLOTS = 4
PRE_SLOTS = (3, 54)
PROJ_SLOTS = (40, 43, 46, 49)
ROW_SLOT = 56


def side_plan(with_proj):
    plan = [[] for _ in range(STEPS * SLOTS)]
    for u in range(PRE):
        plan[PRE_SLOTS[0] + u * (PRE_SLOTS[1] - PRE_SLOTS[0]) // PRE].append(("pre", u))
    if with_proj:
        for u, slot in enumerate(PROJ_SLOTS):
            plan[slot].append(("proj", u))
    plan[ROW_SLOT].append(("row", 0))
    place, count = {}, 0
    for slot in plan:
        for i, unit in enumerate(slot):
            place[unit] = count
            slot[i] = (*unit, count)
            count += 1
    return plan, place, count


PLAN, PLACE, SIDE = side_plan(True)
PLAN_LAST, PLACE_LAST, _ = side_plan(False)


def attention(nc, x, xT, wkqT, wvT, woT, bq, bk, bv, bo, x2):
    with ExitStack() as ctx:
        def sb(name, shape, dt=F32):
            return ctx.enter_context(nc.sbuf_tensor(name, shape, dt))

        def sem(name):
            return ctx.enter_context(nc.semaphore(name))

        ident = sb("ident", [P, P])
        ones = sb("ones", [P, HD])
        bkq = sb("bkq", [P, 2, G])
        bv_bc = sb("bv_bc", [P, D])
        bo_bc = sb("bo_bc", [P, D])
        wstage = sb("wstage", [P, C, P])
        wkq_hi = sb("wkq_hi", [P, 2, C, P], F32R)
        wkq_lo = sb("wkq_lo", [P, 2, C, P], F32R)
        wv_hi = sb("wv_hi", [P, C, D], F32R)
        wv_lo = sb("wv_lo", [P, C, D], F32R)
        wo = sb("wo", [P, C, D])
        xstage = sb("xstage", [P, 2, HALF])
        x_hi = sb("x_hi", [P, C, S], F32R)
        x_lo = sb("x_lo", [P, C, S], F32R)
        kq_hi = sb("kq_hi", [P, 2, S], F32R)
        kq_lo = sb("kq_lo", [P, 2, S], F32R)
        k_stack = [sb(f"k_stack{i}", [P, HG, S], F32R) for i in range(2)]
        q_stack = [sb(f"q_stack{i}", [P, HG, S], F32R) for i in range(2)]
        v_sb = sb("v_sb", [P, KT, D])
        probs = sb("probs", [P, 4, 2, HALF])
        ctx_sb = sb("ctx_sb", [P, G, S])
        max_half = sb("max_half", [P, HG * KT, NHALF])
        max_q = sb("max_q", [P, HG * KT])
        max_row = sb("max_row", [HG * KT, P], F32R)
        x_nat = probs[:].rearrange("p a c d -> p (a c) d")
        assert 8 * HALF == KT * D
        res = sb("res", [P, 2, D])
        rsum = res[:, 0, :]
        stats = sb("stats", [P, 2, 6])
        mv = sb("mv", [P, 2, 2])
        var_eps = sb("var_eps", [P, 2, 1])
        minus_half = sb("minus_half", [P, 1])
        rstd = sb("rstd", [P, 2, 1])

        ps_s = ctx.enter_context(nc.psum_tensor("ps_s", [P, 4, HALF], F32))
        ps_ctx = ctx.enter_context(nc.psum_tensor("ps_ctx", [P, HALF], F32))
        ps_sum = ctx.enter_context(nc.psum_tensor("ps_sum", [P, HALF], F32))
        ps_side = ctx.enter_context(nc.psum_tensor("ps_side", [P, 2, HALF], F32))

        const_in = sem("const_in")
        bias_in = sem("bias_in")
        passed = sem("passed")
        passed_sp = sem("passed_sp")
        const_set = sem("const_set")
        wv_split = sem("wv_split")
        w_in = sem("w_in")
        w_split = sem("w_split")
        x_in = [sem("x_in0"), sem("x_in1")]
        x_split = sem("x_split")
        wv_in = [sem("wv_in0"), sem("wv_in1")]
        w_high, x_high, wv_high = sem("w_high"), sem("x_high"), sem("wv_high")
        side_ready = sem("side_ready")
        side_hi = sem("side_hi")
        side_free = sem("side_free")
        stacked = [sem(f"stacked{h}") for h in range(HG)]
        max_made = sem("max_made")
        row_in = sem("row_in")
        scores_ready = sem("scores_ready")
        probs_ready = sem("probs_ready")
        pv_done = sem("pv_done")
        ctx_made = sem("ctx_made")
        ctx_taken = sem("ctx_taken")
        sum_taken = sem("sum_taken")
        recip_done = sem("recip_done")
        ctx_done = sem("ctx_done")
        tail_ready = sem("tail_ready")
        tail_free = sem("tail_free")
        xnat_in = [sem(f"xnat_in{i}") for i in range(KT // 2)]
        xbias = sem("xbias")
        ln_chain = sem("ln_chain")
        aggr_made = sem("aggr_made")
        var_made = sem("var_made")
        rstd_made = sem("rstd_made")
        x2_ready = sem("x2_ready")
        x2_out = [sem("x2_out0"), sem("x2_out1")]

        block = ctx.enter_context(nc.Block())

        BSTEPS = G * STEPS
        SPREAD = 16 * 6
        CONSTS = 16 * 3
        TAIL = 2 * KT
        CHUNKS = C * NHALF
        QUARTER = HALF // 4

        def base_of(m):
            return PROJ + (m + 1) * SIDE

        def side_in(last, loc, slot):
            g, i = loc // STEPS, loc % STEPS * SLOTS + slot
            if last and g == G - 1:
                return []
            return (PLAN_LAST if last and g == G - 2 else PLAN)[i]

        def prologue():
            for t in range(KT + 2):
                if t < KT:
                    yield t, None
                if t >= 2:
                    for slot in range((t - 2) * 8, (t - 1) * 8):
                        for what in PLAN[slot]:
                            yield slot, what

        @block.sync
        def _(sp):
            def load_w(n, g):
                for sel in range(2):
                    if not (isinstance(n, int) and n + sel == 0):
                        sp.wait_ge(w_split, 2 * n + sel)
                    sp.dma_start(wstage[:], wkqT[g, :, sel]).then_inc(w_in, 16)

            def load_x(b):
                for i in range(CHUNKS):
                    c, half = i % C, i // C
                    if i >= 2:
                        sp.wait_ge(x_split, b * CHUNKS + i - 1)
                    sp.dma_start(xstage[:, i % 2, :],
                                 xT[bass.ds(b, 1), :, c, half * HALF:(half + 1) * HALF].rearrange(
                                     "a p t -> (a p) t")).then_inc(x_in[i % 2], 16)

            def spread(staged, par):
                sp.wait_ge(side_free, staged)
                for h in range(HG):
                    for sel, dst, parts in ((0, k_stack[par], (kq_hi, kq_lo, kq_hi)),
                                            (1, q_stack[par], (kq_hi, kq_hi, kq_lo))):
                        for r, part in enumerate(parts):
                            sp.dma_start(dst[r * HD:(r + 1) * HD, h, :].bitcast(F32),
                                         part[h * HD:(h + 1) * HD, sel, :].bitcast(F32)).then_inc(stacked[h], 16)

            def send_rows(par):
                sp.dma_start(q_stack[par][3 * HD:3 * HD + 1, :, :].rearrange("a h (j q) -> a (h j) q", q=P).bitcast(F32),
                             max_row[:].bitcast(F32)).then_inc(row_in, 16)

            def body(m, g, last):
                if not (last and g > 0):
                    load_w(m + 3, (g + 3) % G)
                if not (last and g == G - 1):
                    sp.wait_ge(side_free, base_of(m) + (PLACE_LAST if last and g == G - 2 else PLACE)[("row", 0)] + 1)
                    send_rows((g + 1) % 2)
                if not (last and g >= G - 2):
                    sp.wait_ge(scores_ready, 2 * STEPS * (m + 1))
                    sp.sem_inc(passed_sp, 1)
                    spread(base_of(m) + PLACE[("proj", PROJ - 1)] + 1, g % 2)

            def tail(b):
                sp.wait_ge(pv_done, (b + 1) * BSTEPS)
                sp.sem_inc(passed_sp, 1)
                for i in range(KT // 2):
                    sp.dma_start(x_nat[:, 2 * i:2 * i + 2, :],
                                 x[bass.ds(b, 1), 2 * i * P:(2 * i + 2) * P, :].rearrange(
                                     "a (t p) d -> p (a t) d", p=P)).then_inc(xnat_in[i], 16)
                for t in range(KT):
                    store(b, t)

            def store(b, t):
                sp.wait_ge(x2_ready, b * KT + t + 1)
                sp.dma_start(x2[bass.ds(b, 1), t * P:(t + 1) * P, :].rearrange("a p d -> (a p) d"),
                             res[:, t % 2, :]).then_inc(x2_out[t % 2], 16)

            for i in range(2):
                sp.sem_inc(x2_out[i], 16)
            load_w(0, 0)
            load_x(0)
            for sel, src in ((0, bk), (1, bq)):
                sp.dma_start(bkq[:, sel, :], src).then_inc(bias_in, 16)
            for c in range(C):
                if c >= 2:
                    sp.wait_ge(wv_split, c - 1)
                else:
                    sp.wait_ge(x_split, CHUNKS - 1 + c)
                sp.dma_start(xstage[:, c % 2, :], wvT[:, c, :]).then_inc(wv_in[c % 2], 16)
            for t, src in ((bv_bc[:], bv.partition_broadcast(P)), (bo_bc[:], bo.partition_broadcast(P)), (wo[:], woT)):
                sp.dma_start(t, src).then_inc(const_in, 16)
            spread(PROJ, 0)
            load_w(1, 1)
            load_w(2, 2)
            sp.wait_ge(side_free, base_of(-1) + PLACE[("row", 0)] + 1)
            send_rows(0)
            spread(base_of(-1) + PLACE[("proj", PROJ - 1)] + 1, 1)
            with sp.Fori(0, B - 1) as b:
                for g in range(G):
                    body(b * G + g, g, False)
                    if g == 1:
                        load_x(b + 1)
                tail(b)
            b = B - 1
            for g in range(G):
                body(b * G + g, g, True)
            tail(b)
            for i in range(2):
                sp.wait_ge(x2_out[i], 16 * (B * KT // 2 + 1))

        @block.gpsimd
        def _(pool):
            nc.gpsimd.memset(ident[:], 0.0).then_inc(const_set, 1)
            pool.wait_ge(const_set, 1)
            nc.gpsimd.affine_select(out=ident[:], in_=ident[:], compare_op=ALU.not_equal, fill=1.0, base=0,
                                    pattern=[[-1, P]], channel_multiplier=1).then_inc(const_set, 1)
            pool.wait_ge(const_set, 2)
            nc.gpsimd.memset(ones[:], 1.0).then_inc(const_set, 1)
            for i in range(2):
                pool.wait_ge(const_set, 3 + i)
                nc.gpsimd.memset(k_stack[i][3 * HD:3 * HD + 1, :, :].bitcast(F32), 1.0).then_inc(const_set, 1)
            pool.wait_ge(const_set, 5)
            nc.gpsimd.memset(minus_half[:], -0.5).then_inc(const_set, 1)
            pool.wait_ge(const_set, 6)

            def split(hi, lo, raw, high_made, count, done):
                nc.gpsimd.tensor_copy(hi, raw).then_inc(high_made, 1)
                pool.wait_ge(high_made, count)
                nc.gpsimd.tensor_tensor(lo, raw, hi.bitcast(F32), ALU.subtract).then_inc(done, 1)

            def split_w(n):
                for sel in range(2):
                    pool.wait_ge(w_in, 16 * (2 * n + sel + 1))
                    pool.sem_inc(passed, 1)
                    split(wkq_hi[:, sel], wkq_lo[:, sel], wstage[:], w_high, 2 * n + sel + 1, w_split)

            def split_x(b):
                for i in range(CHUNKS):
                    c, half = i % C, i // C
                    pool.wait_ge(x_in[i % 2], 16 * (b * (CHUNKS // 2) + i // 2 + 1))
                    pool.sem_inc(passed, 1)
                    at = (slice(None), c, slice(half * HALF, (half + 1) * HALF))
                    split(x_hi[at], x_lo[at], xstage[:, i % 2, :], x_high, b * CHUNKS + i + 1, x_split)

            def projected(m):
                pool.wait_ge(side_ready, base_of(m) + PLACE[("proj", PROJ - 1)] + 1)

            def add_bo(b):
                for t in range(KT + 1):
                    if t < KT:
                        pool.wait_ge(xnat_in[t // 2], 16 * (b + 1))
                        nc.gpsimd.tensor_tensor(x_nat[:, t, :], x_nat[:, t, :], bo_bc[:],
                                                ALU.add).then_inc(xbias, 1)
                    if t >= 1:
                        s = (t - 1) % 2
                        pool.wait_ge(var_made, b * KT + t)
                        nc.gpsimd.tensor_tensor(rstd[:, s, :], var_eps[:, s, :], minus_half[:],
                                                ALU.pow).then_inc(rstd_made, 1)

            split_w(0)
            pool.wait_ge(side_ready, PROJ)
            split_w(1)
            projected(-1)
            split_w(2)
            pool.wait_ge(const_in, CONSTS)
            with pool.Fori(0, B - 1) as b:
                for g in range(G):
                    projected(b * G + g)
                    split_w(b * G + g + 3)
                    if g == 1:
                        split_x(b + 1)
                add_bo(b)
            b = B - 1
            projected(b * G)
            split_w(b * G + 3)
            add_bo(b)

        @block.tensor
        def _(pe):
            def three(out, terms, first, last):
                for i, (w, m) in enumerate(terms):
                    done = nc.tensor.matmul(out, w, m, start=first and i == 0, stop=last and i == 2)
                return done

            def project(n, u, at, bank, first):
                if u == 0:
                    pe.wait_ge(w_split, 2 * n + 2)
                if not (isinstance(at, int) and at < 2):
                    pe.wait_ge(side_free, at - 1)
                sel, half = u // 2, u % 2
                for c in range(C):
                    if first:
                        pe.wait_ge(x_split, half * C + c + 1)
                    wh, wl = wkq_hi[:, sel, c, :], wkq_lo[:, sel, c, :]
                    xh = x_hi[:, c, half * HALF:(half + 1) * HALF]
                    xl = x_lo[:, c, half * HALF:(half + 1) * HALF]
                    done = three(bank, ((wh, xh), (wl, xh), (wh, xl)), c == 0, c == C - 1)
                done.then_inc(side_ready, 1)

            def side_unit(m, g, kind, u, place):
                at = base_of(m) + place
                bank = ps_side[:, (base_of(g) + place) % 2, :]
                par = (g + 1) % 2
                if kind == "proj":
                    project(m + 2, u, at, bank, False)
                elif kind == "pre":
                    h, j, half = u // (KT * NHALF), u // NHALF % KT, u % NHALF
                    if j == 0 and half == 0:
                        pe.wait_ge(stacked[h], SPREAD * (m + 2))
                    pe.wait_ge(side_free, at - 1)
                    nc.tensor.matmul(bank, q_stack[par][0:3 * HD, h, j * P:(j + 1) * P],
                                     k_stack[par][0:3 * HD, h, half * HALF:(half + 1) * HALF],
                                     start=True, stop=True).then_inc(side_ready, 1)
                else:
                    pe.wait_ge(side_free, at - 1)
                    pe.wait_ge(max_made, m + 2)
                    nc.tensor.transpose(bank[0:HG * KT, 0:P], max_q[:], ident[:]).then_inc(side_ready, 1)

            def scores(b, loc, pair):
                g, half, kt = loc // STEPS, loc // KT % NHALF, loc % KT
                par = g % 2
                if loc % STEPS == 0 and pair == 0:
                    pe.wait_ge(row_in, 16 * (b * G + g + 1))
                if loc:
                    pe.wait_ge(probs_ready, b * 2 * BSTEPS + 2 * loc + pair - 1)
                for h in (2 * pair, 2 * pair + 1):
                    done = nc.tensor.matmul(ps_s[:, h, :], k_stack[par][0:3 * HD + 1, h, kt * P:(kt + 1) * P],
                                            q_stack[par][0:3 * HD + 1, h, half * HALF:(half + 1) * HALF],
                                            start=True, stop=True)
                done.then_inc(scores_ready, 1)

            def weighted(b, loc, is_sum):
                g, half, kt = loc // STEPS, loc // KT % NHALF, loc % KT
                out = ps_sum if is_sum else ps_ctx
                pe.wait_ge(probs_ready, b * 2 * BSTEPS + 2 * loc + 2)
                if kt == 0 and loc:
                    pe.wait_ge(sum_taken if is_sum else ctx_taken, b * G * NHALF + loc // KT)
                for h in range(HG):
                    lhsT = ones[:] if is_sum else v_sb[:, kt, (g * HG + h) * HD:(g * HG + h + 1) * HD]
                    done = nc.tensor.matmul(out[h * HD:(h + 1) * HD, :], lhsT,
                                            probs[:, (2 * loc + h // 2) % 4, h % 2, :],
                                            start=kt == 0, stop=kt == KT - 1)
                if is_sum:
                    done.then_inc(pv_done, 1)
                elif kt == KT - 1:
                    done.then_inc(ctx_made, 1)

            def v_tile(u, t):
                if t >= 4 or not isinstance(u, int):
                    pe.wait_ge(tail_free, u - 3)
                for c in range(C):
                    xh, xl = x_hi[:, c, t * P:(t + 1) * P], x_lo[:, c, t * P:(t + 1) * P]
                    wh, wl = wv_hi[:, c, :], wv_lo[:, c, :]
                    done = three(ps_s[:, t % 4, :], ((xh, wh), (xl, wh), (xh, wl)), c == 0, c == C - 1)
                done.then_inc(tail_ready, 1)

            def o_tile(u, t):
                pe.wait_ge(tail_free, u - 3)
                for g in range(G):
                    done = nc.tensor.matmul(ps_s[:, t % 4, :], ctx_sb[:, g, t * P:(t + 1) * P], wo[:, g, :],
                                            start=g == 0, stop=g == G - 1)
                done.then_inc(tail_ready, 1)

            def batch(b, last):
                for pair in range(2):
                    scores(b, 0, pair)
                for loc in range(BSTEPS):
                    g = loc // STEPS
                    for slot in range(SLOTS):
                        if slot >= 2:
                            weighted(b, loc, slot == 3)
                        elif loc + 1 < BSTEPS:
                            scores(b, loc + 1, slot)
                        for kind, u, place in side_in(last, loc, slot):
                            if kind == "proj" and u == 0 and g == 2:
                                pe.wait_ge(x_split, (b + 2) * CHUNKS)
                            side_unit(b * G + g, g, kind, u, place)

            for u in range(PROJ):
                project(0, u, u, ps_side[:, u % 2, :], True)
            pe.wait_ge(wv_split, C)
            pe.wait_ge(const_set, 5)
            for slot, what in prologue():
                if what is None:
                    v_tile(slot, slot)
                else:
                    side_unit(-1, -1, *what)
            pe.wait_ge(const_in, CONSTS)
            with pe.Fori(0, B - 1) as b:
                pe.wait_ge(tail_free, b * TAIL + KT)
                batch(b, False)
                for t in range(KT):
                    v_tile(b * TAIL + KT + t, t)
                pe.wait_ge(ctx_done, (b + 1) * G * NHALF)
                for t in range(KT):
                    o_tile(b * TAIL + 2 * KT + t, t)
            b = B - 1
            pe.wait_ge(tail_free, b * TAIL + KT)
            batch(b, True)
            pe.wait_ge(ctx_done, (b + 1) * G * NHALF)
            for t in range(KT):
                o_tile(b * TAIL + KT + t, t)

        @block.scalar
        def _(act):
            def project(n, u, at, bank, g):
                sel, half = u // 2, u % 2
                act.wait_ge(side_ready, at + 1)
                if not (isinstance(n, int) and n == 0):
                    for s in stacked:
                        act.wait_ge(s, SPREAD * n)
                nc.scalar.activation(kq_hi[:, sel, half * HALF:(half + 1) * HALF], bank, ACT.Identity,
                                     bias=bkq[:, sel, g:g + 1]).then_inc(side_hi, 1)

            def side_unit(m, g, kind, u, place):
                if kind == "proj":
                    project(m + 2, u, base_of(m) + place, ps_side[:, (base_of(g) + place) % 2, :], (g + 2) % G)

            def exps(b, loc, pair):
                act.wait_ge(scores_ready, b * 2 * BSTEPS + 2 * loc + pair + 1)
                if loc >= 2:
                    act.wait_ge(pv_done, b * BSTEPS + loc - 1)
                nc.scalar.activation(probs[:, (2 * loc + pair) % 4, :, :], ps_s[:, 2 * pair:2 * pair + 2, :],
                                     ACT.Exp, scale=HD ** -0.5).then_inc(probs_ready, 1)

            def take(b, loc):
                k = b * G * NHALF + loc // KT
                g, half = loc // STEPS, loc // KT % NHALF
                act.wait_ge(ctx_made, k + 1)
                nc.scalar.activation(ctx_sb[:, g, half * HALF:(half + 1) * HALF], ps_ctx[:],
                                     ACT.Identity).then_inc(ctx_taken, 1)
                act.wait_ge(pv_done, b * BSTEPS + loc + 1)
                if loc >= KT:
                    act.wait_ge(ctx_done, k)
                else:
                    act.wait_ge(x2_out[0], 16 * (b * (KT // 2) + 1))
                nc.scalar.activation(rsum, ps_sum[:], ACT.Identity).then_inc(sum_taken, 1)

            def batch(b, last):
                for pair in range(2):
                    exps(b, 0, pair)
                for loc in range(BSTEPS):
                    g = loc // STEPS
                    for slot in range(SLOTS):
                        if slot < 2 and loc + 1 < BSTEPS:
                            exps(b, loc + 1, slot)
                        for kind, u, place in side_in(last, loc, slot):
                            side_unit(b * G + g, g, kind, u, place)
                    if loc % KT == KT - 1:
                        take(b, loc)

            for i in range(CHUNKS):
                c, half = i % C, i // C
                act.wait_ge(x_in[i % 2], 16 * (i // 2 + 1))
                nc.scalar.activation(x_hi[:, c, half * HALF:(half + 1) * HALF], xstage[:, i % 2, :],
                                     ACT.Copy).then_inc(x_high, 1)
            act.wait_ge(bias_in, 32)
            for u in range(PROJ):
                project(0, u, u, ps_side[:, u % 2, :], 0)
                act.wait_ge(wv_in[u % 2], 16 * (u // 2 + 1))
                nc.scalar.activation(wv_hi[:, u, :], xstage[:, u % 2, :], ACT.Copy).then_inc(wv_high, 1)
            for slot, what in prologue():
                if what is not None:
                    side_unit(-1, -1, *what)
            with act.Fori(0, B - 1) as b:
                batch(b, False)
            batch(B - 1, True)

        @block.vector
        def _(dve):
            def project(n, u, bank, g):
                sel, half = u // 2, slice(u % 2 * HALF, (u % 2 + 1) * HALF)
                dve.wait_ge(side_hi, n * PROJ + u + 1)
                if not (isinstance(n, int) and n == 0):
                    for s in stacked:
                        dve.wait_ge(s, SPREAD * n)
                nc.vector.scalar_tensor_tensor(out=kq_lo[:, sel, half], in0=bank, scalar=bkq[:, sel, g:g + 1],
                                               in1=kq_hi[:, sel, half].bitcast(F32), op0=ALU.add,
                                               op1=ALU.subtract).then_inc(side_free, 1)

            def side_unit(m, g, kind, u, place):
                at = base_of(m) + place
                bank = ps_side[:, (base_of(g) + place) % 2, :]
                if kind == "proj":
                    project(m + 2, u, bank, (g + 2) % G)
                elif kind == "pre":
                    dve.wait_ge(side_ready, at + 1)
                    nc.vector.reduce_max(max_half[:, u // 2, u % 2:u % 2 + 1], bank, AX.X).then_inc(side_free, 1)
                    if u == PRE - 1:
                        dve.wait_ge(side_free, at + 1)
                        nc.vector.tensor_reduce(out=max_q[:], in_=max_half[:], axis=AX.X, op=ALU.max,
                                                negate=True).then_inc(max_made, 1)
                else:
                    dve.wait_ge(side_ready, at + 1)
                    if not (isinstance(m, int) and m < 0):
                        dve.wait_ge(row_in, 16 * (m + 1))
                    nc.vector.tensor_copy(max_row[:], bank[0:HG * KT, 0:P]).then_inc(side_free, 1)

            def invert(b, loc, quarter):
                k = b * G * NHALF + loc // KT
                at = rsum[:, quarter * QUARTER:(quarter + 1) * QUARTER]
                dve.wait_ge(sum_taken, k + 1)
                nc.vector.reciprocal(at, at).then_inc(recip_done, 1)

            def normalise(b, loc):
                k = b * G * NHALF + loc // KT
                g, half = loc // STEPS, loc // KT % NHALF
                out = ctx_sb[:, g, half * HALF:(half + 1) * HALF]
                dve.wait_ge(recip_done, 4 * (k + 1))
                nc.vector.tensor_tensor(out, out, rsum, ALU.mult).then_inc(ctx_done, 1)

            def batch(b, last):
                for loc in range(BSTEPS):
                    g = loc // STEPS
                    for slot in range(SLOTS):
                        for kind, u, place in side_in(last, loc, slot):
                            side_unit(b * G + g, g, kind, u, place)
                        i = (loc % KT) * SLOTS + slot - 2
                        if loc >= KT and i >= 0:
                            ended = loc - loc % KT - 1
                            if i % 3 == 0 and i // 3 < 4:
                                invert(b, ended, i // 3)
                            if i == 12:
                                normalise(b, ended)

            def v_tile(u, t):
                dve.wait_ge(tail_ready, u + 1)
                nc.vector.tensor_tensor(v_sb[:, t, :], ps_s[:, t % 4, :], bv_bc[:], ALU.add).then_inc(tail_free, 1)

            def o_tile(u, b, t):
                s = t % 2
                k = b * KT + t
                dve.wait_ge(tail_ready, u + 1)
                dve.wait_ge(xbias, k + 1)
                dve.wait_ge(x2_out[s], 16 * (b * (KT // 2) + t // 2 + 1))
                nc.vector.tensor_tensor(res[:, s, :], ps_s[:, t % 4, :], x_nat[:, t, :], ALU.add).then_inc(tail_free, 1)
                dve.wait_ge(tail_free, u + 1)
                nc.vector.bn_stats(stats[:, s, :], res[:, s, :]).then_inc(ln_chain, 1)
                dve.wait_ge(const_in, CONSTS)
                dve.wait_ge(ln_chain, k + 1)
                nc.vector.bn_aggr(mv[:, s, :], stats[:, s, :]).then_inc(aggr_made, 1)
                dve.wait_ge(aggr_made, k + 1)
                nc.vector.tensor_scalar(var_eps[:, s, :], mv[:, s, 1:2], EPS, None, ALU.add).then_inc(var_made, 1)
                dve.wait_ge(rstd_made, k + 1)
                nc.vector.tensor_scalar(res[:, s, :], res[:, s, :], mv[:, s, 0:1], rstd[:, s, :],
                                        ALU.subtract, ALU.mult).then_inc(x2_ready, 1)

            for i in range(CHUNKS):
                at = (slice(None), i % C, slice(i // C * HALF, (i // C + 1) * HALF))
                dve.wait_ge(x_high, i + 1)
                nc.vector.tensor_tensor(x_lo[at], xstage[:, i % 2, :], x_hi[at].bitcast(F32),
                                        ALU.subtract).then_inc(x_split, 1)
            dve.wait_ge(bias_in, 32)
            for u in range(PROJ):
                project(0, u, ps_side[:, u % 2, :], 0)
                dve.wait_ge(wv_high, u + 1)
                nc.vector.tensor_tensor(wv_lo[:, u, :], xstage[:, u % 2, :], wv_hi[:, u, :].bitcast(F32),
                                        ALU.subtract).then_inc(wv_split, 1)
            dve.wait_ge(const_in, CONSTS)
            for slot, what in prologue():
                if what is None:
                    v_tile(slot, slot)
                else:
                    side_unit(-1, -1, *what)
            with dve.Fori(0, B - 1) as b:
                batch(b, False)
                for t in range(KT):
                    if t < 4:
                        invert(b, BSTEPS - 1, t)
                    if t == 4:
                        normalise(b, BSTEPS - 1)
                    v_tile(b * TAIL + KT + t, t)
                for t in range(KT):
                    o_tile(b * TAIL + 2 * KT + t, b, t)
            b = B - 1
            batch(b, True)
            for t in range(4):
                invert(b, BSTEPS - 1, t)
            normalise(b, BSTEPS - 1)
            for t in range(KT):
                o_tile(b * TAIL + KT + t, b, t)


TOKENS = B * S
TT = TOKENS // P
E = 8
H = 256
CH = H // P
NT = 2 * TT + E
SLOTS_ALL = NT * P
RW = 16


def shared_and_scores(nc, x2, shg, shu, shd, rw, wgu, wd, base, gu_sb, wd_sb, gu_in, route, ident):
    with ExitStack() as ctx:
        def sb(name, shape, dt=F32):
            return ctx.enter_context(nc.sbuf_tensor(name, shape, dt))

        def sem(name):
            return ctx.enter_context(nc.semaphore(name))

        def psum(name, shape):
            return ctx.enter_context(nc.psum_tensor(name, shape, F32))

        wstage = sb("sh_stage", [P, 2, C, D])
        sgu_hi = sb("sgu_hi", [P, C, 2, D], F32R)
        sgu_lo = sb("sgu_lo", [P, C, 2, D], F32R)
        sd_hi = sb("sd_hi", [P, C, D], F32R)
        sd_lo = sb("sd_lo", [P, C, D], F32R)
        rw_raw = sb("rw_raw", [P, C, RW])
        rw_hi = sb("rw_hi", [P, C, RW], F32R)
        rw_lo = sb("rw_lo", [P, C, RW], F32R)
        x_t = sb("x_t", [P, 4, D])
        xT_hi = sb("xT_hi", [P, 2, C, P], F32R)
        xT_lo = sb("xT_lo", [P, 2, C, P], F32R)
        act_g = sb("act_g", [P, 2, D])
        hid = sb("hid", [P, 2, D])
        hT_hi = sb("hT_hi", [P, 2, C, P], F32R)
        hT_lo = sb("hT_lo", [P, 2, C, P], F32R)
        th = sb("th", [P, 2, 1])
        sgate = sb("sgate", [P, 2, 1])
        out_t = sb("out_t", [P, 2, D])

        ps_t = psum("ps_t", [P, 2, D])
        ps_gu = psum("ps_gu", [P, 2, D])
        ps_r = psum("ps_r", [P, D])
        ps_ht = psum("ps_ht", [P, D])
        ps_d = psum("ps_d", [P, 2, D])

        st_in = [sem(f"st_in{i}") for i in range(6)]
        st_high = sem("st_high")
        st_split = sem("st_split")
        rw_zero = sem("rw_zero")
        rw_in = sem("rw_in")
        x_in = [sem(f"xt_in{i}") for i in range(4)]
        t_ready = sem("t_ready")
        t_hi = sem("t_hi")
        t_lo = sem("t_lo")
        gu_ready = sem("gu_ready")
        silu_done = sem("silu_done")
        hid_done = sem("hid_done")
        sc_done = sem("sc_done")
        th_done = sem("th_done")
        gate_done = sem("gate_done")
        ht_ready = sem("ht_ready")
        ht_hi = sem("ht_hi")
        ht_lo = sem("ht_lo")
        d_ready = sem("d_ready")
        base_done = sem("base_done")
        base_out = [sem("base_out0"), sem("base_out1")]

        shared = (shg, shu, shd)
        PIECES = len(shared) * C

        def piece(i):
            k, c = i // C, i % C
            hi, lo = (sd_hi[:, c, :], sd_lo[:, c, :]) if k == 2 else (sgu_hi[:, c, k, :], sgu_lo[:, c, k, :])
            return wstage[:, k % 2, c, :], hi, lo

        block = ctx.enter_context(nc.Block())

        @block.sync
        def _(sp):
            sp.wait_ge(rw_zero, 1)
            def load_tile(t, s):
                sp.dma_start(x_t[:, s, :], x2[bass.ds(t * P, P), :]).then_inc(x_in[s], 16)

            load_tile(0, 0)
            for i in range(2 * len(shared)):
                k, c = i // 2, i % 2 * (C // 2)
                if k == 2:
                    sp.wait_ge(st_split, c + C // 2)
                sp.dma_start(wstage[:, k % 2, c:c + C // 2], shared[k][:, c:c + C // 2, :]).then_inc(st_in[i], 16)
                if i < 3:
                    load_tile(i + 1, i + 1)
            sp.dma_start(rw_raw[:, :, 0:E + 1], rw).then_inc(rw_in, 16)
            for e in range(E):
                sp.dma_start(gu_sb[:, e], wgu[e]).then_inc(gu_in, 16)
                sp.dma_start(wd_sb[:, e], wd[e]).then_inc(gu_in, 16)

            def store(t, s):
                sp.wait_ge(base_done, t + 1)
                sp.dma_start(base[bass.ds(t * P, P), :], out_t[:, s % 2, :]).then_inc(base_out[s % 2], 16)

            with sp.Fori(0, TT // 4 - 1) as j:
                for s in range(4):
                    store(4 * j + s, s)
                    load_tile(4 * j + s + 4, s)
            for s in range(4):
                store(TT - 4 + s, s)
            for i in range(2):
                sp.wait_ge(base_out[i], 16 * TT // 2)

        @block.gpsimd
        def _(pool):
            nc.gpsimd.memset(rw_raw[:], 0.0).then_inc(rw_zero, 1)

        def pipeline(eng, step):
            step(0, 0, True, False)
            for s in range(1, 4):
                step(s, s, False, False)
            with eng.Fori(1, TT // 4 - 1) as j:
                for s in range(4):
                    step(4 * j + s, s, False, False)
            for s in range(4):
                step(TT - 4 + s, s, False, s == 3)

        @block.tensor
        def _(pe):
            def turn(t, s):
                pe.wait_ge(x_in[s], 16 * (t // 4 + 1) if isinstance(t, int) else x_count(t, s))
                if not (isinstance(t, int) and t < 2):
                    pe.wait_ge(t_hi, t - 1)
                    pe.wait_ge(t_lo, t - 1)
                for c in range(C):
                    done = nc.tensor.transpose(ps_t[:, s % 2, c * P:(c + 1) * P],
                                               x_t[:, s, c * P:(c + 1) * P], ident[:])
                done.then_inc(t_ready, 1)

            def x_count(t, s):
                return (t - s) * 4 + 16

            def three(out, a, b, c, last_c):
                for i, (w, m) in enumerate(((a[0], b[0]), (a[1], b[0]), (a[0], b[1]))):
                    done = nc.tensor.matmul(out, w, m, start=c == 0 and i == 0, stop=c == last_c and i == 2)
                return done

            def up(t, s):
                pe.wait_ge(t_hi, t + 1)
                pe.wait_ge(t_lo, t + 1)
                if not (isinstance(t, int) and t < 1):
                    pe.wait_ge(hid_done, t)
                    pe.wait_ge(sc_done, t)
                    pe.wait_ge(th_done, t)
                for out, m_of in ((ps_r[:, 0:RW], lambda c: (rw_hi[:, c, :], rw_lo[:, c, :])),
                                  (ps_gu[:, 0, :], lambda c: (sgu_hi[:, c, 0, :], sgu_lo[:, c, 0, :])),
                                  (ps_gu[:, 1, :], lambda c: (sgu_hi[:, c, 1, :], sgu_lo[:, c, 1, :]))):
                    for c in range(C):
                        done = three(out, (xT_hi[:, s % 2, c, :], xT_lo[:, s % 2, c, :]), m_of(c), c, C - 1)
                done.then_inc(gu_ready, 1)

            def turn_hidden(t, s):
                pe.wait_ge(hid_done, t + 1)
                if not (isinstance(t, int) and t < 1):
                    pe.wait_ge(ht_hi, t)
                    pe.wait_ge(ht_lo, t)
                for c in range(C):
                    done = nc.tensor.transpose(ps_ht[:, c * P:(c + 1) * P], hid[:, s % 2, c * P:(c + 1) * P], ident[:])
                done.then_inc(ht_ready, 1)

            def down(t, s):
                pe.wait_ge(ht_hi, t + 1)
                pe.wait_ge(ht_lo, t + 1)
                if not (isinstance(t, int) and t < 2):
                    pe.wait_ge(base_done, t - 1)
                for c in range(C):
                    done = three(ps_d[:, s % 2, :], (hT_hi[:, s % 2, c, :], hT_lo[:, s % 2, c, :]),
                                 (sd_hi[:, c, :], sd_lo[:, c, :]), c, C - 1)
                done.then_inc(d_ready, 1)

            def step(t, s, first, last):
                if first:
                    turn(t, s)
                up(t, s)
                if not last:
                    turn(t + 1, (s + 1) % 4)
                if not first:
                    down(t - 1, s - 1 if s else 3)
                turn_hidden(t, s)
                if last:
                    down(t, s)

            pe.wait_ge(st_split, PIECES + 1)
            pipeline(pe, step)

        @block.scalar
        def _(act):
            def x_high(t, s):
                act.wait_ge(t_ready, t + 1)
                if not (isinstance(t, int) and t < 2):
                    act.wait_ge(gu_ready, t - 1)
                nc.scalar.activation(xT_hi[:, s % 2], ps_t[:, s % 2, :].rearrange("p (c t) -> p c t", c=C),
                                     ACT.Copy).then_inc(t_hi, 1)

            def gate(t, s):
                act.wait_ge(gu_ready, t + 1)
                if not (isinstance(t, int) and t < 2):
                    act.wait_ge(hid_done, t - 1)
                    act.wait_ge(gate_done, t - 1)
                nc.scalar.activation(act_g[:, s % 2, :], ps_gu[:, 0, :], ACT.Silu).then_inc(silu_done, 1)
                nc.scalar.activation(th[:, s % 2, :], ps_r[:, E:E + 1], ACT.Tanh, scale=0.5).then_inc(th_done, 1)

            def h_high(t, s):
                act.wait_ge(ht_ready, t + 1)
                if not (isinstance(t, int) and t < 2):
                    act.wait_ge(d_ready, t - 1)
                nc.scalar.activation(hT_hi[:, s % 2], ps_ht[:].rearrange("p (c t) -> p c t", c=C),
                                     ACT.Copy).then_inc(ht_hi, 1)

            def step(t, s, first, last):
                if first:
                    x_high(t, s)
                gate(t, s)
                if not last:
                    x_high(t + 1, s + 1)
                h_high(t, s)

            for i in range(PIECES):
                raw, hi, _ = piece(i)
                if i % 2 == 0:
                    act.wait_ge(st_in[i // 2], 16)
                nc.scalar.activation(hi, raw, ACT.Copy).then_inc(st_high, 1)
            act.wait_ge(rw_in, 16)
            nc.scalar.activation(rw_hi[:], rw_raw[:], ACT.Copy).then_inc(st_high, 1)
            pipeline(act, step)

        @block.vector
        def _(dve):
            def x_low(t, s):
                dve.wait_ge(t_hi, t + 1)
                if not (isinstance(t, int) and t < 2):
                    dve.wait_ge(gu_ready, t - 1)
                nc.vector.tensor_tensor(xT_lo[:, s % 2], ps_t[:, s % 2, :].rearrange("p (c t) -> p c t", c=C),
                                        xT_hi[:, s % 2].bitcast(F32), ALU.subtract).then_inc(t_lo, 1)

            def hidden(t, s):
                dve.wait_ge(silu_done, t + 1)
                if not (isinstance(t, int) and t < 2):
                    dve.wait_ge(ht_ready, t - 1)
                nc.vector.tensor_tensor(hid[:, s % 2, :], act_g[:, s % 2, :], ps_gu[:, 1, :],
                                        ALU.mult).then_inc(hid_done, 1)
                dve.wait_ge(th_done, t + 1)
                nc.vector.tensor_copy(route[:, bass.ds(t, 1), :].rearrange("p a e -> p (a e)"),
                                      ps_r[:, 0:E]).then_inc(sc_done, 1)
                if not (isinstance(t, int) and t < 2):
                    dve.wait_ge(base_done, t - 1)
                nc.vector.tensor_scalar(sgate[:, s % 2, :], th[:, s % 2, :], 0.5, 0.5, ALU.mult,
                                        ALU.add).then_inc(gate_done, 1)

            def h_low(t, s):
                dve.wait_ge(ht_hi, t + 1)
                if not (isinstance(t, int) and t < 2):
                    dve.wait_ge(d_ready, t - 1)
                nc.vector.tensor_tensor(hT_lo[:, s % 2], ps_ht[:].rearrange("p (c t) -> p c t", c=C),
                                        hT_hi[:, s % 2].bitcast(F32), ALU.subtract).then_inc(ht_lo, 1)

            def finish(t, s):
                dve.wait_ge(d_ready, t + 1)
                dve.wait_ge(gate_done, t + 1)
                if not (isinstance(t, int) and t < 2):
                    dve.wait_ge(base_out[s % 2], 16 * (t // 2) if isinstance(t, int) else 8 * (t - s % 2))
                nc.vector.scalar_tensor_tensor(out=out_t[:, s % 2, :], in0=ps_d[:, s % 2, :], scalar=sgate[:, s % 2, :],
                                               in1=x_t[:, s, :], op0=ALU.mult, op1=ALU.add).then_inc(base_done, 1)

            def step(t, s, first, last):
                if first:
                    x_low(t, s)
                hidden(t, s)
                if not last:
                    x_low(t + 1, s + 1)
                if not first:
                    finish(t - 1, s - 1 if s else 3)
                h_low(t, s)
                if last:
                    finish(t, s)

            for i in range(PIECES):
                raw, hi, lo = piece(i)
                dve.wait_ge(st_high, i + 1)
                nc.vector.tensor_tensor(lo, raw, hi.bitcast(F32), ALU.subtract).then_inc(st_split, 1)
            dve.wait_ge(st_high, PIECES + 1)
            nc.vector.tensor_tensor(rw_lo[:], rw_raw[:], rw_hi[:].bitcast(F32), ALU.subtract).then_inc(st_split, 1)
            pipeline(dve, step)


def place(nc, route, weights, pos, tile_expert, table, ident):
    with ExitStack() as ctx:
        def sb(name, shape, dt=F32):
            return ctx.enter_context(nc.sbuf_tensor(name, shape, dt))

        def sem(name):
            return ctx.enter_context(nc.semaphore(name))

        expert = sb("expert", [P, TT, E])
        expert_i = sb("expert_i", [P, TT, E], I32)
        tri = sb("tri", [P, P])
        all_ones = sb("all_ones", [P, P])
        token = sb("token", [P, TT], I32)
        tile_start_i = sb("tile_start_i", [P, NT, E], I32)
        tile_start = sb("tile_start", [P, NT, E])
        zero_table = sb("zero_table", [P, NT], I32)
        big = [sb(f"big{i}", [P, TT, E]) for i in range(6)]
        one = [sb(f"one{i}", [P, 2, TT, E]) for i in range(1)][0]
        col = [sb(f"col{i}", [P, TT]) for i in range(8)]
        cnt = [sb(f"cnt{i}", [P, E]) for i in range(6)]
        cnt_i = [sb(f"cnt_i{i}", [P, E], I32) for i in range(3)]
        col_i = [sb(f"col_i{i}", [P, 2, TT], I32) for i in range(5)]
        ends = sb("ends", [P, NT, E])
        te = sb("te", [P, NT])
        index = sb("index", [P, 8], I32)
        who = sb("who", [P, 4], I32)
        ps_rank = ctx.enter_context(nc.psum_tensor("ps_rank", [P, TT * E], F32))
        ps_total = ctx.enter_context(nc.psum_tensor("ps_total", [P, TT * E], F32))

        passed = sem("passed_p")
        made = sem("made")
        zeroed = sem("zeroed")
        links = sem("links")
        visits = sem("visits")
        counted = sem("counted")
        gap_ready = sem("gap_ready")
        exp_done = sem("exp_done")
        placed = sem("placed")
        copied = sem("copied")
        scattered = [sem(f"scattered{i}") for i in range(8)]

        block = ctx.enter_context(nc.Block())

        @block.gpsimd
        def _(pool):
            n = [0]

            def after(ins):
                n[0] += 1
                ins.then_inc(made, 1)
                pool.wait_ge(made, n[0])

            after(nc.gpsimd.iota(expert_i[:], [[0, TT], [1, E]], base=0, channel_multiplier=0))
            after(nc.gpsimd.iota(token[:], [[P, TT]], base=0, channel_multiplier=1))
            after(nc.gpsimd.iota(tile_start_i[:], [[P, NT], [0, E]], base=0, channel_multiplier=0))
            after(nc.gpsimd.memset(all_ones[:], 1.0))
            after(nc.gpsimd.memset(zero_table[:], 0))
            after(nc.gpsimd.affine_select(out=tri[:], in_=all_ones[:], compare_op=ALU.is_gt, fill=0.0, base=0,
                                          pattern=[[1, P]], channel_multiplier=-1))
            pool.wait_ge(placed, 1)
            pool.wait_ge(zeroed, 16)
            def scatter(j, first):
                for s in range(4):
                    if not first:
                        for v in range(2):
                            pool.wait_ge(scattered[2 * s + v], 16 * j)
                        pool.sem_inc(passed, 1)
                    nc.gpsimd.tensor_copy(who[:, s:s + 1], token[:, bass.ds(4 * j + s, 1)]).then_inc(copied, 1)
                    for v in range(2):
                        nc.gpsimd.tensor_copy(index[:, 2 * s + v:2 * s + v + 1],
                                              col_i[4][:, v, bass.ds(4 * j + s, 1)]).then_inc(copied, 1)
                    pool.wait_ge(copied, 12 * j + 3 * s + 3)
                    pool.sem_inc(passed, 1)
                    for v in range(2):
                        nc.gpsimd.indirect_dma_start(
                            table, bass.IndirectOffsetOnAxis(ap=index[:, 2 * s + v:2 * s + v + 1].bitcast(U32), axis=0),
                            who[:, s:s + 1], None).then_inc(scattered[2 * s + v], 16)

            scatter(0, True)
            with pool.Fori(1, TT // 4) as j:
                scatter(j, False)
            for i in range(8):
                pool.wait_ge(scattered[i], 16 * (TT // 4))

        @block.sync
        def _(sp):
            sp.wait_ge(made, 5)
            sp.dma_start(table.rearrange("(p n) a -> p (n a)", p=P), zero_table[:]).then_inc(zeroed, 16)
            sp.wait_ge(zeroed, 16)

        @block.tensor
        def _(pe):
            pe.wait_ge(made, 6)
            pe.wait_ge(visits, 1)
            flat = big[4][:].rearrange("p t e -> p (t e)")
            nc.tensor.matmul(ps_rank[:], tri[:], flat, start=True, stop=True)
            nc.tensor.matmul(ps_total[:], all_ones[:], flat, start=True, stop=True).then_inc(counted, 1)

        @block.scalar
        def _(act):
            act.wait_ge(gap_ready, 1)
            nc.scalar.activation(col[4][:], col[3][:], ACT.Exp).then_inc(exp_done, 1)

        @block.vector
        def _(dve):
            n = [0]

            def link(ins):
                n[0] += 1
                ins.then_inc(links, 1)
                dve.wait_ge(links, n[0])

            def over_experts(x):
                return x.unsqueeze(2).broadcast_to((P, TT, E))

            v = nc.vector
            dve.wait_ge(made, 3)
            link(v.tensor_copy(expert[:], expert_i[:]))
            link(v.tensor_copy(tile_start[:], tile_start_i[:]))

            def pick(scores, largest, chosen):
                link(v.tensor_reduce(out=largest[:], in_=scores, axis=AX.X, op=ALU.max))
                link(v.tensor_tensor(big[0][:], scores, over_experts(largest[:]), ALU.is_equal))
                link(v.scalar_tensor_tensor(out=big[0][:], in0=big[0][:], scalar=-float(E), in1=expert[:],
                                            op0=ALU.mult, op1=ALU.add))
                link(v.tensor_reduce(out=col[2][:], in_=big[0][:], axis=AX.X, op=ALU.min))
                link(v.tensor_scalar(col[2][:], col[2][:], float(E), None, ALU.add))
                link(v.tensor_tensor(chosen, expert[:], over_experts(col[2][:]), ALU.is_equal))

            pick(route[:], col[0], one[:, 0])
            link(v.tensor_scalar(big[1][:], one[:, 0], -3.0e38, None, ALU.mult))
            link(v.tensor_scalar(big[2][:], one[:, 0], -3.0e38, 3.0e38, ALU.mult, ALU.add))
            link(v.tensor_tensor(big[1][:], big[1][:], big[2][:], ALU.add))
            link(v.tensor_tensor(big[1][:], route[:], big[1][:], ALU.min))
            pick(big[1][:], col[1], one[:, 1])
            link(v.tensor_tensor(big[4][:], one[:, 0], one[:, 1], ALU.add))
            v.tensor_tensor(col[3][:], col[1][:], col[0][:], ALU.subtract).then_inc(gap_ready, 1)
            dve.wait_ge(links, n[0])
            v.tensor_scalar(col[5][:], col[2][:], 0.0, None, ALU.mult).then_inc(visits, 1)
            dve.wait_ge(exp_done, 1)
            link(v.tensor_scalar(col[6][:], col[4][:], 1.0, None, ALU.add))
            link(v.reciprocal(weights[:, 0, :], col[6][:]))
            link(v.tensor_tensor(weights[:, 1, :], weights[:, 0, :], col[4][:], ALU.mult))
            dve.wait_ge(counted, 1)
            link(v.tensor_copy(big[0][:], ps_total[:].rearrange("p (t e) -> p t e", e=E)))
            src, dst = big[0], big[1]
            first = src
            step = 1
            bufs = [big[1], big[2]]
            while step < TT:
                dst = bufs[0]
                bufs.reverse()
                link(v.tensor_tensor(dst[:, step:, :], src[:, step:, :], src[:, :TT - step, :], ALU.add))
                link(v.tensor_copy(dst[:, :step, :], src[:, :step, :]))
                src = dst
                step *= 2
            link(v.tensor_tensor(big[3][:], src[:], first[:], ALU.subtract))
            link(v.tensor_tensor(big[3][:], big[3][:], ps_rank[:].rearrange("p (t e) -> p t e", e=E), ALU.add))
            link(v.tensor_scalar(cnt[0][:], src[:, TT - 1, :], float(P - 1), None, ALU.add))
            link(v.tensor_copy(cnt_i[0][:], cnt[0][:]))
            shift = P.bit_length() - 1
            link(v.tensor_scalar(cnt_i[1][:], cnt_i[0][:], shift, None, ALU.logical_shift_right))
            link(v.tensor_copy(cnt[1][:], cnt_i[1][:]))
            link(v.tensor_scalar(cnt[1][:], cnt[1][:], float(P), None, ALU.mult))
            a, others = cnt[1], [cnt[2], cnt[3]]
            step = 1
            while step < E:
                b = others[0]
                others.reverse()
                link(v.tensor_tensor(b[:, step:], a[:, step:], a[:, :E - step], ALU.add))
                link(v.tensor_copy(b[:, :step], a[:, :step]))
                a = b
                step *= 2
            end = a
            link(v.tensor_tensor(cnt[4][:], end[:], cnt[1][:], ALU.subtract))
            link(v.tensor_tensor(big[3][:], big[3][:], cnt[4][:].unsqueeze(1).broadcast_to((P, TT, E)), ALU.add))
            for k in range(2):
                link(v.tensor_tensor(big[5][:], big[3][:], one[:, k], ALU.mult))
                link(v.tensor_reduce(out=col[7][:], in_=big[5][:], axis=AX.X, op=ALU.add))
                link(v.tensor_copy(pos[:, k, :], col[7][:]))
            link(v.tensor_scalar(col_i[0][:], pos[:], P - 1, None, ALU.bitwise_and))
            link(v.tensor_scalar(col_i[1][:], pos[:], shift, None, ALU.logical_shift_right))
            rows = ends[:].rearrange("p n e -> p (n e)")[:, 0:4 * TT].rearrange("p (a k t) -> p a k t", a=2, k=2)
            link(v.tensor_copy(rows[:, 0], col_i[0][:]))
            link(v.tensor_copy(rows[:, 1], col_i[1][:]))
            link(v.scalar_tensor_tensor(out=rows[:, 0], in0=rows[:, 0], scalar=float(NT), in1=rows[:, 1],
                                        op0=ALU.mult, op1=ALU.add))
            v.tensor_copy(col_i[4][:], rows[:, 0]).then_inc(placed, 1)
            dve.wait_ge(placed, 1)
            link(v.tensor_tensor(ends[:], tile_start[:], end[:].unsqueeze(1).broadcast_to((P, NT, E)), ALU.is_ge))
            link(v.tensor_reduce(out=te[:], in_=ends[:], axis=AX.X, op=ALU.add))
            link(v.tensor_scalar(te[:], te[:], float(E - 1), None, ALU.min))
            link(v.tensor_copy(tile_expert[:], te[:]))


def experts(nc, x2, table, tile_expert, gu_sb, wd_sb, gu_in, y, ident):
    with ExitStack() as ctx:
        def sb(name, shape, dt=F32):
            return ctx.enter_context(nc.sbuf_tensor(name, shape, dt))

        def sem(name):
            return ctx.enter_context(nc.semaphore(name))

        def psum(name, shape):
            return ctx.enter_context(nc.psum_tensor(name, shape, F32))

        who_all = sb("who_all", [P, NT], I32)
        who = sb("who_e", [P, 4], I32)
        x_g = sb("x_g", [P, 4, D])
        xT = sb("xT_e", [P, 2, C, P])
        act_g = sb("act_e", [P, 2, H])
        hid = sb("hid_e", [P, 2, H])
        hT = sb("hT_e", [P, 2, CH, P])
        y_t = sb("y_t", [P, 4, D])
        ps_t = psum("pe_t", [P, 2, D])
        ps_h = psum("pe_h", [P, 2, D])
        ps_ht = psum("pe_ht", [P, 2, D])
        ps_y = psum("pe_y", [P, 2, D])

        passed = sem("passed_e")
        who_in = sem("who_in")
        who_copied = sem("who_copied")
        x_in = [sem(f"xg_in{i}") for i in range(4)]
        t_ready = sem("et_ready")
        t_done = sem("et_done")
        h_ready = sem("eh_ready")
        silu_done = sem("esilu_done")
        hid_done = sem("ehid_done")
        ht_ready = sem("eht_ready")
        ht_done = sem("eht_done")
        y_ready = sem("ey_ready")
        y_done = sem("ey_done")
        y_out = [sem(f"y_out{i}") for i in range(4)]

        block = ctx.enter_context(nc.Block())

        def static(t, n):
            return isinstance(t, int) and t < n

        def turns_of(t, s):
            return 4 * (t - s)

        @block.sync
        def _(sp):
            sp.dma_start(who_all[:], table.rearrange("(p n) a -> p (n a)", p=P)).then_inc(who_in, 16)
            with sp.Fori(0, NT // 4) as j:
                for s in range(4):
                    t = 4 * j + s
                    sp.wait_ge(y_done, t + 1)
                    sp.dma_start(y[bass.ds(t * P, P), :], y_t[:, s, :]).then_inc(y_out[s], 16)
            for s in range(4):
                sp.wait_ge(y_out[s], 16 * (NT // 4))

        @block.gpsimd
        def _(pool):
            pool.wait_ge(who_in, 16)

            def gather(t, s):
                if not static(t, 4):
                    pool.wait_ge(t_ready, t - 3)
                    pool.sem_inc(passed, 1)
                nc.gpsimd.tensor_copy(who[:, s:s + 1], who_all[:, bass.ds(t, 1)]).then_inc(who_copied, 1)
                pool.wait_ge(who_copied, t + 1)
                pool.sem_inc(passed, 1)
                nc.gpsimd.indirect_dma_start(
                    x_g[:, s, :], None, x2, bass.IndirectOffsetOnAxis(ap=who[:, s:s + 1].bitcast(U32), axis=0),
                ).then_inc(x_in[s], 16)

            for s in range(4):
                gather(s, s)
            with pool.Fori(1, NT // 4) as j:
                for s in range(4):
                    gather(4 * j + s, s)

        def pipeline(eng, step):
            step(0, 0, True, False)
            for s in range(1, 4):
                step(s, s, False, False)
            with eng.Fori(1, NT // 4 - 1) as j:
                for s in range(4):
                    step(4 * j + s, s, False, False)
            for s in range(4):
                step(NT - 4 + s, s, False, s == 3)

        @block.tensor
        def _(pe):
            def turn(t, s):
                pe.wait_ge(x_in[s], turns_of(t, s) + 16)
                if not static(t, 2):
                    pe.wait_ge(t_done, t - 1)
                for c in range(C):
                    done = nc.tensor.transpose(ps_t[:, s % 2, c * P:(c + 1) * P], x_g[:, s, c * P:(c + 1) * P], ident[:])
                done.then_inc(t_ready, 1)

            def up(t, s, e):
                pe.wait_ge(t_done, t + 1)
                if not static(t, 2):
                    pe.wait_ge(hid_done, t - 1)
                for c in range(C):
                    done = nc.tensor.matmul(ps_h[:, s % 2, :], xT[:, s % 2, c, :],
                                            gu_sb[:, bass.ds(e, 1), c, :].rearrange("p a n -> p (a n)"),
                                            start=c == 0, stop=c == C - 1)
                done.then_inc(h_ready, 1)

            def turn_hidden(t, s):
                pe.wait_ge(hid_done, t + 1)
                if not static(t, 2):
                    pe.wait_ge(ht_done, t - 1)
                for c in range(CH):
                    done = nc.tensor.transpose(ps_ht[:, s % 2, c * P:(c + 1) * P], hid[:, s % 2, c * P:(c + 1) * P], ident[:])
                done.then_inc(ht_ready, 1)

            def down(t, s, e):
                pe.wait_ge(ht_done, t + 1)
                if not static(t, 2):
                    pe.wait_ge(y_done, t - 1)
                for c in range(CH):
                    done = nc.tensor.matmul(ps_y[:, s % 2, :], hT[:, s % 2, c, :],
                                            wd_sb[:, bass.ds(e, 1), c, :].rearrange("p a n -> p (a n)"),
                                            start=c == 0, stop=c == CH - 1)
                done.then_inc(y_ready, 1)

            def expert_of(t):
                return pe.value_load(tile_expert[0:1, bass.ds(t, 1)], min_val=0, max_val=E - 1)

            def step(t, s, first, last):
                if first:
                    turn(t, s)
                up(t, s, expert_of(t))
                if not last:
                    turn(t + 1, (s + 1) % 4)
                if not first:
                    down(t - 1, (s - 1) % 4, expert_of(t - 1))
                turn_hidden(t, s)
                if last:
                    down(t, s, expert_of(t))

            pe.wait_ge(gu_in, 16 * 2 * E)
            pipeline(pe, step)

        @block.scalar
        def _(act):
            def x_copy(t, s):
                act.wait_ge(t_ready, t + 1)
                if not static(t, 2):
                    act.wait_ge(h_ready, t - 1)
                nc.scalar.activation(xT[:, s % 2], ps_t[:, s % 2, :].rearrange("p (c t) -> p c t", c=C),
                                     ACT.Copy).then_inc(t_done, 1)

            def gate(t, s):
                act.wait_ge(h_ready, t + 1)
                if not static(t, 2):
                    act.wait_ge(hid_done, t - 1)
                nc.scalar.activation(act_g[:, s % 2, :], ps_h[:, s % 2, 0:H], ACT.Silu).then_inc(silu_done, 1)

            def step(t, s, first, last):
                if first:
                    x_copy(t, s)
                gate(t, s)
                if not last:
                    x_copy(t + 1, (s + 1) % 4)

            pipeline(act, step)

        @block.vector
        def _(dve):
            def hidden(t, s):
                dve.wait_ge(silu_done, t + 1)
                if not static(t, 2):
                    dve.wait_ge(ht_ready, t - 1)
                nc.vector.tensor_tensor(hid[:, s % 2, :], act_g[:, s % 2, :], ps_h[:, s % 2, H:2 * H],
                                        ALU.mult).then_inc(hid_done, 1)

            def h_copy(t, s):
                dve.wait_ge(ht_ready, t + 1)
                if not static(t, 2):
                    dve.wait_ge(y_ready, t - 1)
                nc.vector.tensor_copy(hT[:, s % 2], ps_ht[:, s % 2, 0:H].rearrange("p (c t) -> p c t", c=CH)).then_inc(ht_done, 1)

            def y_copy(t, s):
                dve.wait_ge(y_ready, t + 1)
                if not static(t, 4):
                    dve.wait_ge(y_out[s], turns_of(t, s))
                nc.vector.tensor_copy(y_t[:, s, :], ps_y[:, s % 2, :]).then_inc(y_done, 1)

            def step(t, s, first, last):
                hidden(t, s)
                if not first:
                    y_copy(t - 1, (s - 1) % 4)
                h_copy(t, s)
                if last:
                    y_copy(t, s)

            pipeline(dve, step)


def combine(nc, base, y, pos, weights, out):
    with ExitStack() as ctx:
        def sb(name, shape, dt=F32):
            return ctx.enter_context(nc.sbuf_tensor(name, shape, dt))

        def sem(name):
            return ctx.enter_context(nc.semaphore(name))

        index = sb("c_index", [P, 8], I32)
        y_g = sb("y_g", [P, 4, 2, D])
        b_t = sb("b_t", [P, 4, D])
        w_t = sb("w_t", [P, 4, 2])
        acc = sb("acc", [P, 4, D])
        res = sb("res_c", [P, 4, D])
        stats = sb("stats_c", [P, 4, 6])
        mv = sb("mv_c", [P, 4, 2])
        var_eps = sb("var_eps_c", [P, 4, 1])
        minus_half = sb("minus_half_c", [P, 1])
        rstd = sb("rstd_c", [P, 4, 1])

        passed = sem("passed_c")
        copied = sem("c_copied")
        y_in = [sem(f"y_in{i}") for i in range(4)]
        b_in = [sem(f"b_in{i}") for i in range(4)]
        w_copied = sem("w_copied")
        first_added = sem("first_added")
        added = sem("added")
        stats_made = sem("stats_made")
        aggr_made = sem("c_aggr_made")
        var_made = sem("c_var_made")
        rstd_made = sem("c_rstd_made")
        normal = sem("normal")
        out_done = [sem(f"out_done{i}") for i in range(4)]
        half_set = sem("half_set")

        block = ctx.enter_context(nc.Block())
        GROUPS = TT // 4

        @block.sync
        def _(sp):
            def load(t, s):
                sp.dma_start(b_t[:, s, :], base[bass.ds(t * P, P), :]).then_inc(b_in[s], 16)

            def store(t, s):
                sp.wait_ge(normal, t + 1)
                sp.dma_start(out[bass.ds(t * P, P), :], res[:, s, :]).then_inc(out_done[s], 16)

            for s in range(4):
                load(s, s)
            with sp.Fori(0, GROUPS - 1) as j:
                for s in range(4):
                    store(4 * j + s, s)
                    load(4 * j + s + 4, s)
            for s in range(4):
                store(TT - 4 + s, s)
            for s in range(4):
                sp.wait_ge(out_done[s], 16 * GROUPS)

        @block.gpsimd
        def _(pool):
            nc.gpsimd.memset(minus_half[:], -0.5).then_inc(half_set, 1)
            pool.wait_ge(half_set, 1)

            def gather(t, s):
                for k in range(2):
                    nc.gpsimd.tensor_copy(index[:, 2 * s + k:2 * s + k + 1], pos[:, k, bass.ds(t, 1)]).then_inc(copied, 1)
                    pool.wait_ge(copied, 2 * t + k + 1)
                    pool.sem_inc(passed, 1)
                    nc.gpsimd.indirect_dma_start(
                        y_g[:, s, k, :], None, y,
                        bass.IndirectOffsetOnAxis(ap=index[:, 2 * s + k:2 * s + k + 1].bitcast(U32), axis=0),
                    ).then_inc(y_in[s], 16)

            def root(t, s):
                pool.wait_ge(var_made, t + 1)
                nc.gpsimd.tensor_tensor(rstd[:, s, :], var_eps[:, s, :], minus_half[:], ALU.pow).then_inc(rstd_made, 1)

            for s in range(4):
                gather(s, s)
            with pool.Fori(0, GROUPS - 1) as j:
                for s in range(4):
                    root(4 * j + s, s)
                    gather(4 * j + s + 4, s)
            for s in range(4):
                root(TT - 4 + s, s)

        @block.vector
        def _(dve):
            def one_tile(t, s, turn):
                dve.wait_ge(y_in[s], 32 * turn + 32)
                dve.wait_ge(b_in[s], 16 * turn + 16)
                nc.vector.tensor_copy(w_t[:, s, :], weights[:, :, bass.ds(t, 1)].rearrange("p k a -> p (k a)")).then_inc(w_copied, 1)
                dve.wait_ge(w_copied, t + 1)
                nc.vector.scalar_tensor_tensor(out=acc[:, s, :], in0=y_g[:, s, 0, :], scalar=w_t[:, s, 0:1],
                                               in1=b_t[:, s, :], op0=ALU.mult, op1=ALU.add).then_inc(first_added, 1)
                dve.wait_ge(first_added, t + 1)
                if not isinstance(turn, int):
                    dve.wait_ge(out_done[s], 16 * turn)
                nc.vector.scalar_tensor_tensor(out=res[:, s, :], in0=y_g[:, s, 1, :], scalar=w_t[:, s, 1:2],
                                               in1=acc[:, s, :], op0=ALU.mult, op1=ALU.add).then_inc(added, 1)
                dve.wait_ge(added, t + 1)
                nc.vector.bn_stats(stats[:, s, :], res[:, s, :]).then_inc(stats_made, 1)
                dve.wait_ge(y_in[s], 32)
                dve.wait_ge(stats_made, t + 1)
                nc.vector.bn_aggr(mv[:, s, :], stats[:, s, :]).then_inc(aggr_made, 1)
                dve.wait_ge(aggr_made, t + 1)
                nc.vector.tensor_scalar(var_eps[:, s, :], mv[:, s, 1:2], EPS, None, ALU.add).then_inc(var_made, 1)

            def norm(t, s):
                dve.wait_ge(rstd_made, t + 1)
                nc.vector.tensor_scalar(res[:, s, :], res[:, s, :], mv[:, s, 0:1], rstd[:, s, :],
                                        ALU.subtract, ALU.mult).then_inc(normal, 1)

            one_tile(0, 0, 0)
            for s in range(1, 4):
                one_tile(s, s, 0)
                norm(s - 1, s - 1)
            with dve.Fori(1, GROUPS) as j:
                for s in range(4):
                    one_tile(4 * j + s, s, j)
                    norm(4 * j + s - 1, (s - 1) % 4)
            norm(TT - 1, 3)


def moe(nc, x2, shg, shu, shd, rw, wgu, wd, out):
    base = nc.dram_tensor("base", (TOKENS, D), F32, kind="Internal").ap()
    y = nc.dram_tensor("y_slots", (SLOTS_ALL, D), F32, kind="Internal").ap()
    table = nc.dram_tensor("table", (SLOTS_ALL, 1), I32, kind="Internal").ap()
    with ExitStack() as ctx:
        ident = ctx.enter_context(nc.sbuf_tensor("ident_m", [P, P], F32))
        route = ctx.enter_context(nc.sbuf_tensor("route", [P, TT, E], F32))
        weights = ctx.enter_context(nc.sbuf_tensor("weights", [P, 2, TT], F32))
        pos = ctx.enter_context(nc.sbuf_tensor("pos", [P, 2, TT], I32))
        tile_expert = ctx.enter_context(nc.sbuf_tensor("tile_expert", [P, NT], I32))
        gu_in = ctx.enter_context(nc.semaphore("gu_in"))
        ident_set = ctx.enter_context(nc.semaphore("ident_set"))
        with nc.Block() as block:
            @block.gpsimd
            def _(pool):
                nc.gpsimd.memset(ident[:], 0.0).then_inc(ident_set, 1)
                pool.wait_ge(ident_set, 1)
                nc.gpsimd.affine_select(out=ident[:], in_=ident[:], compare_op=ALU.not_equal, fill=1.0, base=0,
                                        pattern=[[-1, P]], channel_multiplier=1).then_inc(ident_set, 1)
                pool.wait_ge(ident_set, 2)
        with ExitStack() as big:
            gu_sb = big.enter_context(nc.sbuf_tensor("gu_sb", [P, E, C, 2 * H], F32))
            wd_sb = big.enter_context(nc.sbuf_tensor("wd_sb", [P, E, CH, D], F32))
            shared_and_scores(nc, x2, shg, shu, shd, rw, wgu, wd, base, gu_sb, wd_sb, gu_in, route, ident)
            place(nc, route, weights, pos, tile_expert, table, ident)
            experts(nc, x2, table, tile_expert, gu_sb, wd_sb, gu_in, y, ident)
        combine(nc, base, y, pos, weights, out)


def build(nc, x, xT, wkqT, wvT, woT, bq, bk, bv, bo, shg, shu, shd, rw, wgu, wd, out):
    x2 = nc.dram_tensor("x2", (TOKENS, D), F32, kind="Internal").ap()
    attention(nc, x, xT, wkqT, wvT, woT, bq, bk, bv, bo, x2.rearrange("(b s) d -> b s d", b=B))
    moe(nc, x2, shg, shu, shd, rw, wgu, wd, out)


def kernel(L0_attn_x, L0_attn_wq, L0_attn_bq, L0_attn_wk, L0_attn_bk, L0_attn_wv, L0_attn_bv, L0_attn_wo,
           L0_attn_bo, L0_ffn_gate_w, L0_ffn_w_gate, L0_ffn_w_up, L0_ffn_w_down, L0_ffn_sh_gate, L0_ffn_sh_up,
           L0_ffn_sh_down, L0_ffn_se_gate_w):
    import numpy as np
    import concourse.bacc as bacc
    from concourse.bass_utils import run_bass_kernel_spmd

    def array(a):
        return np.ascontiguousarray(np.asarray(a))

    def turned(w):
        w = np.asarray(w)
        return array(w.T.reshape(-1, P, w.shape[0]).transpose(1, 0, 2))

    x = array(L0_attn_x)
    kq = np.stack([turned(L0_attn_wk), turned(L0_attn_wq)])
    arrays = {
        "x": x,
        "xT": array(x.transpose(0, 2, 1).reshape(B, C, P, S).transpose(0, 2, 1, 3)),
        "wkqT": array(kq.reshape(2, P, C, G, P).transpose(3, 1, 0, 2, 4)),
        "wvT": turned(L0_attn_wv),
        "woT": turned(L0_attn_wo),
        "bq": array(np.asarray(L0_attn_bq).reshape(G, P).T),
        "bk": array(np.asarray(L0_attn_bk).reshape(G, P).T),
        "bv": array(L0_attn_bv),
        "bo": array(L0_attn_bo),
        "shg": turned(L0_ffn_sh_gate),
        "shu": turned(L0_ffn_sh_up),
        "shd": turned(L0_ffn_sh_down),
        "rw": turned(np.concatenate([np.asarray(L0_ffn_gate_w), np.asarray(L0_ffn_se_gate_w)])),
        "wgu": array(np.stack([turned(np.concatenate([g, u])) for g, u in
                               zip(np.asarray(L0_ffn_w_gate), np.asarray(L0_ffn_w_up))])),
        "wd": array(np.stack([turned(w) for w in np.asarray(L0_ffn_w_down)])),
    }
    nc = bacc.Bacc("TRN2", target_bir_lowering=False, num_devices=1)
    drams = {n: nc.dram_tensor(n, a.shape, F32, kind="ExternalInput").ap() for n, a in arrays.items()}
    out = nc.dram_tensor("out", (TOKENS, D), F32, kind="ExternalOutput").ap()
    build(nc, **drams, out=out)
    r = run_bass_kernel_spmd(nc, [arrays], core_ids=[0])
    return r.results[0]["out"].reshape(B, S, D)
```

```python
from contextlib import ExitStack

import concourse.bass as bass
from concourse import mybir

ALU = mybir.AluOpType
ACT = mybir.ActivationFunctionType
AX = mybir.AxisListType
F32 = mybir.dt.float32
F32R = mybir.dt.float32r
BF16 = mybir.dt.bfloat16
I32 = mybir.dt.int32
U32 = mybir.dt.uint32

P = 128
B, S, D = 4, 1024, 512
HEADS = 16
HD = D // HEADS
C = D // P
HG = P // HD
G = HEADS // HG
HALF = 512
NHALF = S // HALF
KT = S // P
EPS = 1e-5

STEPS = NHALF * KT
PROJ = 4
PRE = HG * KT * NHALF

SLOTS = 4
SLOT_WORK = (1, 1, 1, 1)
PRE_SLOTS = (3, 54)
PROJ_SLOTS = (44, 46, 48, 50)
INVERT_SLOTS = ((1, 1, 2, 2, 3), (25, 26, 27, 28, 29))
ROW_SLOT = 55


def side_plan(with_proj):
    plan = [[] for _ in range(STEPS * SLOTS)]
    room = [slot for slot in range(*PRE_SLOTS) for _ in range(SLOT_WORK[slot % SLOTS])]
    for u in range(PRE):
        plan[room[u * len(room) // PRE]].append(("pre", u))
    if with_proj:
        for u, slot in enumerate(PROJ_SLOTS):
            plan[slot].append(("proj", u))
    plan[ROW_SLOT].append(("row", 0))
    place, count = {}, 0
    for slot in plan:
        for i, unit in enumerate(slot):
            place[unit] = count
            slot[i] = (*unit, count)
            count += 1
    return plan, place, count


PLAN, PLACE, SIDE = side_plan(True)
PLAN_LAST, PLACE_LAST, _ = side_plan(False)


def attention(nc, x, xT, wkqT, wvT, woT, bq, bk, bv, bo, x2):
    with ExitStack() as ctx:
        def sb(name, shape, dt=F32):
            return ctx.enter_context(nc.sbuf_tensor(name, shape, dt))

        def sem(name):
            return ctx.enter_context(nc.semaphore(name))

        ident = sb("ident", [P, P])
        ones = sb("ones", [P, HD])
        bkq = sb("bkq", [P, 2, G])
        bv_bc = sb("bv_bc", [P, D])
        bo_bc = sb("bo_bc", [P, D])
        wstage = sb("wstage", [P, C, P])
        wkq_hi = sb("wkq_hi", [P, 2, C, P], F32R)
        wkq_lo = sb("wkq_lo", [P, 2, C, P], F32R)
        wv_hi = sb("wv_hi", [P, C, D], F32R)
        wv_lo = sb("wv_lo", [P, C, D], F32R)
        wo = sb("wo", [P, C, D])
        xstage = sb("xstage", [P, 2, HALF])
        x_hi = sb("x_hi", [P, C, S], F32R)
        x_lo = sb("x_lo", [P, C, S], F32R)
        kq_hi = sb("kq_hi", [P, 2, S], F32R)
        kq_lo = sb("kq_lo", [P, 2, S], F32R)
        k_stack = [sb(f"k_stack{i}", [P, HG, S], F32R) for i in range(2)]
        q_stack = [sb(f"q_stack{i}", [P, HG, S], F32R) for i in range(2)]
        v_sb = sb("v_sb", [P, KT, D])
        probs = sb("probs", [P, 4, 2, HALF])
        ctx_sb = sb("ctx_sb", [P, G, S])
        first_wv = ctx_sb[:, 0:2, :].rearrange("p g (a d) -> p (g a) d", d=D)

        def first_w(n):
            return ctx_sb[:, 2 + n, :].rearrange("p (s c o) -> p s c o", s=2, c=C)

        max_half = sb("max_half", [P, HG * KT, NHALF])
        max_q = sb("max_q", [P, HG * KT])
        max_row = sb("max_row", [HG * KT, P], F32R)
        x_nat = probs[:].rearrange("p a c d -> p (a c) d")
        assert 8 * HALF == KT * D
        res = sb("res", [P, 2, D])
        rsum = res[:, 0, :]
        stats = sb("stats", [P, 2, 6])
        mv = sb("mv", [P, 2, 2])
        var_eps = sb("var_eps", [P, 2, 1])
        minus_half = sb("minus_half", [P, 1])
        rstd = sb("rstd", [P, 2, 1])

        ps_s = ctx.enter_context(nc.psum_tensor("ps_s", [P, 4, HALF], F32))
        ps_ctx = ctx.enter_context(nc.psum_tensor("ps_ctx", [P, HALF], F32))
        ps_sum = ctx.enter_context(nc.psum_tensor("ps_sum", [P, HALF], F32))
        ps_side = ctx.enter_context(nc.psum_tensor("ps_side", [P, 2, HALF], F32))

        const_in = sem("const_in")
        bias_in = sem("bias_in")
        passed = sem("passed")
        passed_sp = sem("passed_sp")
        const_set = sem("const_set")
        wv_split = sem("wv_split")
        w_in = sem("w_in")
        w_split = sem("w_split")
        x_in = [sem("x_in0"), sem("x_in1")]
        x_split = sem("x_split")
        wv_in = sem("wv_in")
        x_first = [sem(f"x_first{i}") for i in range(4)]
        w_high, x_high, wv_high = sem("w_high"), sem("x_high"), sem("wv_high")
        side_ready = sem("side_ready")
        side_hi = sem("side_hi")
        side_free = sem("side_free")
        stacked = [sem(f"stacked{h}") for h in range(HG)]
        max_made = sem("max_made")
        row_in = sem("row_in")
        scores_ready = sem("scores_ready")
        probs_ready = sem("probs_ready")
        pv_done = sem("pv_done")
        ctx_made = sem("ctx_made")
        ctx_taken = sem("ctx_taken")
        sum_taken = sem("sum_taken")
        recip_done = sem("recip_done")
        ctx_done = sem("ctx_done")
        tail_ready = sem("tail_ready")
        tail_free = sem("tail_free")
        xnat_in = [sem(f"xnat_in{i}") for i in range(KT // 2)]
        xbias = sem("xbias")
        ln_chain = sem("ln_chain")
        aggr_made = sem("aggr_made")
        var_made = sem("var_made")
        rstd_made = sem("rstd_made")
        x2_ready = sem("x2_ready")
        x2_out = [sem("x2_out0"), sem("x2_out1")]

        block = ctx.enter_context(nc.Block())

        BSTEPS = G * STEPS
        SPREAD = 16 * 6
        CONSTS = 16 * 3
        TAIL = 2 * KT
        CHUNKS = C * NHALF
        QUARTER = HALF // 4

        def base_of(m):
            return PROJ + (m + 1) * SIDE

        def side_in(last, loc, slot):
            g, i = loc // STEPS, loc % STEPS * SLOTS + slot
            if last and g == G - 1:
                return []
            return (PLAN_LAST if last and g == G - 2 else PLAN)[i]

        def prologue():
            chunks = [(t, c, None) for t in range(KT) for c in range(C)]
            units = [(0, 0, what) for slot in PLAN for what in slot]
            first = len(chunks) // 4
            yield from chunks[:first]
            done = first
            for i, unit in enumerate(units):
                yield unit
                while done < len(chunks) and (done - first) * PRE <= i * (len(chunks) - first):
                    yield chunks[done]
                    done += 1

        @block.sync
        def _(sp):
            def load_w(n, g):
                for sel in range(2):
                    sp.wait_ge(w_split, 2 * n + sel)
                    sp.dma_start(wstage[:], wkqT[g, :, sel]).then_inc(w_in, 16)

            def load_x(b):
                for i in range(CHUNKS):
                    c, half = i % C, i // C
                    if i >= 2:
                        sp.wait_ge(x_split, b * CHUNKS + i - 1)
                    sp.dma_start(xstage[:, i % 2, :],
                                 xT[bass.ds(b, 1), :, c, half * HALF:(half + 1) * HALF].rearrange(
                                     "a p t -> (a p) t")).then_inc(x_in[i % 2], 16)

            def spread(staged, par):
                sp.wait_ge(side_free, staged)
                for h in range(HG):
                    for sel, dst, parts in ((0, k_stack[par], (kq_hi, kq_lo, kq_hi)),
                                            (1, q_stack[par], (kq_hi, kq_hi, kq_lo))):
                        for r, part in enumerate(parts):
                            sp.dma_start(dst[r * HD:(r + 1) * HD, h, :].bitcast(F32),
                                         part[h * HD:(h + 1) * HD, sel, :].bitcast(F32)).then_inc(stacked[h], 16)

            def send_rows(par):
                sp.dma_start(q_stack[par][3 * HD:3 * HD + 1, :, :].rearrange("a h (j q) -> a (h j) q", q=P).bitcast(F32),
                             max_row[:].bitcast(F32)).then_inc(row_in, 16)

            def body(m, g, last):
                if not (last and g > 0):
                    load_w(m + 3, (g + 3) % G)
                if not (last and g == G - 1):
                    sp.wait_ge(side_free, base_of(m) + (PLACE_LAST if last and g == G - 2 else PLACE)[("row", 0)] + 1)
                    send_rows((g + 1) % 2)
                if not (last and g >= G - 2):
                    sp.wait_ge(scores_ready, 2 * STEPS * (m + 1))
                    sp.sem_inc(passed_sp, 1)
                    spread(base_of(m) + PLACE[("proj", PROJ - 1)] + 1, g % 2)

            def tail(b):
                sp.wait_ge(pv_done, (b + 1) * BSTEPS)
                sp.sem_inc(passed_sp, 1)
                for i in range(KT // 2):
                    sp.dma_start(x_nat[:, 2 * i:2 * i + 2, :],
                                 x[bass.ds(b, 1), 2 * i * P:(2 * i + 2) * P, :].rearrange(
                                     "a (t p) d -> p (a t) d", p=P)).then_inc(xnat_in[i], 16)
                for t in range(KT):
                    store(b, t)

            def store(b, t):
                sp.wait_ge(x2_ready, b * KT + t + 1)
                sp.dma_start(x2[bass.ds(b, 1), t * P:(t + 1) * P, :].rearrange("a p d -> (a p) d"),
                             res[:, t % 2, :]).then_inc(x2_out[t % 2], 16)

            for i in range(2):
                sp.sem_inc(x2_out[i], 16)
            sp.dma_start(first_w(0), wkqT[0]).then_inc(x_first[0], 16)
            for i in range(4):
                c, half = i % 2 * 2, i // 2
                sp.dma_start(x_nat[:, 2 * i:2 * i + 2, :],
                             xT[0, :, c:c + 2, half * HALF:(half + 1) * HALF]).then_inc(x_first[i], 16)
                if i == 1:
                    for sel, src in ((0, bk), (1, bq)):
                        sp.dma_start(bkq[:, sel, :], src).then_inc(bias_in, 16)
            sp.dma_start(first_wv, wvT).then_inc(wv_in, 16)
            sp.dma_start(first_w(1), wkqT[1]).then_inc(wv_in, 16)
            for t, src in ((bv_bc[:], bv.partition_broadcast(P)), (bo_bc[:], bo.partition_broadcast(P)), (wo[:], woT)):
                sp.dma_start(t, src).then_inc(const_in, 16)
            spread(PROJ, 0)
            load_w(2, 2)
            sp.wait_ge(side_free, base_of(-1) + PLACE[("row", 0)] + 1)
            send_rows(0)
            spread(base_of(-1) + PLACE[("proj", PROJ - 1)] + 1, 1)
            with sp.Fori(0, B - 1) as b:
                for g in range(G):
                    body(b * G + g, g, False)
                    if g == 1:
                        load_x(b + 1)
                tail(b)
            b = B - 1
            for g in range(G):
                body(b * G + g, g, True)
            tail(b)
            for i in range(2):
                sp.wait_ge(x2_out[i], 16 * (B * KT // 2 + 1))

        @block.gpsimd
        def _(pool):
            nc.gpsimd.memset(ident[:], 0.0).then_inc(const_set, 1)
            pool.wait_ge(const_set, 1)
            nc.gpsimd.affine_select(out=ident[:], in_=ident[:], compare_op=ALU.not_equal, fill=1.0, base=0,
                                    pattern=[[-1, P]], channel_multiplier=1).then_inc(const_set, 1)
            pool.wait_ge(const_set, 2)
            nc.gpsimd.memset(ones[:], 1.0).then_inc(const_set, 1)
            for i in range(2):
                pool.wait_ge(const_set, 3 + i)
                nc.gpsimd.memset(k_stack[i][3 * HD:3 * HD + 1, :, :].bitcast(F32), 1.0).then_inc(const_set, 1)
            pool.wait_ge(const_set, 5)
            nc.gpsimd.memset(minus_half[:], -0.5).then_inc(const_set, 1)
            pool.wait_ge(const_set, 6)

            def split(hi, lo, raw, high_made, count, done):
                nc.gpsimd.tensor_copy(hi, raw).then_inc(high_made, 1)
                pool.wait_ge(high_made, count)
                nc.gpsimd.tensor_tensor(lo, raw, hi.bitcast(F32), ALU.subtract).then_inc(done, 1)

            def split_w(n):
                for sel in range(2):
                    pool.wait_ge(w_in, 16 * (2 * (n - 2) + sel + 1))
                    pool.sem_inc(passed, 1)
                    split(wkq_hi[:, sel], wkq_lo[:, sel], wstage[:], w_high, 2 * n + sel + 1, w_split)

            def split_x(b):
                for i in range(CHUNKS):
                    c, half = i % C, i // C
                    pool.wait_ge(x_in[i % 2], 16 * ((b - 1) * (CHUNKS // 2) + i // 2 + 1))
                    pool.sem_inc(passed, 1)
                    at = (slice(None), c, slice(half * HALF, (half + 1) * HALF))
                    split(x_hi[at], x_lo[at], xstage[:, i % 2, :], x_high, b * CHUNKS + i + 1, x_split)

            def projected(m):
                pool.wait_ge(side_ready, base_of(m) + PLACE[("proj", PROJ - 1)] + 1)

            def add_bo(b):
                for t in range(KT + 1):
                    if t < KT:
                        pool.wait_ge(xnat_in[t // 2], 16 * (b + 1))
                        nc.gpsimd.tensor_tensor(x_nat[:, t, :], x_nat[:, t, :], bo_bc[:],
                                                ALU.add).then_inc(xbias, 1)
                    if t >= 1:
                        s = (t - 1) % 2
                        pool.wait_ge(var_made, b * KT + t)
                        nc.gpsimd.tensor_tensor(rstd[:, s, :], var_eps[:, s, :], minus_half[:],
                                                ALU.pow).then_inc(rstd_made, 1)

            pool.wait_ge(wv_in, 32)
            pool.wait_ge(side_ready, PROJ)
            nc.gpsimd.tensor_copy(wkq_hi[:], first_w(1)).then_inc(w_high, 2)
            pool.wait_ge(w_high, 4)
            nc.gpsimd.tensor_tensor(wkq_lo[:], first_w(1), wkq_hi[:].bitcast(F32), ALU.subtract).then_inc(w_split, 2)
            projected(-1)
            split_w(2)
            pool.wait_ge(const_in, CONSTS)
            with pool.Fori(0, B - 1) as b:
                for g in range(G):
                    projected(b * G + g)
                    split_w(b * G + g + 3)
                    if g == 1:
                        split_x(b + 1)
                add_bo(b)
            b = B - 1
            projected(b * G)
            split_w(b * G + 3)
            add_bo(b)

        @block.tensor
        def _(pe):
            def three(out, terms, first, last):
                for i, (w, m) in enumerate(terms):
                    done = nc.tensor.matmul(out, w, m, start=first and i == 0, stop=last and i == 2)
                return done

            def project(n, u, at, bank, first):
                if u == 0:
                    pe.wait_ge(w_split, 2 * n + 2)
                if not (isinstance(at, int) and at < 2):
                    pe.wait_ge(side_free, at - 1)
                sel, half = u // 2, u % 2
                for c in range(C):
                    if first:
                        pe.wait_ge(x_split, half * C + c + 1)
                    wh, wl = wkq_hi[:, sel, c, :], wkq_lo[:, sel, c, :]
                    xh = x_hi[:, c, half * HALF:(half + 1) * HALF]
                    xl = x_lo[:, c, half * HALF:(half + 1) * HALF]
                    done = three(bank, ((wh, xh), (wl, xh), (wh, xl)), c == 0, c == C - 1)
                done.then_inc(side_ready, 1)

            def side_unit(m, g, kind, u, place):
                at = base_of(m) + place
                bank = ps_side[:, (base_of(g) + place) % 2, :]
                par = (g + 1) % 2
                if kind == "proj":
                    project(m + 2, u, at, bank, False)
                elif kind == "pre":
                    h, j, half = u // (KT * NHALF), u // NHALF % KT, u % NHALF
                    if j == 0 and half == 0:
                        pe.wait_ge(stacked[h], SPREAD * (m + 2))
                    pe.wait_ge(side_free, at - 1)
                    nc.tensor.matmul(bank, q_stack[par][0:3 * HD, h, j * P:(j + 1) * P],
                                     k_stack[par][0:3 * HD, h, half * HALF:(half + 1) * HALF],
                                     start=True, stop=True).then_inc(side_ready, 1)
                else:
                    pe.wait_ge(side_free, at - 1)
                    pe.wait_ge(max_made, m + 2)
                    nc.tensor.transpose(bank[0:HG * KT, 0:P], max_q[:], ident[:]).then_inc(side_ready, 1)

            def scores(b, loc, pair):
                g, half, kt = loc // STEPS, loc // KT % NHALF, loc % KT
                par = g % 2
                if loc % STEPS == 0 and pair == 0:
                    pe.wait_ge(row_in, 16 * (b * G + g + 1))
                if loc:
                    pe.wait_ge(probs_ready, b * 2 * BSTEPS + 2 * loc + pair - 1)
                for h in (2 * pair, 2 * pair + 1):
                    done = nc.tensor.matmul(ps_s[:, h, :], k_stack[par][0:3 * HD + 1, h, kt * P:(kt + 1) * P],
                                            q_stack[par][0:3 * HD + 1, h, half * HALF:(half + 1) * HALF],
                                            start=True, stop=True)
                done.then_inc(scores_ready, 1)

            def weighted(b, loc, is_sum):
                g, half, kt = loc // STEPS, loc // KT % NHALF, loc % KT
                out = ps_sum if is_sum else ps_ctx
                pe.wait_ge(probs_ready, b * 2 * BSTEPS + 2 * loc + 2)
                if kt == 0 and loc:
                    pe.wait_ge(sum_taken if is_sum else ctx_taken, b * G * NHALF + loc // KT)
                for h in range(HG):
                    lhsT = ones[:] if is_sum else v_sb[:, kt, (g * HG + h) * HD:(g * HG + h + 1) * HD]
                    done = nc.tensor.matmul(out[h * HD:(h + 1) * HD, :], lhsT,
                                            probs[:, (2 * loc + h // 2) % 4, h % 2, :],
                                            start=kt == 0, stop=kt == KT - 1)
                if is_sum:
                    done.then_inc(pv_done, 1)
                elif kt == KT - 1:
                    done.then_inc(ctx_made, 1)

            def v_tile(u, t, chunks=range(C)):
                if (t >= 4 or not isinstance(u, int)) and 0 in chunks:
                    pe.wait_ge(tail_free, u - 3)
                for c in chunks:
                    xh, xl = x_hi[:, c, t * P:(t + 1) * P], x_lo[:, c, t * P:(t + 1) * P]
                    wh, wl = wv_hi[:, c, :], wv_lo[:, c, :]
                    done = three(ps_s[:, t % 4, :], ((xh, wh), (xl, wh), (xh, wl)), c == 0, c == C - 1)
                if C - 1 in chunks:
                    done.then_inc(tail_ready, 1)

            def o_tile(u, t):
                pe.wait_ge(tail_free, u - 3)
                for g in range(G):
                    done = nc.tensor.matmul(ps_s[:, t % 4, :], ctx_sb[:, g, t * P:(t + 1) * P], wo[:, g, :],
                                            start=g == 0, stop=g == G - 1)
                done.then_inc(tail_ready, 1)

            def batch(b, last):
                for pair in range(2):
                    scores(b, 0, pair)
                for loc in range(BSTEPS):
                    g = loc // STEPS
                    for slot in range(SLOTS):
                        if slot >= 2:
                            weighted(b, loc, slot == 3)
                        elif loc + 1 < BSTEPS:
                            scores(b, loc + 1, slot)
                        for kind, u, place in side_in(last, loc, slot):
                            if kind == "proj" and u == 0 and g == 2:
                                pe.wait_ge(x_split, (b + 2) * CHUNKS)
                            side_unit(b * G + g, g, kind, u, place)

            for u in range(PROJ):
                project(0, u, u, ps_side[:, u % 2, :], True)
            pe.wait_ge(wv_split, C)
            pe.wait_ge(const_set, 5)
            for t, c, what in prologue():
                if what is None:
                    v_tile(t, t, [c])
                else:
                    side_unit(-1, -1, *what)
            pe.wait_ge(const_in, CONSTS)
            with pe.Fori(0, B - 1) as b:
                pe.wait_ge(tail_free, b * TAIL + KT)
                batch(b, False)
                for t in range(KT):
                    v_tile(b * TAIL + KT + t, t)
                pe.wait_ge(ctx_done, (b + 1) * G * NHALF)
                for t in range(KT):
                    o_tile(b * TAIL + 2 * KT + t, t)
            b = B - 1
            pe.wait_ge(tail_free, b * TAIL + KT)
            batch(b, True)
            pe.wait_ge(ctx_done, (b + 1) * G * NHALF)
            for t in range(KT):
                o_tile(b * TAIL + KT + t, t)

        @block.scalar
        def _(act):
            def project(n, u, at, bank, g):
                sel, half = u // 2, u % 2
                act.wait_ge(side_ready, at + 1)
                if not (isinstance(n, int) and n == 0):
                    for s in stacked:
                        act.wait_ge(s, SPREAD * n)
                nc.scalar.activation(kq_hi[:, sel, half * HALF:(half + 1) * HALF], bank, ACT.Identity,
                                     bias=bkq[:, sel, g:g + 1]).then_inc(side_hi, 1)

            def side_unit(m, g, kind, u, place):
                if kind == "proj":
                    project(m + 2, u, base_of(m) + place, ps_side[:, (base_of(g) + place) % 2, :], (g + 2) % G)

            def exps(b, loc, pair):
                act.wait_ge(scores_ready, b * 2 * BSTEPS + 2 * loc + pair + 1)
                if loc >= 2:
                    act.wait_ge(pv_done, b * BSTEPS + loc - 1)
                nc.scalar.activation(probs[:, (2 * loc + pair) % 4, :, :], ps_s[:, 2 * pair:2 * pair + 2, :],
                                     ACT.Exp, scale=HD ** -0.5).then_inc(probs_ready, 1)

            def take(b, loc):
                k = b * G * NHALF + loc // KT
                g, half = loc // STEPS, loc // KT % NHALF
                act.wait_ge(ctx_made, k + 1)
                nc.scalar.activation(ctx_sb[:, g, half * HALF:(half + 1) * HALF], ps_ctx[:],
                                     ACT.Identity).then_inc(ctx_taken, 1)
                act.wait_ge(pv_done, b * BSTEPS + loc + 1)
                if loc >= KT:
                    act.wait_ge(ctx_done, k)
                else:
                    act.wait_ge(x2_out[0], 16 * (b * (KT // 2) + 1))
                nc.scalar.activation(rsum, ps_sum[:], ACT.Identity).then_inc(sum_taken, 1)

            def batch(b, last):
                for pair in range(2):
                    exps(b, 0, pair)
                for loc in range(BSTEPS):
                    g = loc // STEPS
                    for slot in range(SLOTS):
                        if slot < 2 and loc + 1 < BSTEPS:
                            exps(b, loc + 1, slot)
                        for kind, u, place in side_in(last, loc, slot):
                            side_unit(b * G + g, g, kind, u, place)
                    if loc % KT == KT - 1:
                        take(b, loc)

            act.wait_ge(x_first[0], 32)
            nc.scalar.activation(wkq_hi[:], first_w(0), ACT.Copy).then_inc(w_high, 2)
            for i in range(CHUNKS):
                c, half = i % C, i // C
                act.wait_ge(x_first[i // 2], 32 if i < 2 else 16)
                nc.scalar.activation(x_hi[:, c, half * HALF:(half + 1) * HALF], x_nat[:, i, :],
                                     ACT.Copy).then_inc(x_high, 1)
            act.wait_ge(bias_in, 32)
            for u in range(PROJ):
                project(0, u, u, ps_side[:, u % 2, :], 0)
                act.wait_ge(wv_in, 32)
                nc.scalar.activation(wv_hi[:, u, :], first_wv[:, u, :], ACT.Copy).then_inc(wv_high, 1)
            for _, _, what in prologue():
                if what is not None:
                    side_unit(-1, -1, *what)
            with act.Fori(0, B - 1) as b:
                batch(b, False)
            batch(B - 1, True)

        @block.vector
        def _(dve):
            def project(n, u, bank, g):
                sel, half = u // 2, slice(u % 2 * HALF, (u % 2 + 1) * HALF)
                dve.wait_ge(side_hi, n * PROJ + u + 1)
                if not (isinstance(n, int) and n == 0):
                    for s in stacked:
                        dve.wait_ge(s, SPREAD * n)
                nc.vector.scalar_tensor_tensor(out=kq_lo[:, sel, half], in0=bank, scalar=bkq[:, sel, g:g + 1],
                                               in1=kq_hi[:, sel, half].bitcast(F32), op0=ALU.add,
                                               op1=ALU.subtract).then_inc(side_free, 1)

            def side_unit(m, g, kind, u, place):
                at = base_of(m) + place
                bank = ps_side[:, (base_of(g) + place) % 2, :]
                if kind == "proj":
                    project(m + 2, u, bank, (g + 2) % G)
                elif kind == "pre":
                    dve.wait_ge(side_ready, at + 1)
                    nc.vector.reduce_max(max_half[:, u // 2, u % 2:u % 2 + 1], bank, AX.X).then_inc(side_free, 1)
                    if u == PRE - 1:
                        dve.wait_ge(side_free, at + 1)
                        nc.vector.tensor_reduce(out=max_q[:], in_=max_half[:], axis=AX.X, op=ALU.max,
                                                negate=True).then_inc(max_made, 1)
                else:
                    dve.wait_ge(side_ready, at + 1)
                    if not (isinstance(m, int) and m < 0):
                        dve.wait_ge(row_in, 16 * (m + 1))
                    nc.vector.tensor_copy(max_row[:], bank[0:HG * KT, 0:P]).then_inc(side_free, 1)

            def invert(b, loc, quarter):
                k = b * G * NHALF + loc // KT
                at = rsum[:, quarter * QUARTER:(quarter + 1) * QUARTER]
                dve.wait_ge(sum_taken, k + 1)
                nc.vector.reciprocal(at, at).then_inc(recip_done, 1)

            def normalise(b, loc):
                k = b * G * NHALF + loc // KT
                g, half = loc // STEPS, loc // KT % NHALF
                out = ctx_sb[:, g, half * HALF:(half + 1) * HALF]
                dve.wait_ge(recip_done, 4 * (k + 1))
                nc.vector.tensor_tensor(out, out, rsum, ALU.mult).then_inc(ctx_done, 1)

            def batch(b, last):
                for loc in range(BSTEPS):
                    g = loc // STEPS
                    for slot in range(SLOTS):
                        for kind, u, place in side_in(last, loc, slot):
                            side_unit(b * G + g, g, kind, u, place)
                        when = INVERT_SLOTS[loc // KT % NHALF]
                        i = loc % KT * SLOTS + slot
                        if loc >= KT and i in when:
                            ended = loc - loc % KT - 1
                            for k, at in enumerate(when):
                                if at == i and k < 4:
                                    invert(b, ended, k)
                                elif at == i:
                                    normalise(b, ended)

            def v_tile(u, t):
                dve.wait_ge(tail_ready, u + 1)
                nc.vector.tensor_tensor(v_sb[:, t, :], ps_s[:, t % 4, :], bv_bc[:], ALU.add).then_inc(tail_free, 1)

            def o_tile(u, b, t):
                s = t % 2
                k = b * KT + t
                dve.wait_ge(tail_ready, u + 1)
                dve.wait_ge(xbias, k + 1)
                dve.wait_ge(x2_out[s], 16 * (b * (KT // 2) + t // 2 + 1))
                nc.vector.tensor_tensor(res[:, s, :], ps_s[:, t % 4, :], x_nat[:, t, :], ALU.add).then_inc(tail_free, 1)
                dve.wait_ge(tail_free, u + 1)
                nc.vector.bn_stats(stats[:, s, :], res[:, s, :]).then_inc(ln_chain, 1)
                dve.wait_ge(const_in, CONSTS)
                dve.wait_ge(ln_chain, k + 1)
                nc.vector.bn_aggr(mv[:, s, :], stats[:, s, :]).then_inc(aggr_made, 1)
                dve.wait_ge(aggr_made, k + 1)
                nc.vector.tensor_scalar(var_eps[:, s, :], mv[:, s, 1:2], EPS, None, ALU.add).then_inc(var_made, 1)
                dve.wait_ge(rstd_made, k + 1)
                nc.vector.tensor_scalar(res[:, s, :], res[:, s, :], mv[:, s, 0:1], rstd[:, s, :],
                                        ALU.subtract, ALU.mult).then_inc(x2_ready, 1)

            dve.wait_ge(w_high, 2)
            nc.vector.tensor_tensor(wkq_lo[:], first_w(0), wkq_hi[:].bitcast(F32), ALU.subtract).then_inc(w_split, 2)
            for i in range(CHUNKS):
                at = (slice(None), i % C, slice(i // C * HALF, (i // C + 1) * HALF))
                dve.wait_ge(x_high, i + 1)
                nc.vector.tensor_tensor(x_lo[at], x_nat[:, i, :], x_hi[at].bitcast(F32),
                                        ALU.subtract).then_inc(x_split, 1)
            dve.wait_ge(bias_in, 32)
            for u in range(PROJ):
                project(0, u, ps_side[:, u % 2, :], 0)
                dve.wait_ge(wv_high, u + 1)
                nc.vector.tensor_tensor(wv_lo[:, u, :], first_wv[:, u, :], wv_hi[:, u, :].bitcast(F32),
                                        ALU.subtract).then_inc(wv_split, 1)
            dve.wait_ge(const_in, CONSTS)
            for t, c, what in prologue():
                if what is None:
                    if c == C - 1:
                        v_tile(t, t)
                else:
                    side_unit(-1, -1, *what)
            with dve.Fori(0, B - 1) as b:
                batch(b, False)
                for t in range(KT):
                    if t < 4:
                        invert(b, BSTEPS - 1, t)
                    if t == 4:
                        normalise(b, BSTEPS - 1)
                    v_tile(b * TAIL + KT + t, t)
                for t in range(KT):
                    o_tile(b * TAIL + 2 * KT + t, b, t)
            b = B - 1
            batch(b, True)
            for t in range(4):
                invert(b, BSTEPS - 1, t)
            normalise(b, BSTEPS - 1)
            for t in range(KT):
                o_tile(b * TAIL + KT + t, b, t)


TOKENS = B * S
TT = TOKENS // P
E = 8
H = 256
CH = H // P
NT = 2 * TT + E
SLOTS_ALL = NT * P
RW = 16


def four_by_four(eng, step, after=None):
    for s in range(4):
        step(s, s, s == 0, False)
        if after is not None:
            after(s)
    with eng.Fori(1, TT // 4 - 1) as j:
        for s in range(4):
            step(4 * j + s, s, False, False)
    for s in range(4):
        step(TT - 4 + s, s, False, s == 3)


def static(t, n):
    return isinstance(t, int) and t < n


def in_groups(eng, group):
    last = TT // 4 - 1
    group(0, 0, True, False)
    group(1, 1, False, False)
    with eng.Fori(1, TT // 8 - 1) as j:
        for g in range(2):
            group(2 * j + g, g, False, False)
    group(last - 1, 0, False, False)
    group(last, 1, False, True)


def scores(nc, x2, shared, stage, rw, weights_hi_lo, route, sgate_all, ident):
    with ExitStack() as ctx:
        def sb(name, shape, dt=F32):
            return ctx.enter_context(nc.sbuf_tensor(name, shape, dt))

        def sem(name):
            return ctx.enter_context(nc.semaphore(name))

        rw_raw = sb("rw_raw", [P, C, RW])
        rw_hi = sb("rw_hi", [P, C, RW], F32R)
        rw_lo = sb("rw_lo", [P, C, RW], F32R)
        x_t = sb("x_r", [P, 4, D])
        xT_hi = sb("xT_hi_r", [P, 2, C, 4 * P], F32R)
        xT_lo = sb("xT_lo_r", [P, 2, C, 4 * P], F32R)
        sT = sb("sT", [RW, 2, 4 * P])
        th = sb("th", [P, TT])
        ps_t = ctx.enter_context(nc.psum_tensor("pr_t", [P, 4, D], F32))
        ps_s = ctx.enter_context(nc.psum_tensor("pr_s", [P, 2, 4 * P], F32))
        ps_b = ctx.enter_context(nc.psum_tensor("pr_b", [P, 4, RW], F32))

        st_in = [sem(f"st_in{i}") for i in range(3)]
        st_high = sem("st_high")
        st_split = sem("st_split")
        rw_zero, rw_in, rw_high, rw_split = sem("rw_zero"), sem("rw_in"), sem("rw_high"), sem("rw_split")
        x_in = [sem(f"xr_in{i}") for i in range(4)]
        t_ready, t_hi, t_lo = sem("r_t_ready"), sem("r_t_hi"), sem("r_t_lo")
        sc_ready, sc_taken = sem("sc_ready"), sem("sc_taken")
        passed = sem("passed_s")
        back_ready, sc_done = sem("back_ready"), sem("sc_done")
        th_done, gate_done = sem("th_done"), sem("gate_done")

        block = ctx.enter_context(nc.Block())

        @block.sync
        def _(sp):
            def load_tile(t, s):
                sp.dma_start(x_t[:, s, :], x2[bass.ds(t * P, P), :]).then_inc(x_in[s], 16)

            sp.wait_ge(rw_zero, 1)
            sp.dma_start(rw_raw[:, :, 0:E + 1], rw).then_inc(rw_in, 16)
            for s in range(4):
                load_tile(s, s)
            sp.dma_start(stage[:, 0], shared[0]).then_inc(st_in[0], 16)
            for s in range(4):
                sp.wait_ge(t_ready, s + 1)
                load_tile(4 + s, s)
            for k in range(1, 3):
                sp.dma_start(stage[:, k], shared[k]).then_inc(st_in[k], 16)
            with sp.Fori(1, TT // 4 - 1) as j:
                for s in range(4):
                    sp.wait_ge(t_ready, 4 * j + s + 1)
                    load_tile(4 * j + s + 4, s)

        @block.gpsimd
        def _(pool):
            nc.gpsimd.memset(rw_raw[:], 0.0).then_inc(rw_zero, 1)
            for i in range(3 * C):
                k, c = i // C, i % C
                hi, lo = weights_hi_lo(k, c)
                pool.wait_ge(st_in[k], 16)
                nc.gpsimd.tensor_copy(hi, stage[:, k, c, :]).then_inc(st_high, 1)
                pool.wait_ge(st_high, i + 1)
                nc.gpsimd.tensor_tensor(lo, stage[:, k, c, :], hi.bitcast(F32), ALU.subtract).then_inc(st_split, 1)

        @block.tensor
        def _(pe):
            def turn(q, s):
                t = 4 * q + s
                pe.wait_ge(x_in[s], 16 * (q + 1))
                if not static(q, 1):
                    pe.wait_ge(t_hi, t - 3)
                    pe.wait_ge(t_lo, t - 3)
                for c in range(C):
                    done = nc.tensor.transpose(ps_t[:, s, c * P:(c + 1) * P], x_t[:, s, c * P:(c + 1) * P], ident[:])
                done.then_inc(t_ready, 1)

            def score(q, g):
                pe.wait_ge(t_hi, 4 * q + 4)
                pe.wait_ge(t_lo, 4 * q + 4)
                if not static(q, 2):
                    pe.wait_ge(sc_taken, q - 1)
                for c in range(C):
                    xh, xl = xT_hi[:, g, c, :], xT_lo[:, g, c, :]
                    for i, (w, m) in enumerate(((rw_hi, xh), (rw_lo, xh), (rw_hi, xl))):
                        done = nc.tensor.matmul(ps_s[0:RW, g, :], w[:, c, :], m, start=c == 0 and i == 0,
                                                stop=c == C - 1 and i == 2)
                done.then_inc(sc_ready, 1)

            def back(q, g):
                pe.wait_ge(sc_taken, q + 1)
                if not static(q, 1):
                    pe.wait_ge(sc_done, q)
                pe.sem_inc(passed, 1)
                for s in range(4):
                    done = nc.tensor.transpose(ps_b[:, s, :], sT[:, g, s * P:(s + 1) * P], ident[0:RW, 0:RW])
                done.then_inc(back_ready, 1)

            def group(q, g, first, last):
                if first:
                    for s in range(4):
                        turn(q, s)
                if not last:
                    for s in range(4):
                        turn(q + 1, s)
                if first:
                    pe.wait_ge(rw_split, 1)
                score(q, g)
                if not first:
                    back(q - 1, 1 - g)
                if last:
                    back(q, g)

            in_groups(pe, group)

        @block.scalar
        def _(act):
            def high(q, g):
                if not static(q, 2):
                    act.wait_ge(sc_ready, q - 1)
                for s in range(4):
                    act.wait_ge(t_ready, 4 * q + s + 1)
                    nc.scalar.activation(xT_hi[:, g, :, s * P:(s + 1) * P],
                                         ps_t[:, s, :].rearrange("p (c t) -> p c t", c=C), ACT.Copy).then_inc(t_hi, 1)

            def group(q, g, first, last):
                if first:
                    high(q, g)
                if not last:
                    high(q + 1, 1 - g)

            act.wait_ge(rw_in, 16)
            nc.scalar.activation(rw_hi[:], rw_raw[:], ACT.Copy).then_inc(rw_high, 1)
            in_groups(act, group)
            act.wait_ge(sc_done, TT // 4)
            nc.scalar.activation(th[:], route[:, :, E], ACT.Tanh, scale=0.5).then_inc(th_done, 1)

        @block.vector
        def _(dve):
            def low(q, g):
                if not static(q, 2):
                    dve.wait_ge(sc_ready, q - 1)
                for s in range(4):
                    dve.wait_ge(t_hi, 4 * q + s + 1)
                    nc.vector.tensor_tensor(xT_lo[:, g, :, s * P:(s + 1) * P],
                                            ps_t[:, s, :].rearrange("p (c t) -> p c t", c=C),
                                            xT_hi[:, g, :, s * P:(s + 1) * P].bitcast(F32),
                                            ALU.subtract).then_inc(t_lo, 1)

            def take(q, g):
                dve.wait_ge(sc_ready, q + 1)
                if not static(q, 2):
                    dve.wait_ge(back_ready, q - 1)
                nc.vector.tensor_copy(sT[:, g, :], ps_s[0:RW, g, :]).then_inc(sc_taken, 1)

            def read(q):
                dve.wait_ge(back_ready, q + 1)
                nc.vector.tensor_copy(route[:, bass.ds(4 * q, 4), :], ps_b[:, :, 0:E + 1]).then_inc(sc_done, 1)

            def group(q, g, first, last):
                if first:
                    low(q, g)
                if not last:
                    low(q + 1, 1 - g)
                take(q, g)
                if not first:
                    read(q - 1)
                if last:
                    read(q)

            dve.wait_ge(rw_high, 1)
            nc.vector.tensor_tensor(rw_lo[:], rw_raw[:], rw_hi[:].bitcast(F32), ALU.subtract).then_inc(rw_split, 1)
            in_groups(dve, group)
            dve.wait_ge(th_done, 1)
            nc.vector.tensor_scalar(sgate_all[:], th[:], 0.5, 0.5, ALU.mult, ALU.add).then_inc(gate_done, 1)


def shared_and_place(nc, x2, sgu_hi, sgu_lo, sd_hi, sd_lo, wgu, wd, base, gu_sb, wd_sb, gu_in, route, sgate_all, weights, pos,
                     tile_expert, table, ident):
    with ExitStack() as ctx:
        def sb(name, shape, dt=F32):
            return ctx.enter_context(nc.sbuf_tensor(name, shape, dt))

        def sem(name):
            return ctx.enter_context(nc.semaphore(name))

        def psum(name, shape):
            return ctx.enter_context(nc.psum_tensor(name, shape, F32))

        x_t = sb("x_t", [P, 4, D])
        xT_hi = sb("xT_hi", [P, 2, C, P], F32R)
        xT_lo = sb("xT_lo", [P, 2, C, P], F32R)
        act_g = sb("act_g", [P, 2, D])
        hid = sb("hid", [P, 2, D])
        hT_hi = sb("hT_hi", [P, 2, C, P], F32R)
        hT_lo = sb("hT_lo", [P, 2, C, P], F32R)
        sgate = sb("sgate", [P, 2, 1])
        out_t = sb("out_t", [P, 2, D])

        ps_t = psum("ps_t", [P, 2, D])
        ps_gu = psum("ps_gu", [P, 2, D])
        ps_ht = psum("ps_ht", [P, D])
        ps_d = psum("ps_d", [P, 2, D])

        x_in = [sem(f"xt_in{i}") for i in range(4)]
        t_ready = sem("t_ready")
        t_hi = sem("t_hi")
        t_lo = sem("t_lo")
        gu_ready = sem("gu_ready")
        silu_done = sem("silu_done")
        hid_done = sem("hid_done")
        gate_done = sem("gate_copied")
        ht_ready = sem("ht_ready")
        ht_hi = sem("ht_hi")
        ht_lo = sem("ht_lo")
        d_ready = sem("d_ready")
        base_done = sem("base_done")
        base_out = [sem("base_out0"), sem("base_out1")]

        expert = sb("expert", [P, TT, E])
        expert_i = sb("expert_i", [P, TT, E], I32)
        tri = sb("tri", [P, P])
        all_ones = sb("all_ones", [P, P])
        token = sb("token", [P, TT], I32)
        tile_start_i = sb("tile_start_i", [P, NT, E], I32)
        tile_start = sb("tile_start", [P, NT, E])
        zero_table = sb("zero_table", [P, NT], I32)
        big = [sb(f"big{i}", [P, TT, E]) for i in range(6)]
        one = sb("one", [P, 2, TT, E])
        col = [sb(f"col{i}", [P, TT]) for i in range(8)]
        cnt = [sb(f"cnt{i}", [P, E]) for i in range(6)]
        cnt_i = [sb(f"cnt_i{i}", [P, E], I32) for i in range(3)]
        col_i = [sb(f"col_i{i}", [P, 2, TT], I32) for i in range(5)]
        ends = sb("ends", [P, NT, E])
        te = sb("te", [P, NT])
        index = sb("index", [P, 8], I32)
        who = sb("who", [P, 4], I32)
        ps_count = psum("ps_count", [P, 2, TT * E])
        ps_rank, ps_total = ps_count[:, 0, :], ps_count[:, 1, :]

        passed = sem("passed_p")
        made = sem("made")
        zeroed = sem("zeroed")
        links = sem("links")
        visits = sem("visits")
        counted = sem("counted")
        gap_ready = sem("gap_ready")
        exp_done = sem("exp_done")
        placed = sem("placed")
        copied = sem("copied")
        scattered = [sem(f"scattered{i}") for i in range(8)]

        block = ctx.enter_context(nc.Block())

        @block.sync
        def _(sp):
            def load_tile(t, s):
                sp.dma_start(x_t[:, s, :], x2[bass.ds(t * P, P), :]).then_inc(x_in[s], 16)

            for s in range(4):
                load_tile(s, s)
            sp.wait_ge(made, 5)
            sp.dma_start(table.rearrange("(p n) a -> p (n a)", p=P), zero_table[:]).then_inc(zeroed, 16)
            for e in range(E):
                sp.dma_start(gu_sb[:, e], wgu[e]).then_inc(gu_in, 16)
                sp.dma_start(wd_sb[:, e], wd[e]).then_inc(gu_in, 16)

            def store(t, s):
                sp.wait_ge(base_done, t + 1)
                sp.dma_start(base[bass.ds(t * P, P), :], out_t[:, s % 2, :]).then_inc(base_out[s % 2], 16)

            with sp.Fori(0, TT // 4 - 1) as j:
                for s in range(4):
                    store(4 * j + s, s)
                    load_tile(4 * j + s + 4, s)
            for s in range(4):
                store(TT - 4 + s, s)
            for i in range(2):
                sp.wait_ge(base_out[i], 16 * TT // 2)

        @block.gpsimd
        def _(pool):
            n = [0]

            def after(ins):
                n[0] += 1
                ins.then_inc(made, 1)
                pool.wait_ge(made, n[0])

            after(nc.gpsimd.iota(expert_i[:], [[0, TT], [1, E]], base=0, channel_multiplier=0))
            after(nc.gpsimd.iota(token[:], [[P, TT]], base=0, channel_multiplier=1))
            after(nc.gpsimd.iota(tile_start_i[:], [[P, NT], [0, E]], base=0, channel_multiplier=0))
            after(nc.gpsimd.memset(all_ones[:], 1.0))
            after(nc.gpsimd.memset(zero_table[:], 0))
            after(nc.gpsimd.affine_select(out=tri[:], in_=all_ones[:], compare_op=ALU.is_gt, fill=0.0, base=0,
                                          pattern=[[1, P]], channel_multiplier=-1))
            pool.wait_ge(placed, 1)
            pool.wait_ge(zeroed, 16)
            def scatter(j, first):
                for s in range(4):
                    if not first:
                        for v in range(2):
                            pool.wait_ge(scattered[2 * s + v], 16 * j)
                        pool.sem_inc(passed, 1)
                    nc.gpsimd.tensor_copy(who[:, s:s + 1], token[:, bass.ds(4 * j + s, 1)]).then_inc(copied, 1)
                    for v in range(2):
                        nc.gpsimd.tensor_copy(index[:, 2 * s + v:2 * s + v + 1],
                                              col_i[4][:, v, bass.ds(4 * j + s, 1)]).then_inc(copied, 1)
                    pool.wait_ge(copied, 12 * j + 3 * s + 3)
                    pool.sem_inc(passed, 1)
                    for v in range(2):
                        nc.gpsimd.indirect_dma_start(
                            table, bass.IndirectOffsetOnAxis(ap=index[:, 2 * s + v:2 * s + v + 1].bitcast(U32), axis=0),
                            who[:, s:s + 1], None).then_inc(scattered[2 * s + v], 16)

            scatter(0, True)
            with pool.Fori(1, TT // 4) as j:
                scatter(j, False)
            for i in range(8):
                pool.wait_ge(scattered[i], 16 * (TT // 4))

        @block.tensor
        def _(pe):
            def turn(t, s):
                pe.wait_ge(x_in[s], 16 * (t // 4 + 1) if isinstance(t, int) else x_count(t, s))
                if not static(t, 2):
                    pe.wait_ge(t_hi, t - 1)
                    pe.wait_ge(t_lo, t - 1)
                for c in range(C):
                    done = nc.tensor.transpose(ps_t[:, s % 2, c * P:(c + 1) * P],
                                               x_t[:, s, c * P:(c + 1) * P], ident[:])
                done.then_inc(t_ready, 1)

            def x_count(t, s):
                return (t - s) * 4 + 16

            def three(out, a, b, c, last_c):
                for i, (w, m) in enumerate(((a[0], b[0]), (a[1], b[0]), (a[0], b[1]))):
                    done = nc.tensor.matmul(out, w, m, start=c == 0 and i == 0, stop=c == last_c and i == 2)
                return done

            def up(t, s):
                pe.wait_ge(t_hi, t + 1)
                pe.wait_ge(t_lo, t + 1)
                if not static(t, 1):
                    pe.wait_ge(hid_done, t)
                for out, m_of in ((ps_gu[:, 0, :], lambda c: (sgu_hi[:, c, 0, :], sgu_lo[:, c, 0, :])),
                                  (ps_gu[:, 1, :], lambda c: (sgu_hi[:, c, 1, :], sgu_lo[:, c, 1, :]))):
                    for c in range(C):
                        done = three(out, (xT_hi[:, s % 2, c, :], xT_lo[:, s % 2, c, :]), m_of(c), c, C - 1)
                done.then_inc(gu_ready, 1)

            def turn_hidden(t, s):
                pe.wait_ge(hid_done, t + 1)
                if not static(t, 1):
                    pe.wait_ge(ht_hi, t)
                    pe.wait_ge(ht_lo, t)
                for c in range(C):
                    done = nc.tensor.transpose(ps_ht[:, c * P:(c + 1) * P], hid[:, s % 2, c * P:(c + 1) * P], ident[:])
                done.then_inc(ht_ready, 1)

            def down(t, s):
                pe.wait_ge(ht_hi, t + 1)
                pe.wait_ge(ht_lo, t + 1)
                if not static(t, 2):
                    pe.wait_ge(base_done, t - 1)
                for c in range(C):
                    done = three(ps_d[:, s % 2, :], (hT_hi[:, s % 2, c, :], hT_lo[:, s % 2, c, :]),
                                 (sd_hi[:, c, :], sd_lo[:, c, :]), c, C - 1)
                done.then_inc(d_ready, 1)

            def step(t, s, first, last):
                if first:
                    turn(t, s)
                up(t, s)
                if not last:
                    turn(t + 1, (s + 1) % 4)
                if not first:
                    down(t - 1, s - 1 if s else 3)
                turn_hidden(t, s)
                if last:
                    down(t, s)

            def after(i):
                if i != 2:
                    return
                pe.wait_ge(made, 6)
                pe.wait_ge(visits, 1)
                flat = big[4][:].rearrange("p t e -> p (t e)")
                nc.tensor.matmul(ps_rank[:], tri[:], flat, start=True, stop=True)
                nc.tensor.matmul(ps_total[:], all_ones[:], flat, start=True, stop=True).then_inc(counted, 1)

            four_by_four(pe, step, after)

        @block.scalar
        def _(act):
            def x_high(t, s):
                act.wait_ge(t_ready, t + 1)
                if not static(t, 2):
                    act.wait_ge(gu_ready, t - 1)
                nc.scalar.activation(xT_hi[:, s % 2], ps_t[:, s % 2, :].rearrange("p (c t) -> p c t", c=C),
                                     ACT.Copy).then_inc(t_hi, 1)

            def gate(t, s):
                act.wait_ge(gu_ready, t + 1)
                if not static(t, 2):
                    act.wait_ge(hid_done, t - 1)
                nc.scalar.activation(act_g[:, s % 2, :], ps_gu[:, 0, :], ACT.Silu).then_inc(silu_done, 1)

            def h_high(t, s):
                act.wait_ge(ht_ready, t + 1)
                if not static(t, 2):
                    act.wait_ge(d_ready, t - 1)
                nc.scalar.activation(hT_hi[:, s % 2], ps_ht[:].rearrange("p (c t) -> p c t", c=C),
                                     ACT.Copy).then_inc(ht_hi, 1)

            def step(t, s, first, last):
                if first:
                    x_high(t, s)
                gate(t, s)
                if not last:
                    x_high(t + 1, s + 1)
                h_high(t, s)

            def after(i):
                if i == 2:
                    act.wait_ge(gap_ready, 1)
                    nc.scalar.activation(col[4][:], col[3][:], ACT.Exp).then_inc(exp_done, 1)

            four_by_four(act, step, after)

        @block.vector
        def _(dve):
            def x_low(t, s):
                dve.wait_ge(t_hi, t + 1)
                if not static(t, 2):
                    dve.wait_ge(gu_ready, t - 1)
                nc.vector.tensor_tensor(xT_lo[:, s % 2], ps_t[:, s % 2, :].rearrange("p (c t) -> p c t", c=C),
                                        xT_hi[:, s % 2].bitcast(F32), ALU.subtract).then_inc(t_lo, 1)

            def hidden(t, s):
                dve.wait_ge(silu_done, t + 1)
                if not static(t, 2):
                    dve.wait_ge(ht_ready, t - 1)
                nc.vector.tensor_tensor(hid[:, s % 2, :], act_g[:, s % 2, :], ps_gu[:, 1, :],
                                        ALU.mult).then_inc(hid_done, 1)
                if not static(t, 2):
                    dve.wait_ge(base_done, t - 1)
                nc.vector.tensor_copy(sgate[:, s % 2, :], sgate_all[:, bass.ds(t, 1)]).then_inc(gate_done, 1)

            def h_low(t, s):
                dve.wait_ge(ht_hi, t + 1)
                if not static(t, 2):
                    dve.wait_ge(d_ready, t - 1)
                nc.vector.tensor_tensor(hT_lo[:, s % 2], ps_ht[:].rearrange("p (c t) -> p c t", c=C),
                                        hT_hi[:, s % 2].bitcast(F32), ALU.subtract).then_inc(ht_lo, 1)

            def finish(t, s):
                dve.wait_ge(d_ready, t + 1)
                dve.wait_ge(gate_done, t + 1)
                if not static(t, 2):
                    dve.wait_ge(base_out[s % 2], 16 * (t // 2) if isinstance(t, int) else 8 * (t - s % 2))
                nc.vector.scalar_tensor_tensor(out=out_t[:, s % 2, :], in0=ps_d[:, s % 2, :], scalar=sgate[:, s % 2, :],
                                               in1=x_t[:, s, :], op0=ALU.mult, op1=ALU.add).then_inc(base_done, 1)

            def step(t, s, first, last):
                if first:
                    x_low(t, s)
                hidden(t, s)
                if not last:
                    x_low(t + 1, s + 1)
                if not first:
                    finish(t - 1, s - 1 if s else 3)
                h_low(t, s)
                if last:
                    finish(t, s)

            n = [0]

            def link(ins):
                n[0] += 1
                ins.then_inc(links, 1)
                dve.wait_ge(links, n[0])

            def over_experts(x):
                return x.unsqueeze(2).broadcast_to((P, TT, E))

            v = nc.vector
            def pick(scores, largest, chosen):
                link(v.tensor_reduce(out=largest[:], in_=scores, axis=AX.X, op=ALU.max))
                link(v.tensor_tensor(big[0][:], scores, over_experts(largest[:]), ALU.is_equal))
                link(v.scalar_tensor_tensor(out=big[0][:], in0=big[0][:], scalar=-float(E), in1=expert[:],
                                            op0=ALU.mult, op1=ALU.add))
                link(v.tensor_reduce(out=col[2][:], in_=big[0][:], axis=AX.X, op=ALU.min))
                link(v.tensor_scalar(col[2][:], col[2][:], float(E), None, ALU.add))
                link(v.tensor_tensor(chosen, expert[:], over_experts(col[2][:]), ALU.is_equal))

            def first_choice():
                dve.wait_ge(made, 3)
                link(v.tensor_copy(expert[:], expert_i[:]))
                link(v.tensor_copy(tile_start[:], tile_start_i[:]))

                pick(route[:, :, 0:E], col[0], one[:, 0])

            def second_choice():
                link(v.tensor_scalar(big[1][:], one[:, 0], -3.0e38, None, ALU.mult))
                link(v.tensor_scalar(big[2][:], one[:, 0], -3.0e38, 3.0e38, ALU.mult, ALU.add))
                link(v.tensor_tensor(big[1][:], big[1][:], big[2][:], ALU.add))
                link(v.tensor_tensor(big[1][:], route[:, :, 0:E], big[1][:], ALU.min))
                pick(big[1][:], col[1], one[:, 1])
                link(v.tensor_tensor(big[4][:], one[:, 0], one[:, 1], ALU.add))
                v.tensor_tensor(col[3][:], col[1][:], col[0][:], ALU.subtract).then_inc(gap_ready, 1)
                dve.wait_ge(links, n[0])
                v.tensor_scalar(col[5][:], col[2][:], 0.0, None, ALU.mult).then_inc(visits, 1)

            def count():
                dve.wait_ge(exp_done, 1)
                link(v.tensor_scalar(col[6][:], col[4][:], 1.0, None, ALU.add))
                link(v.reciprocal(weights[:, 0, :], col[6][:]))
                link(v.tensor_tensor(weights[:, 1, :], weights[:, 0, :], col[4][:], ALU.mult))
                dve.wait_ge(counted, 1)
                link(v.tensor_copy(big[0][:], ps_total[:].rearrange("p (t e) -> p t e", e=E)))
                src, dst = big[0], big[1]
                first = src
                step = 1
                bufs = [big[1], big[2]]
                while step < TT:
                    dst = bufs[0]
                    bufs.reverse()
                    link(v.tensor_tensor(dst[:, step:, :], src[:, step:, :], src[:, :TT - step, :], ALU.add))
                    link(v.tensor_copy(dst[:, :step, :], src[:, :step, :]))
                    src = dst
                    step *= 2
                link(v.tensor_tensor(big[3][:], src[:], first[:], ALU.subtract))
                link(v.tensor_tensor(big[3][:], big[3][:], ps_rank[:].rearrange("p (t e) -> p t e", e=E), ALU.add))
                return src

            def positions(src):
                link(v.tensor_scalar(cnt[0][:], src[:, TT - 1, :], float(P - 1), None, ALU.add))
                link(v.tensor_copy(cnt_i[0][:], cnt[0][:]))
                shift = P.bit_length() - 1
                link(v.tensor_scalar(cnt_i[1][:], cnt_i[0][:], shift, None, ALU.logical_shift_right))
                link(v.tensor_copy(cnt[1][:], cnt_i[1][:]))
                link(v.tensor_scalar(cnt[1][:], cnt[1][:], float(P), None, ALU.mult))
                a, others = cnt[1], [cnt[2], cnt[3]]
                step = 1
                while step < E:
                    b = others[0]
                    others.reverse()
                    link(v.tensor_tensor(b[:, step:], a[:, step:], a[:, :E - step], ALU.add))
                    link(v.tensor_copy(b[:, :step], a[:, :step]))
                    a = b
                    step *= 2
                end = a
                link(v.tensor_tensor(cnt[4][:], end[:], cnt[1][:], ALU.subtract))
                link(v.tensor_tensor(big[3][:], big[3][:], cnt[4][:].unsqueeze(1).broadcast_to((P, TT, E)), ALU.add))
                for k in range(2):
                    link(v.tensor_tensor(big[5][:], big[3][:], one[:, k], ALU.mult))
                    link(v.tensor_reduce(out=col[7][:], in_=big[5][:], axis=AX.X, op=ALU.add))
                    link(v.tensor_copy(pos[:, k, :], col[7][:]))
                link(v.tensor_scalar(col_i[0][:], pos[:], P - 1, None, ALU.bitwise_and))
                link(v.tensor_scalar(col_i[1][:], pos[:], shift, None, ALU.logical_shift_right))
                rows = ends[:].rearrange("p n e -> p (n e)")[:, 0:4 * TT].rearrange("p (a k t) -> p a k t", a=2, k=2)
                link(v.tensor_copy(rows[:, 0], col_i[0][:]))
                link(v.tensor_copy(rows[:, 1], col_i[1][:]))
                link(v.scalar_tensor_tensor(out=rows[:, 0], in0=rows[:, 0], scalar=float(NT), in1=rows[:, 1],
                                            op0=ALU.mult, op1=ALU.add))
                v.tensor_copy(col_i[4][:], rows[:, 0]).then_inc(placed, 1)
                dve.wait_ge(placed, 1)
                link(v.tensor_tensor(ends[:], tile_start[:], end[:].unsqueeze(1).broadcast_to((P, NT, E)), ALU.is_ge))
                link(v.tensor_reduce(out=te[:], in_=ends[:], axis=AX.X, op=ALU.add))
                link(v.tensor_scalar(te[:], te[:], float(E - 1), None, ALU.min))
                link(v.tensor_copy(tile_expert[:], te[:]))

            def after(i):
                if i == 0:
                    first_choice()
                elif i == 1:
                    second_choice()
                elif i == 2:
                    running.append(count())
                else:
                    positions(running[0])

            running = []
            four_by_four(dve, step, after)


def experts(nc, x2, table, tile_expert, gu_sb, wd_sb, gu_in, y, ident):
    with ExitStack() as ctx:
        def sb(name, shape, dt=F32):
            return ctx.enter_context(nc.sbuf_tensor(name, shape, dt))

        def sem(name):
            return ctx.enter_context(nc.semaphore(name))

        def psum(name, shape):
            return ctx.enter_context(nc.psum_tensor(name, shape, F32))

        who_all = sb("who_all", [P, NT], I32)
        who = sb("who_e", [P, 4], I32)
        x_g = sb("x_g", [P, 4, D])
        xT = sb("xT_e", [P, 2, C, P])
        act_g = sb("act_e", [P, 2, H])
        hid = sb("hid_e", [P, 2, H])
        hT = sb("hT_e", [P, 2, CH, P])
        y_t = sb("y_t", [P, 4, D])
        ps_t = psum("pe_t", [P, 2, D])
        ps_h = psum("pe_h", [P, 2, D])
        ps_ht = psum("pe_ht", [P, 2, D])
        ps_y = psum("pe_y", [P, 2, D])

        passed = sem("passed_e")
        who_in = sem("who_in")
        who_copied = sem("who_copied")
        x_in = [sem(f"xg_in{i}") for i in range(4)]
        t_ready = sem("et_ready")
        t_done = sem("et_done")
        h_ready = sem("eh_ready")
        silu_done = sem("esilu_done")
        hid_done = sem("ehid_done")
        ht_ready = sem("eht_ready")
        ht_done = sem("eht_done")
        y_ready = sem("ey_ready")
        y_done = sem("ey_done")
        y_out = [sem(f"y_out{i}") for i in range(4)]

        block = ctx.enter_context(nc.Block())

        def static(t, n):
            return isinstance(t, int) and t < n

        def turns_of(t, s):
            return 4 * (t - s)

        @block.sync
        def _(sp):
            sp.dma_start(who_all[:], table.rearrange("(p n) a -> p (n a)", p=P)).then_inc(who_in, 16)
            with sp.Fori(0, NT // 4) as j:
                for s in range(4):
                    t = 4 * j + s
                    sp.wait_ge(y_done, t + 1)
                    sp.dma_start(y[bass.ds(t * P, P), :], y_t[:, s, :]).then_inc(y_out[s], 16)
            for s in range(4):
                sp.wait_ge(y_out[s], 16 * (NT // 4))

        @block.gpsimd
        def _(pool):
            pool.wait_ge(who_in, 16)

            def gather(t, s):
                if not static(t, 4):
                    pool.wait_ge(t_ready, t - 3)
                    pool.sem_inc(passed, 1)
                nc.gpsimd.tensor_copy(who[:, s:s + 1], who_all[:, bass.ds(t, 1)]).then_inc(who_copied, 1)
                pool.wait_ge(who_copied, t + 1)
                pool.sem_inc(passed, 1)
                nc.gpsimd.indirect_dma_start(
                    x_g[:, s, :], None, x2, bass.IndirectOffsetOnAxis(ap=who[:, s:s + 1].bitcast(U32), axis=0),
                ).then_inc(x_in[s], 16)

            for s in range(4):
                gather(s, s)
            with pool.Fori(1, NT // 4) as j:
                for s in range(4):
                    gather(4 * j + s, s)

        def pipeline(eng, step):
            step(0, 0, True, False)
            for s in range(1, 4):
                step(s, s, False, False)
            with eng.Fori(1, NT // 4 - 1) as j:
                for s in range(4):
                    step(4 * j + s, s, False, False)
            for s in range(4):
                step(NT - 4 + s, s, False, s == 3)

        @block.tensor
        def _(pe):
            def turn(t, s):
                pe.wait_ge(x_in[s], turns_of(t, s) + 16)
                if not static(t, 2):
                    pe.wait_ge(t_done, t - 1)
                for c in range(C):
                    done = nc.tensor.transpose(ps_t[:, s % 2, c * P:(c + 1) * P], x_g[:, s, c * P:(c + 1) * P], ident[:])
                done.then_inc(t_ready, 1)

            def up(t, s, e):
                pe.wait_ge(t_done, t + 1)
                if not static(t, 2):
                    pe.wait_ge(hid_done, t - 1)
                for c in range(C):
                    done = nc.tensor.matmul(ps_h[:, s % 2, :], xT[:, s % 2, c, :],
                                            gu_sb[:, bass.ds(e, 1), c, :].rearrange("p a n -> p (a n)"),
                                            start=c == 0, stop=c == C - 1)
                done.then_inc(h_ready, 1)

            def turn_hidden(t, s):
                pe.wait_ge(hid_done, t + 1)
                if not static(t, 2):
                    pe.wait_ge(ht_done, t - 1)
                for c in range(CH):
                    done = nc.tensor.transpose(ps_ht[:, s % 2, c * P:(c + 1) * P], hid[:, s % 2, c * P:(c + 1) * P], ident[:])
                done.then_inc(ht_ready, 1)

            def down(t, s, e):
                pe.wait_ge(ht_done, t + 1)
                if not static(t, 2):
                    pe.wait_ge(y_done, t - 1)
                for c in range(CH):
                    done = nc.tensor.matmul(ps_y[:, s % 2, :], hT[:, s % 2, c, :],
                                            wd_sb[:, bass.ds(e, 1), c, :].rearrange("p a n -> p (a n)"),
                                            start=c == 0, stop=c == CH - 1)
                done.then_inc(y_ready, 1)

            def expert_of(t):
                return pe.value_load(tile_expert[0:1, bass.ds(t, 1)], min_val=0, max_val=E - 1)

            def step(t, s, first, last):
                if first:
                    turn(t, s)
                up(t, s, expert_of(t))
                if not last:
                    turn(t + 1, (s + 1) % 4)
                if not first:
                    down(t - 1, (s - 1) % 4, expert_of(t - 1))
                turn_hidden(t, s)
                if last:
                    down(t, s, expert_of(t))

            pe.wait_ge(gu_in, 16 * 2 * E)
            pipeline(pe, step)

        @block.scalar
        def _(act):
            def x_copy(t, s):
                act.wait_ge(t_ready, t + 1)
                if not static(t, 2):
                    act.wait_ge(h_ready, t - 1)
                nc.scalar.activation(xT[:, s % 2], ps_t[:, s % 2, :].rearrange("p (c t) -> p c t", c=C),
                                     ACT.Copy).then_inc(t_done, 1)

            def gate(t, s):
                act.wait_ge(h_ready, t + 1)
                if not static(t, 2):
                    act.wait_ge(hid_done, t - 1)
                nc.scalar.activation(act_g[:, s % 2, :], ps_h[:, s % 2, 0:H], ACT.Silu).then_inc(silu_done, 1)

            def step(t, s, first, last):
                if first:
                    x_copy(t, s)
                gate(t, s)
                if not last:
                    x_copy(t + 1, (s + 1) % 4)

            pipeline(act, step)

        @block.vector
        def _(dve):
            def hidden(t, s):
                dve.wait_ge(silu_done, t + 1)
                if not static(t, 2):
                    dve.wait_ge(ht_ready, t - 1)
                nc.vector.tensor_tensor(hid[:, s % 2, :], act_g[:, s % 2, :], ps_h[:, s % 2, H:2 * H],
                                        ALU.mult).then_inc(hid_done, 1)

            def h_copy(t, s):
                dve.wait_ge(ht_ready, t + 1)
                if not static(t, 2):
                    dve.wait_ge(y_ready, t - 1)
                nc.vector.tensor_copy(hT[:, s % 2], ps_ht[:, s % 2, 0:H].rearrange("p (c t) -> p c t", c=CH)).then_inc(ht_done, 1)

            def y_copy(t, s):
                dve.wait_ge(y_ready, t + 1)
                if not static(t, 4):
                    dve.wait_ge(y_out[s], turns_of(t, s))
                nc.vector.tensor_copy(y_t[:, s, :], ps_y[:, s % 2, :]).then_inc(y_done, 1)

            def step(t, s, first, last):
                hidden(t, s)
                if not first:
                    y_copy(t - 1, (s - 1) % 4)
                h_copy(t, s)
                if last:
                    y_copy(t, s)

            pipeline(dve, step)


def combine(nc, base, y, pos, weights, out):
    with ExitStack() as ctx:
        def sb(name, shape, dt=F32):
            return ctx.enter_context(nc.sbuf_tensor(name, shape, dt))

        def sem(name):
            return ctx.enter_context(nc.semaphore(name))

        index = sb("c_index", [P, 8], I32)
        y_g = sb("y_g", [P, 4, 2, D])
        b_t = sb("b_t", [P, 4, D])
        w_t = sb("w_t", [P, 4, 2])
        acc = sb("acc", [P, 4, D])
        res = sb("res_c", [P, 4, D])
        stats = sb("stats_c", [P, 4, 6])
        mv = sb("mv_c", [P, 4, 2])
        var_eps = sb("var_eps_c", [P, 4, 1])
        minus_half = sb("minus_half_c", [P, 1])
        rstd = sb("rstd_c", [P, 4, 1])

        passed = sem("passed_c")
        copied = sem("c_copied")
        y_in = [sem(f"y_in{i}") for i in range(4)]
        b_in = [sem(f"b_in{i}") for i in range(4)]
        w_copied = sem("w_copied")
        first_added = sem("first_added")
        added = sem("added")
        stats_made = sem("stats_made")
        aggr_made = sem("c_aggr_made")
        var_made = sem("c_var_made")
        rstd_made = sem("c_rstd_made")
        normal = sem("normal")
        out_done = [sem(f"out_done{i}") for i in range(4)]
        half_set = sem("half_set")

        block = ctx.enter_context(nc.Block())
        GROUPS = TT // 4

        @block.sync
        def _(sp):
            def load(t, s):
                sp.dma_start(b_t[:, s, :], base[bass.ds(t * P, P), :]).then_inc(b_in[s], 16)

            def store(t, s):
                sp.wait_ge(normal, t + 1)
                sp.dma_start(out[bass.ds(t * P, P), :], res[:, s, :]).then_inc(out_done[s], 16)

            for s in range(4):
                load(s, s)
            with sp.Fori(0, GROUPS - 1) as j:
                for s in range(4):
                    store(4 * j + s, s)
                    load(4 * j + s + 4, s)
            for s in range(4):
                store(TT - 4 + s, s)
            for s in range(4):
                sp.wait_ge(out_done[s], 16 * GROUPS)

        @block.gpsimd
        def _(pool):
            nc.gpsimd.memset(minus_half[:], -0.5).then_inc(half_set, 1)
            pool.wait_ge(half_set, 1)

            def gather(t, s):
                for k in range(2):
                    nc.gpsimd.tensor_copy(index[:, 2 * s + k:2 * s + k + 1], pos[:, k, bass.ds(t, 1)]).then_inc(copied, 1)
                    pool.wait_ge(copied, 2 * t + k + 1)
                    pool.sem_inc(passed, 1)
                    nc.gpsimd.indirect_dma_start(
                        y_g[:, s, k, :], None, y,
                        bass.IndirectOffsetOnAxis(ap=index[:, 2 * s + k:2 * s + k + 1].bitcast(U32), axis=0),
                    ).then_inc(y_in[s], 16)

            def root(t, s):
                pool.wait_ge(var_made, t + 1)
                nc.gpsimd.tensor_tensor(rstd[:, s, :], var_eps[:, s, :], minus_half[:], ALU.pow).then_inc(rstd_made, 1)

            for s in range(4):
                gather(s, s)
            with pool.Fori(0, GROUPS - 1) as j:
                for s in range(4):
                    root(4 * j + s, s)
                    gather(4 * j + s + 4, s)
            for s in range(4):
                root(TT - 4 + s, s)

        @block.vector
        def _(dve):
            def one_tile(t, s, turn):
                dve.wait_ge(y_in[s], 32 * turn + 32)
                dve.wait_ge(b_in[s], 16 * turn + 16)
                nc.vector.tensor_copy(w_t[:, s, :], weights[:, :, bass.ds(t, 1)].rearrange("p k a -> p (k a)")).then_inc(w_copied, 1)
                dve.wait_ge(w_copied, t + 1)
                nc.vector.scalar_tensor_tensor(out=acc[:, s, :], in0=y_g[:, s, 0, :], scalar=w_t[:, s, 0:1],
                                               in1=b_t[:, s, :], op0=ALU.mult, op1=ALU.add).then_inc(first_added, 1)
                dve.wait_ge(first_added, t + 1)
                if not isinstance(turn, int):
                    dve.wait_ge(out_done[s], 16 * turn)
                nc.vector.scalar_tensor_tensor(out=res[:, s, :], in0=y_g[:, s, 1, :], scalar=w_t[:, s, 1:2],
                                               in1=acc[:, s, :], op0=ALU.mult, op1=ALU.add).then_inc(added, 1)
                dve.wait_ge(added, t + 1)
                nc.vector.bn_stats(stats[:, s, :], res[:, s, :]).then_inc(stats_made, 1)
                dve.wait_ge(y_in[s], 32)
                dve.wait_ge(stats_made, t + 1)
                nc.vector.bn_aggr(mv[:, s, :], stats[:, s, :]).then_inc(aggr_made, 1)
                dve.wait_ge(aggr_made, t + 1)
                nc.vector.tensor_scalar(var_eps[:, s, :], mv[:, s, 1:2], EPS, None, ALU.add).then_inc(var_made, 1)

            def norm(t, s):
                dve.wait_ge(rstd_made, t + 1)
                nc.vector.tensor_scalar(res[:, s, :], res[:, s, :], mv[:, s, 0:1], rstd[:, s, :],
                                        ALU.subtract, ALU.mult).then_inc(normal, 1)

            one_tile(0, 0, 0)
            for s in range(1, 4):
                one_tile(s, s, 0)
                norm(s - 1, s - 1)
            with dve.Fori(1, GROUPS) as j:
                for s in range(4):
                    one_tile(4 * j + s, s, j)
                    norm(4 * j + s - 1, (s - 1) % 4)
            norm(TT - 1, 3)


def moe(nc, x2, shg, shu, shd, rw, wgu, wd, out):
    base = nc.dram_tensor("base", (TOKENS, D), F32, kind="Internal").ap()
    y = nc.dram_tensor("y_slots", (SLOTS_ALL, D), F32, kind="Internal").ap()
    table = nc.dram_tensor("table", (SLOTS_ALL, 1), I32, kind="Internal").ap()
    with ExitStack() as ctx:
        ident = ctx.enter_context(nc.sbuf_tensor("ident_m", [P, P], F32))
        route = ctx.enter_context(nc.sbuf_tensor("route", [P, TT, E + 1], F32))
        sgate_all = ctx.enter_context(nc.sbuf_tensor("sgate_all", [P, TT], F32))
        weights = ctx.enter_context(nc.sbuf_tensor("weights", [P, 2, TT], F32))
        pos = ctx.enter_context(nc.sbuf_tensor("pos", [P, 2, TT], I32))
        tile_expert = ctx.enter_context(nc.sbuf_tensor("tile_expert", [P, NT], I32))
        gu_in = ctx.enter_context(nc.semaphore("gu_in"))
        ident_set = ctx.enter_context(nc.semaphore("ident_set"))
        with nc.Block() as block:
            @block.gpsimd
            def _(pool):
                nc.gpsimd.memset(ident[:], 0.0).then_inc(ident_set, 1)
                pool.wait_ge(ident_set, 1)
                nc.gpsimd.affine_select(out=ident[:], in_=ident[:], compare_op=ALU.not_equal, fill=1.0, base=0,
                                        pattern=[[-1, P]], channel_multiplier=1).then_inc(ident_set, 1)
                pool.wait_ge(ident_set, 2)
        with ExitStack() as big:
            gu_sb = big.enter_context(nc.sbuf_tensor("gu_sb", [P, E, C, 2 * H], F32))
            wd_sb = big.enter_context(nc.sbuf_tensor("wd_sb", [P, E, CH, D], F32))
            with ExitStack() as small:
                sgu_hi, sgu_lo = [small.enter_context(nc.sbuf_tensor(f"sgu_{i}", [P, C, 2, D], F32R)) for i in ("hi", "lo")]
                sd_hi, sd_lo = [small.enter_context(nc.sbuf_tensor(f"sd_{i}", [P, C, D], F32R)) for i in ("hi", "lo")]

                def weights_hi_lo(k, c):
                    return (sd_hi[:, c, :], sd_lo[:, c, :]) if k == 2 else (sgu_hi[:, c, k, :], sgu_lo[:, c, k, :])

                stage = wd_sb[:].rearrange("p e c d -> p (e c) d")[:, 0:3 * C, :].rearrange("p (k c) d -> p k c d", k=3)
                scores(nc, x2, (shg, shu, shd), stage, rw, weights_hi_lo, route, sgate_all, ident)
                shared_and_place(nc, x2, sgu_hi, sgu_lo, sd_hi, sd_lo, wgu, wd, base, gu_sb, wd_sb, gu_in, route,
                                 sgate_all, weights, pos, tile_expert, table, ident)
            experts(nc, x2, table, tile_expert, gu_sb, wd_sb, gu_in, y, ident)
        combine(nc, base, y, pos, weights, out)


def build(nc, x, xT, wkqT, wvT, woT, bq, bk, bv, bo, shg, shu, shd, rw, wgu, wd, out):
    x2 = nc.dram_tensor("x2", (TOKENS, D), F32, kind="Internal").ap()
    attention(nc, x, xT, wkqT, wvT, woT, bq, bk, bv, bo, x2.rearrange("(b s) d -> b s d", b=B))
    moe(nc, x2, shg, shu, shd, rw, wgu, wd, out)


def kernel(L0_attn_x, L0_attn_wq, L0_attn_bq, L0_attn_wk, L0_attn_bk, L0_attn_wv, L0_attn_bv, L0_attn_wo,
           L0_attn_bo, L0_ffn_gate_w, L0_ffn_w_gate, L0_ffn_w_up, L0_ffn_w_down, L0_ffn_sh_gate, L0_ffn_sh_up,
           L0_ffn_sh_down, L0_ffn_se_gate_w):
    import numpy as np
    import concourse.bacc as bacc
    from concourse.bass_utils import run_bass_kernel_spmd

    def array(a):
        return np.ascontiguousarray(np.asarray(a))

    def turned(w):
        w = np.asarray(w)
        return array(w.T.reshape(-1, P, w.shape[0]).transpose(1, 0, 2))

    x = array(L0_attn_x)
    kq = np.stack([turned(L0_attn_wk), turned(L0_attn_wq)])
    arrays = {
        "x": x,
        "xT": array(x.transpose(0, 2, 1).reshape(B, C, P, S).transpose(0, 2, 1, 3)),
        "wkqT": array(kq.reshape(2, P, C, G, P).transpose(3, 1, 0, 2, 4)),
        "wvT": turned(L0_attn_wv),
        "woT": turned(L0_attn_wo),
        "bq": array(np.asarray(L0_attn_bq).reshape(G, P).T),
        "bk": array(np.asarray(L0_attn_bk).reshape(G, P).T),
        "bv": array(L0_attn_bv),
        "bo": array(L0_attn_bo),
        "shg": turned(L0_ffn_sh_gate),
        "shu": turned(L0_ffn_sh_up),
        "shd": turned(L0_ffn_sh_down),
        "rw": turned(np.concatenate([np.asarray(L0_ffn_gate_w), np.asarray(L0_ffn_se_gate_w)])),
        "wgu": array(np.stack([turned(np.concatenate([g, u])) for g, u in
                               zip(np.asarray(L0_ffn_w_gate), np.asarray(L0_ffn_w_up))])),
        "wd": array(np.stack([turned(w) for w in np.asarray(L0_ffn_w_down)])),
    }
    nc = bacc.Bacc("TRN2", target_bir_lowering=False, num_devices=1)
    drams = {n: nc.dram_tensor(n, a.shape, F32, kind="ExternalInput").ap() for n, a in arrays.items()}
    out = nc.dram_tensor("out", (TOKENS, D), F32, kind="ExternalOutput").ap()
    build(nc, **drams, out=out)
    r = run_bass_kernel_spmd(nc, [arrays], core_ids=[0])
    return r.results[0]["out"].reshape(B, S, D)
```
